# Optimizing a Trainium2 kernel written in Bass

```python
import numpy as np
import jax
import jax.numpy as jnp

def _softmax(x, axis=-1):
    return jax.nn.softmax(x, axis=axis)
def _gelu(x):
    return jax.nn.gelu(x, approximate=True)
def _silu(x):
    return jax.nn.silu(x)
def _sigmoid(x):
    return jax.nn.sigmoid(x)
def _layernorm(x, axis=-1, eps=1e-5):
    m = jnp.mean(x, axis=axis, keepdims=True)
    v = jnp.var(x, axis=axis, keepdims=True)
    return (x - m) / jnp.sqrt(v + eps)
def _scatter_add(tgt, idx, src, axis=0):
    return tgt.at[idx].add(src)
def _segment_sum(src, seg, n):
    return jax.ops.segment_sum(src, seg, n)

kernel_name = 'mk_conv_preact_d2_conv_nchw1024_40ef30'

def setup_inputs(seed: int = 0):
    np.random.seed(seed)
    _w = jnp.asarray
    def _rec_inputs():
        import jax
        import jax.numpy as jnp
        _gk = jax.random.key(seed)
        x = -7.109e-05 + 0.9999 * jax.random.normal(jax.random.fold_in(_gk, 1), (16, 1024, 64, 64), jnp.float32)
        return x
    x = _rec_inputs()
    def _L0_conv_setup():
        import jax, jax.numpy as jnp
        import numpy as np
        CH = 1024
        HEADS = 8
        RED = 4
        PH, PW = (16, 16)
        DPH = max(CH // RED // HEADS, 1)
        TD = DPH * HEADS
        EPS_NORM = 1e-12
        EPS_BN = 1e-05

        def _l2norm(t):
            n = jnp.sqrt(jnp.sum(t * t, axis=-1, keepdims=True))
            return t / jnp.maximum(n, EPS_NORM)
        key = jax.random.key(seed)
        ks = jax.random.split(key, 6)
        b, h, w = (16, 64, 64)
        x = jax.random.normal(ks[0], (b, CH, h, w), dtype=jnp.float32)
        w_qkv = jax.random.normal(ks[1], (3 * TD, CH), dtype=jnp.float32) * (1.0 / np.sqrt(CH))
        temperature = jnp.ones((HEADS, 1, 1), dtype=jnp.float32)
        w_proj = jax.random.normal(ks[2], (CH, TD), dtype=jnp.float32) * (1.0 / np.sqrt(TD))
        bn_gamma = jnp.ones((CH,), dtype=jnp.float32)
        bn_beta = jnp.zeros((CH,), dtype=jnp.float32)
        return {'x': x, 'w_qkv': w_qkv, 'temperature': temperature, 'w_proj': w_proj, 'bn_gamma': bn_gamma, 'bn_beta': bn_beta}
    _L0_conv_all = _L0_conv_setup()
    _L0_conv_in = {k: v for k, v in _L0_conv_all.items() if k in ('w_qkv', 'temperature', 'w_proj', 'bn_gamma', 'bn_beta', )}
    del _L0_conv_all

    def _L1_conv_setup():
        import jax, jax.numpy as jnp
        import numpy as np
        from jax import lax
        GROUPS = 32
        EPS = 1e-05

        def _bilinear_resize(img, oh, ow):
            H, W = (img.shape[-2], img.shape[-1])

            def idx(n_in, n_out):
                x = (jnp.arange(n_out, dtype=jnp.float32) + 0.5) * (n_in / n_out) - 0.5
                x = jnp.clip(x, 0.0, n_in - 1)
                i0 = jnp.floor(x).astype(jnp.int32)
                i1 = jnp.minimum(i0 + 1, n_in - 1)
                return (i0, i1, x - i0)
            r0, r1, tr = idx(H, oh)
            c0, c1, tc = idx(W, ow)
            top = img[..., r0, :]
            bot = img[..., r1, :]
            row = top + (bot - top) * tr[:, None]
            left = row[..., c0]
            right = row[..., c1]
            return left + (right - left) * tc
        key = jax.random.key(seed)
        ks = jax.random.split(key, 12)
        b, c, h, w = (8, 1024, 64, 64)
        cg = c // GROUPS
        s = 1.0 / np.sqrt(cg)
        inp = {'x': jax.random.normal(ks[0], (b, c, h, w), jnp.float32), 'w1': jax.random.normal(ks[1], (cg, cg), jnp.float32) * s, 'b1': jax.random.normal(ks[2], (cg,), jnp.float32) * 0.01, 'gn_gamma': jnp.ones((cg,), jnp.float32), 'gn_beta': jnp.zeros((cg,), jnp.float32), 'w_dw': jax.random.normal(ks[3], (cg, 1, 3, 3), jnp.float32) * (1.0 / 3.0), 'b_dw': jax.random.normal(ks[4], (cg,), jnp.float32) * 0.01, 'w_pw': jax.random.normal(ks[5], (cg, cg), jnp.float32) * s, 'b_pw': jax.random.normal(ks[6], (cg,), jnp.float32) * 0.01, 'w_fp': jax.random.normal(ks[7], (cg, cg), jnp.float32) * s, 'b_fp': jax.random.normal(ks[8], (cg,), jnp.float32) * 0.01}
        return inp
    _L1_conv_all = _L1_conv_setup()
    _L1_conv_in = {k: v for k, v in _L1_conv_all.items() if k in ('w1', 'b1', 'gn_gamma', 'gn_beta', 'w_dw', 'b_dw', 'w_pw', 'b_pw', 'w_fp', 'b_fp', )}
    del _L1_conv_all

    return {
        "x": x,
        "L0_conv_w_qkv": _L0_conv_in["w_qkv"],
        "L0_conv_temperature": _L0_conv_in["temperature"],
        "L0_conv_w_proj": _L0_conv_in["w_proj"],
        "L0_conv_bn_gamma": _L0_conv_in["bn_gamma"],
        "L0_conv_bn_beta": _L0_conv_in["bn_beta"],
        "L1_conv_w1": _L1_conv_in["w1"],
        "L1_conv_b1": _L1_conv_in["b1"],
        "L1_conv_gn_gamma": _L1_conv_in["gn_gamma"],
        "L1_conv_gn_beta": _L1_conv_in["gn_beta"],
        "L1_conv_w_dw": _L1_conv_in["w_dw"],
        "L1_conv_b_dw": _L1_conv_in["b_dw"],
        "L1_conv_w_pw": _L1_conv_in["w_pw"],
        "L1_conv_b_pw": _L1_conv_in["b_pw"],
        "L1_conv_w_fp": _L1_conv_in["w_fp"],
        "L1_conv_b_fp": _L1_conv_in["b_fp"],
    }

def reference(x, L0_conv_w_qkv, L0_conv_temperature, L0_conv_w_proj, L0_conv_bn_gamma, L0_conv_bn_beta, L1_conv_w1, L1_conv_b1, L1_conv_gn_gamma, L1_conv_gn_beta, L1_conv_w_dw, L1_conv_b_dw, L1_conv_w_pw, L1_conv_b_pw, L1_conv_w_fp, L1_conv_b_fp):
    import jax
    import jax.numpy as jnp
    def _L0_conv_ref(x, w_qkv, temperature, w_proj, bn_gamma, bn_beta):
        import jax, jax.numpy as jnp
        import numpy as np
        CH = 1024
        HEADS = 8
        RED = 4
        PH, PW = (16, 16)
        DPH = max(CH // RED // HEADS, 1)
        TD = DPH * HEADS
        EPS_NORM = 1e-12
        EPS_BN = 1e-05

        def _l2norm(t):
            n = jnp.sqrt(jnp.sum(t * t, axis=-1, keepdims=True))
            return t / jnp.maximum(n, EPS_NORM)
        b, c, h, w = x.shape
        fh, fw = (h // PH, w // PW)
        xr = x.reshape(b, c, PH, fh, PW, fw).mean(axis=(3, 5))
        qkv = jnp.einsum('ochw->ohwc', jnp.zeros((1, 1, 1, 1)))
        qkv = jnp.einsum('bchw,oc->bohw', xr, w_qkv)
        q, k, v = jnp.split(qkv, 3, axis=1)
        L = PH * PW

        def to_heads(t):
            return t.reshape(b, HEADS, DPH, L).transpose(0, 1, 3, 2)
        q, k, v = (to_heads(q), to_heads(k), to_heads(v))
        q = _l2norm(q)
        k = _l2norm(k)
        attn = jnp.einsum('bhld,bhmd->bhlm', q, k) * temperature
        attn = jax.nn.softmax(attn, axis=-1)
        out = jnp.einsum('bhlm,bhmd->bhld', attn, v)
        out = out.transpose(0, 1, 3, 2).reshape(b, TD, PH, PW)
        out = jax.image.resize(out, (b, TD, h, w), method='bilinear')
        out = jnp.einsum('bchw,oc->bohw', out, w_proj)
        mean = out.mean(axis=(0, 2, 3), keepdims=True)
        var = out.var(axis=(0, 2, 3), keepdims=True)
        out = (out - mean) * jax.lax.rsqrt(var + EPS_BN)
        out = out * bn_gamma[None, :, None, None] + bn_beta[None, :, None, None]
        return out

    def _L1_conv_ref(x, w1, b1, gn_gamma, gn_beta, w_dw, b_dw, w_pw, b_pw, w_fp, b_fp):
        import jax, jax.numpy as jnp
        import numpy as np
        from jax import lax
        GROUPS = 32
        EPS = 1e-05

        def _bilinear_resize(img, oh, ow):
            H, W = (img.shape[-2], img.shape[-1])

            def idx(n_in, n_out):
                x = (jnp.arange(n_out, dtype=jnp.float32) + 0.5) * (n_in / n_out) - 0.5
                x = jnp.clip(x, 0.0, n_in - 1)
                i0 = jnp.floor(x).astype(jnp.int32)
                i1 = jnp.minimum(i0 + 1, n_in - 1)
                return (i0, i1, x - i0)
            r0, r1, tr = idx(H, oh)
            c0, c1, tc = idx(W, ow)
            top = img[..., r0, :]
            bot = img[..., r1, :]
            row = top + (bot - top) * tr[:, None]
            left = row[..., c0]
            right = row[..., c1]
            return left + (right - left) * tc
        b, c, h, w = x.shape
        cg = c // GROUPS
        bg = b * GROUPS
        gx = x.reshape(bg, cg, h, w)
        x_h = gx.mean(axis=3, keepdims=True)
        x_w = gx.mean(axis=2, keepdims=True)
        cat = jnp.concatenate([x_h, jnp.transpose(x_w, (0, 1, 3, 2))], axis=2)
        hw = jnp.einsum('oc,bcln->boln', w1, cat) + b1[None, :, None, None]
        xh_g, xw_g = (hw[:, :, :h], hw[:, :, h:])
        gated = gx * jax.nn.sigmoid(xh_g) * jax.nn.sigmoid(jnp.transpose(xw_g, (0, 1, 3, 2)))
        mu = gated.mean(axis=(-2, -1), keepdims=True)
        var = gated.var(axis=(-2, -1), keepdims=True)
        x1 = (gated - mu) / jnp.sqrt(var + EPS) * gn_gamma[None, :, None, None] + gn_beta[None, :, None, None]
        dw = lax.conv_general_dilated(gx, w_dw, window_strides=(1, 1), padding=((1, 1), (1, 1)), feature_group_count=cg, dimension_numbers=('NCHW', 'OIHW', 'NCHW'))
        dw = dw + b_dw[None, :, None, None]
        x2 = jnp.einsum('oc,bchw->bohw', w_pw, dw) + b_pw[None, :, None, None]
        freq_mag = jnp.abs(jnp.fft.rfft2(gx, norm='ortho'))
        fm = freq_mag.mean(axis=-1)
        fmap = _bilinear_resize(fm, h, w)
        freq_feat = fmap[:, None] * w_fp.sum(axis=1)[None, :, None, None] + b_fp[None, :, None, None]
        s1 = jax.nn.softmax(x1.mean(axis=(-2, -1)), axis=-1)
        s2 = jax.nn.softmax(x2.mean(axis=(-2, -1)), axis=-1)
        wts = jnp.einsum('bc,bchw->bhw', s1, x2) + jnp.einsum('bc,bchw->bhw', s2, x1)
        weights = wts[:, None] + freq_feat
        return (gx * jax.nn.sigmoid(weights)).reshape(b, c, h, w)

    def _gn(v, G=32, eps=1e-5):
        B_, C_, H_, W_ = v.shape
        g = v.reshape(B_, G, C_ // G, H_, W_)
        m = jnp.mean(g, axis=(2, 3, 4), keepdims=True)
        s = jnp.var(g, axis=(2, 3, 4), keepdims=True)
        return ((g - m) / jnp.sqrt(s + eps)).reshape(v.shape)

    def _ln_c(v, eps=1e-6):
        m = jnp.mean(v, axis=1, keepdims=True)
        s = jnp.var(v, axis=1, keepdims=True)
        return (v - m) / jnp.sqrt(s + eps)

    def _ln_t(v, eps=1e-5):
        m = jnp.mean(v, axis=-1, keepdims=True)
        s = jnp.var(v, axis=-1, keepdims=True)
        return (v - m) / jnp.sqrt(s + eps)

    def _to_tokens(v):
        B_, C_, H_, W_ = v.shape
        return v.reshape(B_, C_, H_ * W_).transpose(0, 2, 1)
    def _from_tokens(t, like):
        B_, C_, H_, W_ = like.shape
        return t.transpose(0, 2, 1).reshape(B_, C_, H_, W_)

    x = x + _L0_conv_ref(_gn(x), L0_conv_w_qkv, L0_conv_temperature, L0_conv_w_proj, L0_conv_bn_gamma, L0_conv_bn_beta)
    x = x + _L1_conv_ref(_gn(x), L1_conv_w1, L1_conv_b1, L1_conv_gn_gamma, L1_conv_gn_beta, L1_conv_w_dw, L1_conv_b_dw, L1_conv_w_pw, L1_conv_b_pw, L1_conv_w_fp, L1_conv_b_fp)
    return x


_drawn_inputs = setup_inputs


def setup_inputs(seed=0):
    import zlib

    import numpy as np

    out = dict(_drawn_inputs(seed))
    spreads = {'L0_conv_temperature': (1.0, 0.6),
     'L0_conv_bn_gamma': (1.0, 0.2),
     'L0_conv_bn_beta': (0.0, 0.1),
     'L1_conv_gn_gamma': (1.0, 0.6),
     'L1_conv_gn_beta': (0.0, 0.8)}
    factors = {'L1_conv_w1': 8.0,
     'L1_conv_b1': 64.0,
     'L1_conv_w_dw': 2.899,
     'L1_conv_b_dw': 56.426,
     'L1_conv_w_pw': 3.28,
     'L1_conv_b_pw': 64.0,
     'L1_conv_b_fp': 61.87}
    for name, (base, spread) in spreads.items():
        noise = np.random.default_rng([zlib.crc32(name.encode()), seed]).standard_normal(out[name].shape)
        drawn = base * np.exp(spread * noise) if base else spread * noise
        out[name] = jnp.asarray(drawn.astype(out[name].dtype))
    for name, factor in factors.items():
        out[name] = (out[name] * factor).astype(out[name].dtype)
    return out
```

```python
import math
from contextlib import ExitStack

import numpy as np

import concourse.bass as bass
from concourse import mybir

F32 = mybir.dt.float32
BF16 = mybir.dt.bfloat16
ALU = mybir.AluOpType
ACT = mybir.ActivationFunctionType
AX = mybir.AxisListType

B, CH, H, W = 16, 1024, 64, 64
PIX = H * W
P = 128
TPB = CH // P
NT = B * TPB
GC = 32
NG = P // GC
HEADS, DPH = 8, 32
TD = HEADS * DPH
PH = PW = 16
LOW = PH * PW
EPS = 1e-5
KW = W // 2 + 1
HH = H // 2
ROW3 = 3 * PH


def constants():
    c = {}
    k = np.arange(64)
    ang = 2 * math.pi * np.outer(k, k) / 64
    cos, sin = np.cos(ang) / 8, np.sin(ang) / 8
    fh = np.concatenate([cos[:, :33], sin[:, 1:32]], axis=1)
    c["dft_h"] = np.kron(np.eye(2), fh)
    wc = np.zeros((2, 64, 2, 2, 32))
    ws = np.zeros((2, 64, 2, 2, 32))
    for j in range(2):
        wc[j, :, 0, j], wc[j, :, 1, j] = cos[:, :32], sin[:, :32]
        ws[j, :, 0, j], ws[j, :, 1, j] = -sin[:, :32], cos[:, :32]
    c["dft_w"] = np.stack([wc.reshape(P, P), ws.reshape(P, P), -ws.reshape(P, P)], 1).reshape(P, 3 * P)
    c["nyq_w"] = np.kron(np.eye(2), cos[:, 32:33])
    comb = np.zeros((2, 64, 2, 64))
    for col in range(64):
        f = col if col <= 32 else col - 32
        for j in range(2):
            comb[j, col, j, f] = 1
            comb[j, col, j, (64 - f) % 64] = 1
    c["nyq_comb"] = comb.reshape(P, P)
    spread = np.zeros((P, 2 * P))
    for p in range(P):
        spread[p, P + (p // 64) * 32 + (p // 32) % 2] = 1
    c["spread"] = spread
    ures = np.zeros((2, 32, 32))
    for i in range(64):
        x = min(max((i + 0.5) * 0.5 - 0.5, 0.0), 31.0)
        i0 = int(math.floor(x))
        i1 = min(i0 + 1, 31)
        ures[i % 2, i0, i // 2] += 1 - (x - i0)
        ures[i % 2, i1, i // 2] += x - i0
    c["resize"] = np.concatenate([np.einsum("gk,ci->gcik", np.eye(NG), ures[a] / KW).reshape(P, P)
                                   for a in range(2)], axis=1)
    shifts = []
    for dh in (-1, 0, 1):
        for dw in (-1, 0, 1):
            for d in (-1, 0, 1):
                m = np.zeros((2, 64, 2, 64))
                for ho in range(2):
                    hi = ho + dh - 2 * d
                    if 0 <= hi < 2:
                        for wo in range(64):
                            if 0 <= wo + dw < 64:
                                m[hi, wo + dw, ho, wo] = 1
                if m.any():
                    shifts.append(m.reshape(P, P))
    c["shifts"] = np.concatenate(shifts, axis=1)
    up = np.zeros((64, 16))
    for o in range(64):
        s = (o + 0.5) / 4 - 0.5
        i0 = math.floor(s)
        up[o, min(max(i0, 0), 15)] += 1 - (s - i0)
        up[o, min(max(i0 + 1, 0), 15)] += s - i0
    wr = np.array([[7, 1], [5, 3], [3, 5], [1, 7]]) / 8.0
    u = np.einsum("dr,ws->rsdw", wr, up).reshape(2, 1, 16, 256)
    c["upsample"] = np.broadcast_to(u.transpose(1, 0, 2, 3), (3, 2, 16, 256)).reshape(96, 256)
    g = up.T @ up
    kk = np.kron(g, g)
    c["up_gram"] = np.concatenate([kk[:P], kk[P:]], axis=1)
    c["ident"] = np.eye(P)
    c["group_ones"] = np.kron(np.eye(NG), np.ones((GC, GC)))
    c["group_sel"] = np.kron(np.eye(NG), np.ones((GC, 1)))
    c["group_cols"] = np.tile(np.kron(np.eye(NG), np.ones((GC, 1))), (1, HH))
    c["chan_sel"] = np.tile(np.eye(GC), (NG, 1))
    return {"c_" + n: np.ascontiguousarray(a, dtype=np.float32) for n, a in c.items()}


TAP_FILLS = [(0, 12), (12, 12), (24, 8)]
SHIFT_PLAN = [(kh * 3 + kw, d) for kh in range(3) for kw in range(3) for d in (-1, 0, 1)
              if any(0 <= ho + (kh - 1) - 2 * d < 2 for ho in range(2))]


class Steps:

    def __init__(self, sem, names):
        self.sem, self.names, self.pos = sem, names, 0

    def done(self, name):
        assert self.names[self.pos] == name, (self.names[self.pos], name)
        self.pos = (self.pos + 1) % len(self.names)
        return self.sem

    def at(self, i, name):
        return i * len(self.names) + self.names.index(name) + 1


def begun(i):
    return not isinstance(i, int) or i >= 0


def build(nc, a, out):
    ctx = ExitStack()
    x_tiles = a["x"].rearrange("b (t p) h w -> (b t) p (h w)", p=P)
    out_tiles = out.rearrange("b (t p) h w -> (b t) p (h w)", p=P)
    low3 = nc.dram_tensor("low3", [NT, 3, 18 * PW, P], BF16, kind="Internal").ap()

    turn = nc.dram_tensor("turn", [2, P, PIX], F32, kind="Internal").ap()

    with ctx:
        def sb(name, cols, dt=F32, parts=P):
            return ctx.enter_context(nc.sbuf_tensor(name, [parts, cols], dt))

        def sem(name):
            return ctx.enter_context(nc.semaphore(name))

        def steps(name, names):
            return Steps(sem(name), names)

        bank = [ctx.enter_context(nc.psum_tensor(f"bank{k}", [P, 512], F32)) for k in range(8)]

        ident = sb("ident", P)
        gones = sb("group_ones", P)
        gsel = sb("group_sel", NG)
        gcols = sb("group_cols", P)
        csel = sb("chan_sel", GC)
        dft_h = sb("dft_h", P)
        dft_w = sb("dft_w", 3 * P)
        nyq_w = sb("nyq_w", 2)
        nyq_comb = sb("nyq_comb", P)
        spread = sb("spread", 2 * P)
        resize = sb("resize", 2 * P)
        shifts = sb("shifts", len(SHIFT_PLAN) * P)
        upmat = sb("upmat", 256, BF16, 96)
        w1bd = sb("w1bd", P)
        wpbd = sb("wpbd", P)
        wptbd = sb("wptbd", P)
        colw = sb("colw", 16)
        B1, GAMMA, BETA, BDW, BPW, BFP = range(6)
        wdw = sb("wdw", 9)
        taps = sb("taps", 36)
        argw = sb("argw", P, F32, 8)
        wts0 = sb("wts0", 1)
        beta_row = sb("beta_row", GC)
        cw = sb("cw", 64)
        consts = [(ident, "c_ident"), (gones, "c_group_ones"), (gsel, "c_group_sel"), (csel, "c_chan_sel"), (gcols, "c_group_cols"),
                  (dft_h, "c_dft_h"), (dft_w, "c_dft_w"), (nyq_w, "c_nyq_w"), (nyq_comb, "c_nyq_comb"),
                  (spread, "c_spread"), (resize, "c_resize"), (shifts, "c_shifts")]

        ARENA = 46000
        arena = sb("arena", ARENA)
        at = [0]

        def carve(cols, dt=F32, parts=P):
            n = cols if dt == F32 else cols // 2
            v = arena[0:parts, at[0]:at[0] + n]
            at[0] += n
            assert at[0] <= ARENA, at[0]
            return v if dt == F32 else v.bitcast(BF16)

        XR = 4
        oall = carve(2 * B * LOW).rearrange("p (o b l) -> p o b l", o=2, b=B)
        gram = carve(2 * LOW).rearrange("p (k l) -> p k l", k=2)
        wp = carve(2 * CH).rearrange("p (o c) -> p o c", o=2)
        cov = carve(2 * TD).rearrange("p (o d) -> p o d", o=2)
        mark = at[0]
        xr = [carve(PIX) for _ in range(XR)]
        wq = carve(TPB * 3 * TD).rearrange("p (t o) -> p t o", t=TPB)
        pooled = [carve(TPB * LOW).rearrange("p (t l) -> p t l", t=TPB) for _ in range(1)] * 2
        xn = carve(TPB * LOW).rearrange("p (t l) -> p t l", t=TPB)
        st = carve(2 * TPB)
        gn = carve(8 * TPB)
        tempc = carve(2)
        qk = carve(4 * LOW).rearrange("p (o l) -> p o l", o=4)
        qk2 = carve(4 * LOW).rearrange("p (o l) -> p o l", o=4)
        vt = carve(2 * TD).rearrange("p (m d) -> p m d", m=2)
        prob = carve(2 * LOW).rearrange("p (l m) -> p l m", l=2)
        probT = carve(2 * LOW).rearrange("p (m l) -> p m l", m=2)
        hc = carve(8)
        oT = carve(2 * TD).rearrange("p (l d) -> p l d", l=2)
        ko = carve(2 * TD).rearrange("p (l d) -> p l d", l=2)
        junk1 = carve(PIX, BF16)
        at[0] = mark
        omean = carve(2)
        zw = carve(2 * CH).rearrange("p (o c) -> p o c", o=2)
        wm = carve(2 * CH).rearrange("p (o c) -> p o c", o=2)
        bmean, bvar, bgam, bbet = carve(CH), carve(CH), carve(CH), carve(CH)
        ob = carve(2 * LOW).rearrange("p (o l) -> p o l", o=2)
        ylow = carve(CH)
        part = [[carve(CH, BF16) for _ in range(3)] for _ in range(2)]
        ones = carve(P)

        at[0] = 0
        X = [carve(PIX) for _ in range(2)]
        YS = [carve(17 * P, BF16, 96).rearrange("p (i c) -> p i c", i=17) for _ in range(2)]
        GT = carve(PIX)
        G2 = carve(PIX)
        AH = carve(PIX)
        MAG = carve(2048)
        SQ = [carve(512) for _ in range(2)]
        SIG = [carve(1024) for _ in range(4)]
        TR = carve(2048)
        JUNK = carve(PIX, BF16)
        TP = carve(9 * NG * 34).rearrange("p (t h g) -> p t h g", t=9, g=NG)
        TG = carve(NG * HH)
        ROWS = carve(PIX, F32, 8)
        RC = carve(P)
        CATS = [carve(P) for _ in range(2)]
        FRL = carve(GC)
        EDGE = carve(6)
        SHW = [carve(P) for _ in range(2)]
        PAR = [carve(32) for _ in range(2)]
        SM = carve(64)
        FR = carve(32)
        ALG = carve(NG)
        SQN = carve(64)
        NYM = carve(64)
        FM = carve(64)
        MAP = carve(2 * P).rearrange("p (m x) -> p m x", m=2)

        cst = sem("consts_landed")
        upl = sem("upmat_landed")
        zeroed = sem("tables_zeroed")
        blocks = sem("blocks_landed")
        xl = [sem(f"x_slot{k}_landed") for k in range(XR)]
        vector_setup = steps("vector_setup", ["wfp", "sel", "selw", "max", "rsum", "s1", "p", "wp9", "taps", "c0", "c1", "wts0", "argw"])
        scalar_setup = steps("scalar_setup", ["exprow", "expcol"])
        tensor_setup = steps("tensor_setup", ["argw", "p", "const"])
        vector_pool = steps("vector_pool", ["pool", "sum"])
        scalar_squares = steps("scalar_squares", ["sq"])
        tensor_imagestats = steps("tensor_imagestats", ["stats"])
        vector_imagestats = steps("vector_imagestats", ["mean", "msq", "var0", "var", "rstd", "r16", "shift"]
                      + [f"xn{t}" for t in range(TPB)])
        scalar_imagestats = steps("scalar_imagestats", ["std"])
        tensor_qkv = steps("tensor_qkv", ["qk", "v", "norms"])
        vector_qkv = steps("vector_qkv", ["copy", "v", "floor", "recip", "qn", "kn"])
        scalar_qkv = steps("scalar_qkv", ["sq", "norm"])
        tensor_head = steps("tensor_head", ["scores", "transpose", "out"])
        vector_head = steps("vector_head", ["max", "rsum", "scale0", "scale1", "probT"])
        scalar_head = steps("scalar_head", ["exp0", "exp1"])
        tensor_image_end = steps("tensor_image_end", ["ko", "cov"])
        vector_image_end = steps("vector_image_end", ["o", "oT", "ko", "cov"])
        vector_cov_zero = steps("vector_cov_zero", ["zero"])
        bnl = sem("bn_rows_landed")
        vector_bn = steps("vector_bn", ["ones", "osum0", "osum1", "omean", "zw0", "zw1", "zw2", "zw3", "wm0", "wm1",
                                   "mean0", "mean1", "e0", "e1", "msq", "var", "eps", "rstd", "scale", "ms", "shift"])
        tensor_bn = steps("tensor_bn", ["z", "mean", "sq"])
        scalar_bn = steps("scalar_bn", ["std"])
        vector_low = steps("vector_low", ["ob"] + [f"{n}{k}" for k in range(2)
                                            for n in ("mul0", "mul1", "add", "hi", "r1", "mid", "lo")])
        tensor_low = steps("tensor_low", ["y0", "y1"])
        lows = [sem(f"low_parts{k}_stored") for k in range(2)]
        XL = [sem(f"tile_slot{k}_landed") for k in range(2)]
        YL = [sem(f"low_slot{k}_landed") for k in range(2)]
        tensor_front = steps("tensor_front", [f"up{q}" for q in range(8)] + ["stats"])
        vector_front = steps("vector_front", [f"add{q}" for q in range(8)]
                   + ["rows", "total", "mean", "msq", "var", "rstd", "shift", "r64", "gx", "cat"])
        scalar_front = steps("scalar_front", ["sq", "std"])
        pool_front = steps("pool_front", [f"col{k}" for k in range(6)])
        vector_pads = steps("vector_pads", ["edge"])
        turned = sem("gx_in_dram")
        g2l = sem("rows_layout_landed")
        tensor_gate = steps("tensor_gate", ["w1", "pw", "lrow", "const"])
        scalar_gate = steps("scalar_gate", ["sig", "sq", "std", "exprow", "expcol"])
        vector_gate = steps("vector_gate", ["t1", "gated", "tot", "edges0", "edges1", "f0", "f1", "corner", "fw", "dw",
                                   "dwb", "x2m", "lsel", "max", "gmean", "gmsq", "gvar", "grstd", "rsum", "s2",
                                   "sg", "alpha", "alg", "am", "kc", "kcon"])
        tensor_taps = steps("tensor_taps", ["t0", "t1", "t2"])
        scalar_taps = steps("scalar_taps", ["t0", "t1", "t2"])
        tensor_spectrum = steps("tensor_spectrum", [f"h{k}" for k in range(8)] + ["nyq"] + [f"w{k}" for k in range(8)]
                   + ["nyqsum", "chan"])
        scalar_spectrum = steps("scalar_spectrum", [f"h{k}" for k in range(8)] + ["nyqsq"] + [f"w{k}" for k in range(8)]
                    + ["nyqroot", "root"])
        vector_spectrum = steps("vector_spectrum", [f"w{k}" for k in range(8)] + ["fm0", "fm1"])
        tensor_back = steps("tensor_back", ["gsum", "wmap", "fmap"] + [f"arg{q}" for q in range(8)])
        vector_back = steps("vector_back", ["gsum", "wmap", "fmap"] + [f"mul{q}" for q in range(4)])
        scalar_back = steps("scalar_back", [f"sig{q}" for q in range(8)] + [f"mean{q}" for q in range(4)])
        mapl = sem("map_rows_landed")
        stored = [sem(f"out_slot{k}_stored") for k in range(4)]
        pads = sem("pads_zeroed")

        block = ctx.enter_context(nc.Block())
        N_CONST = len(consts) + 7 + 6

        @block.sync
        def _(sp):
            for dst, name in consts:
                sp.dma_start(dst[:, :], a[name]).then_inc(cst, 16)
            for k, name in enumerate(["b1", "gn_gamma", "gn_beta", "b_dw", "b_pw", "b_fp"]):
                sp.dma_start(colw[:, k:k + 1], a[name]).then_inc(cst, 16)
            sp.dma_start(wdw[:, :], a["w_dw"]).then_inc(cst, 16)
            sp.dma_start(gram, a["c_up_gram"].rearrange("p (k l) -> p k l", k=2)).then_inc(cst, 16)
            sp.dma_start(wp, a["w_proj_t"].rearrange("(o p) c -> p o c", p=P)).then_inc(cst, 16)
            sp.dma_start(wq, a["w_qkv_t"].rearrange("(t p) o -> p t o", p=P)).then_inc(cst, 16)
            sp.dma_start(tempc, a["temperature"]).then_inc(cst, 16)
            sp.dma_start(beta_row[:, :], a["beta_row"]).then_inc(cst, 16)
            sp.dma_start(cw[:, 0:32], a["w_fp"]).then_inc(cst, 16)
            sp.wait_ge(zeroed, 1)
            for g in range(NG):
                s = slice(g * GC, g * GC + GC)
                sp.dma_start(w1bd[s, s], a["w1_t"]).then_inc(blocks, 16)
                sp.dma_start(wpbd[s, s], a["w_pw"]).then_inc(blocks, 16)
                sp.dma_start(wptbd[s, s], a["w_pw_t"]).then_inc(blocks, 16)

            def load1(b, s):
                n = b * TPB + s - XR
                if begun(n):
                    sp.wait_ge(scalar_squares.sem, scalar_squares.at(n, "sq"))
                    sp.wait_ge(vector_pool.sem, vector_pool.at(n, "pool"))
                sp.dma_start(xr[s % XR], x_tiles[b * TPB + s]).then_inc(xl[s % XR], 16)

            for s in range(TPB):
                load1(0, s)
            with sp.Fori(1, B) as b:
                for s in range(TPB):
                    load1(b, s)

            sp.wait_ge(vector_image_end.sem, vector_image_end.at(B - 1, "cov"))
            sp.wait_ge(tensor_image_end.sem, tensor_image_end.at(B - 1, "cov"))
            sp.dma_start(bgam, a["bn_gamma"].partition_broadcast(P)).then_inc(bnl, 16)
            sp.dma_start(bbet, a["bn_beta"].partition_broadcast(P)).then_inc(bnl, 16)
            with sp.Fori(0, B) as b:
                for k in range(2):
                    for s in range(3):
                        sp.wait_ge(vector_low.sem, vector_low.at(b, ("hi", "mid", "lo")[s] + str(k)))
                        dst = low3[bass.ds(b * TPB, TPB), s]
                        dst = dst.rearrange("t q c -> q t c")
                        src = part[k][s].rearrange("p (t c) -> p t c", t=TPB)
                        sp.dma_start(dst[16 + k * P:16 + (k + 1) * P], src).then_inc(lows[k], 16)
                        if k == 0:
                            sp.dma_start(dst[0:16], src[0:16]).then_inc(lows[k], 16)
                        else:
                            sp.dma_start(dst[272:288], src[112:128]).then_inc(lows[k], 16)
            sp.wait_ge(lows[0], 16 * (6 * B))
            sp.wait_ge(lows[1], 16 * (6 * B))

            def load2(pr, u):
                i = 2 * pr + u
                if begun(i - 2):
                    sp.wait_ge(scalar_back.sem, scalar_back.at(i - 2, "mean3"))
                sp.dma_start(X[u], x_tiles[i]).then_inc(XL[u], 16)
                if begun(i - 2):
                    sp.wait_ge(tensor_front.sem, tensor_front.at(i - 2, "up7"))
                for s in range(3):
                    for r in range(2):
                        p0 = s * 32 + r * 16
                        sp.dma_start(YS[u][p0:p0 + 16], low3[i, s, r * 16:r * 16 + 272, :].rearrange(
                            "(k q) c -> q k c", q=16)).then_inc(YL[u], 16)

            def turn2(i, u):
                sp.wait_ge(vector_front.sem, vector_front.at(i, "gx"))
                sp.dma_start(turn[u], X[u]).then_inc(turned, 16)
                sp.wait_ge(turned, 16 * (i + 1))
                if begun(i - 1):
                    sp.wait_ge(tensor_spectrum.sem, tensor_spectrum.at(i - 1, "h7"))
                for j in range(2):
                    sp.dma_start(G2[64 * j:64 * j + 64, :].rearrange("h (c w) -> h c w", c=64),
                                 turn[u, 64 * j:64 * j + 64, :].rearrange("c (h w) -> h c w", h=64)).then_inc(g2l, 16)

            def rows2(i):
                sp.wait_ge(vector_back.sem, vector_back.at(i, "fmap"))
                if begun(i - 1):
                    sp.wait_ge(tensor_back.sem, tensor_back.at(i - 1, "arg7"))
                for m in range(2):
                    for g in range(NG):
                        r = NG * m + g
                        sp.dma_start(ROWS[r:r + 1, :].rearrange("r (h x) -> r h x", h=HH),
                                     MAP[g::NG, m, :]).then_inc(mapl, 16)

            def store2(i, u):
                for q in range(4):
                    sp.wait_ge(scalar_back.sem, scalar_back.at(i, f"mean{q}"))
                    sp.dma_start(out_tiles[i][:, q * 1024:(q + 1) * 1024], SIG[q]).then_inc(stored[q], 16)

            def step(pr, u, load=True):
                i = 2 * pr + u
                if load:
                    load2(pr + u, 1 - u)
                turn2(i, u)
                rows2(i)
                store2(i, u)

            load2(0, 0)
            step(0, 0)
            step(0, 1)
            with sp.Fori(1, NT // 2 - 1) as pr:
                step(pr, 0)
                step(pr, 1)
            step(NT // 2 - 1, 0)
            step(NT // 2 - 1, 1, load=False)
            for q in range(4):
                sp.wait_ge(stored[q], 16 * (NT))

        @block.gpsimd
        def _(pool):
            pool.memset(w1bd[:, :], 0.0)
            pool.memset(wpbd[:, :], 0.0)
            pool.memset(wptbd[:, :], 0.0).then_inc(zeroed, 1)
            pool.dma_start(upmat[:, :], a["c_upsample"]).then_inc(upl, 16)

            pool.wait_ge(lows[0], 16 * (6 * B))
            pool.wait_ge(lows[1], 16 * (6 * B))
            pool.wait_ge(vector_low.sem, vector_low.at(B - 1, "lo1"))
            pool.wait_ge(tensor_low.sem, tensor_low.at(B - 1, "y1"))
            pool.memset(TP, 0.0).then_inc(pads, 1)

            def front(i, u):
                pool.wait_ge(vector_front.sem, vector_front.at(i, "add7"))
                if begun(i - 1):
                    pool.wait_ge(vector_front.sem, vector_front.at(i - 1, "cat"))
                pool.tensor_tensor(TR[:, 0:2048], X[u][:, 0:2048], X[u][:, 2048:4096],
                                   op=ALU.add).then_inc(pool_front.done("col0"), 1)
                n = 1024
                for k in range(1, 6):
                    pool.wait_ge(pool_front.sem, pool_front.at(i, f"col{k - 1}"))
                    dst = RC[:, 64:128] if n == 64 else TR[:, 0:n]
                    pool.tensor_tensor(dst, TR[:, 0:n], TR[:, n:2 * n], op=ALU.add).then_inc(pool_front.done(f"col{k}"), 1)
                    n //= 2

            front(0, 0)
            front(1, 1)
            with pool.Fori(1, NT // 2) as pr:
                front(2 * pr, 0)
                front(2 * pr + 1, 1)

        @block.scalar
        def _(act):
            act.wait_ge(vector_setup.sem, vector_setup.at(0, "max"))
            act.activation(beta_row[:, :], beta_row[:, :], ACT.Exp, bias=cw[:, 33:34],
                           accum_out=cw[:, 40:41]).then_inc(scalar_setup.done("exprow"), 1)
            act.activation(cw[:, 41:42], colw[:, BETA:BETA + 1], ACT.Exp, bias=cw[:, 33:34]).then_inc(scalar_setup.done("expcol"), 1)

            def square1(b, s):
                act.wait_ge(xl[s % XR], 16 * (2 * b + s // XR + 1))
                if s == 0:
                    if begun(b - 1):
                        act.wait_ge(tensor_imagestats.sem, tensor_imagestats.at(b - 1, "stats"))
                if begun(b * TPB + s - 1):
                    act.wait_ge(scalar_squares.sem, scalar_squares.at(b * TPB + s - 1, "sq"))
                act.activation(junk1, xr[s % XR], ACT.Square, accum_out=st[:, TPB + s:TPB + s + 1]).then_inc(scalar_squares.done("sq"), 1)

            def image1(b):
                act.wait_ge(vector_imagestats.sem, vector_imagestats.at(b, "var"))
                act.activation(gn[:, 24:32], gn[:, 16:24], ACT.Sqrt).then_inc(scalar_imagestats.done("std"), 1)
                act.wait_ge(vector_qkv.sem, vector_qkv.at(b, "copy"))
                act.activation(qk2, qk, ACT.Square).then_inc(scalar_qkv.done("sq"), 1)
                act.wait_ge(tensor_qkv.sem, tensor_qkv.at(b, "norms"))
                act.activation(qk2[:, 0:2, :], bank[4][:, :].rearrange("p (o l) -> p o l", o=2), ACT.Sqrt)
                act.activation(qk2[:, 2:4, :], bank[5][:, :].rearrange("p (o l) -> p o l", o=2),
                               ACT.Sqrt).then_inc(scalar_qkv.done("norm"), 1)

            def head1(n):
                act.wait_ge(vector_head.sem, vector_head.at(n, "max"))
                for l in range(2):
                    act.activation(prob[:, l, :], bank[6][:, l * LOW:(l + 1) * LOW], ACT.Exp, bias=hc[:, l:l + 1],
                                   accum_out=hc[:, 2 + l:3 + l]).then_inc(scalar_head.done(f"exp{l}"), 1)

            for s in range(TPB):
                square1(0, s)
            image1(0)

            def image_step(b):
                for s in range(TPB):
                    square1(b, s)
                    head1((b - 1) * TPB + s)
                image1(b)

            image_step(1)
            with act.Fori(2, B) as b:
                image_step(b)
            for s in range(TPB):
                head1((B - 1) * TPB + s)

            act.wait_ge(vector_bn.sem, vector_bn.at(0, "eps"))
            act.activation(bvar, bvar, ACT.Sqrt).then_inc(scalar_bn.done("std"), 1)

            def front(i, u):
                act.wait_ge(vector_front.sem, vector_front.at(i, "add7"))
                if begun(i - 1):
                    act.wait_ge(tensor_front.sem, tensor_front.at(i - 1, "stats"))
                if begun(i - 1):
                    act.wait_ge(scalar_gate.sem, scalar_gate.at(i - 1, "sq"))
                act.activation(JUNK, X[u], ACT.Square, accum_out=PAR[u][:, 1:2]).then_inc(scalar_front.done("sq"), 1)
                act.wait_ge(vector_front.sem, vector_front.at(i, "var"))
                act.activation(PAR[u][:, 5:6], PAR[u][:, 4:5], ACT.Sqrt).then_inc(scalar_front.done("std"), 1)

            def gate(i, u):
                act.wait_ge(tensor_gate.sem, tensor_gate.at(i, "w1"))
                act.activation(SHW[u], bank[7][:, 128:256], ACT.Sigmoid, bias=colw[:, B1:B1 + 1]).then_inc(scalar_gate.done("sig"), 1)

            def gate_stats(i, u):
                act.wait_ge(vector_gate.sem, vector_gate.at(i, "gated"))
                act.wait_ge(scalar_front.sem, scalar_front.at(i, "sq"))
                act.activation(JUNK, GT, ACT.Square, accum_out=SM[:, 1:2]).then_inc(scalar_gate.done("sq"), 1)
                act.wait_ge(vector_gate.sem, vector_gate.at(i, "gvar"))
                act.activation(SM[:, 5:6], SM[:, 4:5], ACT.Sqrt).then_inc(scalar_gate.done("std"), 1)
                act.wait_ge(vector_gate.sem, vector_gate.at(i, "max"))
                act.activation(FR, bank[7][:, 320:352], ACT.Exp, bias=SM[:, 10:11],
                               accum_out=SM[:, 11:12]).then_inc(scalar_gate.done("exprow"), 1)
                act.activation(SM[:, 12:13], SM[:, 9:10], ACT.Exp, bias=SM[:, 10:11]).then_inc(scalar_gate.done("expcol"), 1)

            def taps2(i):
                for k, (c0, n) in enumerate(TAP_FILLS):
                    act.wait_ge(tensor_taps.sem, tensor_taps.at(i, f"t{k}"))
                    if k == 0:
                        if begun(i - 1):
                            act.wait_ge(tensor_back.sem, tensor_back.at(i - 1, "wmap"))
                    act.activation(TP[:, :, 1 + c0:1 + c0 + n, :],
                                   bank[4 + k % 2][:, 0:36 * n].rearrange("p (c t g) -> p t c g", t=9, g=NG),
                                   ACT.Copy).then_inc(scalar_taps.done(f"t{k}"), 1)

            def spectrum(i):
                for k in range(8):
                    act.wait_ge(tensor_spectrum.sem, tensor_spectrum.at(i, f"h{k}"))
                    if k == 0:
                        if begun(i - 1):
                            act.wait_ge(tensor_spectrum.sem, tensor_spectrum.at(i - 1, "w7"))
                    act.activation(AH[:, k * 512:(k + 1) * 512], bank[2 + k % 2][:, :], ACT.Copy).then_inc(scalar_spectrum.done(f"h{k}"), 1)
                act.wait_ge(tensor_spectrum.sem, tensor_spectrum.at(i, "nyq"))
                act.activation(SQN, bank[6][:, 384:448], ACT.Square).then_inc(scalar_spectrum.done("nyqsq"), 1)
                for k in range(8):
                    act.wait_ge(tensor_spectrum.sem, tensor_spectrum.at(i, f"w{k}"))
                    if k >= 2:
                        act.wait_ge(vector_spectrum.sem, vector_spectrum.at(i, f"w{k - 2}"))
                    else:
                        if begun(i - 1):
                            act.wait_ge(vector_spectrum.sem, vector_spectrum.at(i - 1, f"w{k + 6}"))
                    act.activation(SQ[k % 2], bank[2 + k % 2][:, :], ACT.Square).then_inc(scalar_spectrum.done(f"w{k}"), 1)
                act.wait_ge(tensor_spectrum.sem, tensor_spectrum.at(i, "nyqsum"))
                if begun(i - 1):
                    act.wait_ge(vector_spectrum.sem, vector_spectrum.at(i - 1, "fm1"))
                act.activation(NYM, bank[6][:, 448:512], ACT.Sqrt).then_inc(scalar_spectrum.done("nyqroot"), 1)
                act.wait_ge(vector_spectrum.sem, vector_spectrum.at(i, "w7"))
                act.activation(MAG, MAG, ACT.Sqrt).then_inc(scalar_spectrum.done("root"), 1)

            def back(i, u):
                for q in range(8):
                    act.wait_ge(tensor_back.sem, tensor_back.at(i, f"arg{q}"))
                    if q % 2 == 0:
                        if begun(i - 1):
                            act.wait_ge(stored[q // 2], 16 * (i))
                    act.activation(SIG[q // 2][:, (q % 2) * 512:(q % 2 + 1) * 512], bank[q % 2][:, :], ACT.Sigmoid,
                                   bias=colw[:, BFP:BFP + 1]).then_inc(scalar_back.done(f"sig{q}"), 1)
                for q in range(4):
                    act.wait_ge(vector_back.sem, vector_back.at(i, f"mul{q}"))
                    act.activation(SIG[q], SIG[q], ACT.Identity, bias=PAR[u][:, 2:3]).then_inc(scalar_back.done(f"mean{q}"), 1)

            def step(i, u):
                front(i, u)
                gate(i, u)
                taps2(i)
                gate_stats(i, u)
                spectrum(i)
                back(i, u)

            step(0, 0)
            step(1, 1)
            with act.Fori(1, NT // 2) as pr:
                step(2 * pr, 0)
                step(2 * pr + 1, 1)

        @block.vector
        def _(dve):
            dve.wait_ge(cst, 16 * N_CONST)
            dve.memset(cov, 0.0).then_inc(vector_cov_zero.done("zero"), 1)
            dve.tensor_reduce(cw[:, 32:33], cw[:, 0:32], axis=AX.X, op=ALU.add).then_inc(vector_setup.done("wfp"), 1)
            dve.wait_ge(vector_setup.sem, vector_setup.at(0, "wfp"))
            dve.tensor_copy(cw[:, 44:48], gsel[:, :]).then_inc(vector_setup.done("sel"), 1)
            dve.tensor_scalar(cw[:, 48:52], gsel[:, :], cw[:, 32:33], None, ALU.mult).then_inc(vector_setup.done("selw"), 1)
            dve.tensor_reduce(cw[:, 33:34], beta_row[:, :], axis=AX.X, op=ALU.max,
                              negate=True).then_inc(vector_setup.done("max"), 1)
            dve.wait_ge(scalar_setup.sem, scalar_setup.at(0, "expcol"))
            dve.reciprocal(cw[:, 34:35], cw[:, 40:41]).then_inc(vector_setup.done("rsum"), 1)
            dve.wait_ge(vector_setup.sem, vector_setup.at(0, "rsum"))
            dve.tensor_tensor(cw[:, 35:36], cw[:, 41:42], cw[:, 34:35], op=ALU.mult).then_inc(vector_setup.done("s1"), 1)
            dve.wait_ge(tensor_setup.sem, tensor_setup.at(0, "p"))
            dve.tensor_copy(cw[:, 42:43], bank[0][:, 0:1]).then_inc(vector_setup.done("p"), 1)
            dve.wait_ge(vector_setup.sem, vector_setup.at(0, "p"))
            dve.tensor_scalar(cw[:, 52:61], wdw[:, :], cw[:, 42:43], None, ALU.mult).then_inc(vector_setup.done("wp9"), 1)
            dve.wait_ge(vector_setup.sem, vector_setup.at(0, "wp9"))
            dve.tensor_tensor(taps[:, :].rearrange("p (t g) -> p t g", g=NG),
                              cw[:, 52:61].unsqueeze(2).to_broadcast([P, 9, NG]),
                              gsel[:, :].unsqueeze(1).to_broadcast([P, 9, NG]), op=ALU.mult).then_inc(vector_setup.done("taps"), 1)
            dve.tensor_tensor(cw[:, 36:37], cw[:, 35:36], colw[:, BPW:BPW + 1], op=ALU.mult).then_inc(vector_setup.done("c0"), 1)
            dve.wait_ge(vector_setup.sem, vector_setup.at(0, "c0"))
            dve.scalar_tensor_tensor(cw[:, 43:44], colw[:, BDW:BDW + 1], cw[:, 42:43], cw[:, 36:37],
                                     op0=ALU.mult, op1=ALU.add).then_inc(vector_setup.done("c1"), 1)
            dve.wait_ge(tensor_setup.sem, tensor_setup.at(0, "const"))
            dve.tensor_copy(wts0[:, :], bank[0][:, 1:2]).then_inc(vector_setup.done("wts0"), 1)
            dve.tensor_copy(argw[:, :], bank[0][0:8, 128:256]).then_inc(vector_setup.done("argw"), 1)

            def pool1(b, s):
                dve.wait_ge(xl[s % XR], 16 * (2 * b + s // XR + 1))
                dve.tensor_reduce(pooled[0][:, s, :].rearrange("p (r c) -> p r c", r=PH),
                                  xr[s % XR].rearrange("p (r a c e) -> p r c a e", r=PH, a=4, c=PW),
                                  axis=AX.XY, op=ALU.add).then_inc(vector_pool.done("pool"), 1)
                dve.wait_ge(vector_pool.sem, vector_pool.at(b * TPB + s, "pool"))
                if s == 0:
                    if begun(b - 1):
                        dve.wait_ge(tensor_imagestats.sem, tensor_imagestats.at(b - 1, "stats"))
                dve.tensor_reduce(st[:, s:s + 1], pooled[0][:, s, :], axis=AX.X, op=ALU.add).then_inc(vector_pool.done("sum"), 1)

            def image1(b):
                dve.wait_ge(tensor_imagestats.sem, tensor_imagestats.at(b, "stats"))
                n = 1.0 / (GC * PIX)
                dve.tensor_scalar(gn[:, 0:8], bank[0][:, 0:8], n, None, ALU.mult).then_inc(vector_imagestats.done("mean"), 1)
                dve.wait_ge(vector_imagestats.sem, vector_imagestats.at(b, "mean"))
                dve.tensor_tensor(gn[:, 8:16], gn[:, 0:8], gn[:, 0:8], op=ALU.mult).then_inc(vector_imagestats.done("msq"), 1)
                dve.wait_ge(vector_imagestats.sem, vector_imagestats.at(b, "msq"))
                dve.scalar_tensor_tensor(gn[:, 16:24], bank[0][:, 8:16], n, gn[:, 8:16], op0=ALU.mult,
                                         op1=ALU.subtract).then_inc(vector_imagestats.done("var0"), 1)
                dve.wait_ge(vector_imagestats.sem, vector_imagestats.at(b, "var0"))
                dve.tensor_scalar(gn[:, 16:24], gn[:, 16:24], EPS, None, ALU.add).then_inc(vector_imagestats.done("var"), 1)
                dve.wait_ge(scalar_imagestats.sem, scalar_imagestats.at(b, "std"))
                dve.reciprocal(gn[:, 32:40], gn[:, 24:32]).then_inc(vector_imagestats.done("rstd"), 1)
                dve.wait_ge(vector_imagestats.sem, vector_imagestats.at(b, "rstd"))
                dve.tensor_scalar(gn[:, 40:48], gn[:, 32:40], 1.0 / 16, None, ALU.mult).then_inc(vector_imagestats.done("r16"), 1)
                dve.scalar_tensor_tensor(gn[:, 48:56], gn[:, 0:8], -1.0, gn[:, 32:40], op0=ALU.mult,
                                         op1=ALU.mult).then_inc(vector_imagestats.done("shift"), 1)
                dve.wait_ge(vector_imagestats.sem, vector_imagestats.at(b, "shift"))
                if begun(b - 1):
                    dve.wait_ge(tensor_qkv.sem, tensor_qkv.at(b - 1, "v"))
                for t in range(TPB):
                    dve.tensor_scalar(xn[:, t, :], pooled[0][:, t, :], gn[:, 40 + t:41 + t], gn[:, 48 + t:49 + t],
                                      ALU.mult, ALU.add).then_inc(vector_imagestats.done(f"xn{t}"), 1)
                dve.wait_ge(tensor_qkv.sem, tensor_qkv.at(b, "qk"))
                dve.tensor_copy(qk[:, 0:2, :], bank[1][:, :].rearrange("p (o l) -> p o l", o=2))
                dve.tensor_copy(qk[:, 2:4, :], bank[2][:, :].rearrange("p (o l) -> p o l", o=2)).then_inc(vector_qkv.done("copy"), 1)
                dve.wait_ge(tensor_qkv.sem, tensor_qkv.at(b, "v"))
                dve.tensor_copy(vt, bank[3][:, :].rearrange("p (m d) -> p m d", m=2)).then_inc(vector_qkv.done("v"), 1)
                dve.wait_ge(scalar_qkv.sem, scalar_qkv.at(b, "norm"))
                dve.tensor_scalar(qk2, qk2, 1e-12, None, ALU.max).then_inc(vector_qkv.done("floor"), 1)
                dve.wait_ge(vector_qkv.sem, vector_qkv.at(b, "floor"))
                dve.reciprocal(qk2, qk2).then_inc(vector_qkv.done("recip"), 1)
                dve.wait_ge(vector_qkv.sem, vector_qkv.at(b, "recip"))
                for o in range(2):
                    ins = dve.scalar_tensor_tensor(qk[:, o, :], qk[:, o, :], tempc[:, o:o + 1], qk2[:, o, :],
                                                   op0=ALU.mult, op1=ALU.mult)
                ins.then_inc(vector_qkv.done("qn"), 1)
                dve.tensor_tensor(qk[:, 2:4, :], qk[:, 2:4, :], qk2[:, 2:4, :], op=ALU.mult).then_inc(vector_qkv.done("kn"), 1)

            def head1(n):
                dve.wait_ge(tensor_head.sem, tensor_head.at(n, "scores"))
                dve.tensor_reduce(hc[:, 0:2], bank[6][:, :].rearrange("p (l m) -> p l m", l=2), axis=AX.X,
                                  op=ALU.max, negate=True).then_inc(vector_head.done("max"), 1)
                dve.wait_ge(scalar_head.sem, scalar_head.at(n, "exp1"))
                dve.reciprocal(hc[:, 4:6], hc[:, 2:4]).then_inc(vector_head.done("rsum"), 1)
                dve.wait_ge(vector_head.sem, vector_head.at(n, "rsum"))
                for l in range(2):
                    dve.tensor_scalar(prob[:, l, :], prob[:, l, :], hc[:, 4 + l:5 + l], None,
                                      ALU.mult).then_inc(vector_head.done(f"scale{l}"), 1)
                dve.wait_ge(tensor_head.sem, tensor_head.at(n, "transpose"))
                if begun(n - 1):
                    dve.wait_ge(tensor_head.sem, tensor_head.at(n - 1, "out"))
                dve.tensor_copy(probT, bank[7][:, :].rearrange("p (m l) -> p m l", m=2)).then_inc(vector_head.done("probT"), 1)

            def finish1(b):
                dve.wait_ge(tensor_head.sem, tensor_head.at(b * TPB + TPB - 1, "out"))
                dst = oall[:, :, b, :] if isinstance(b, int) else oall[:, :, bass.ds(b, 1), :].squeeze(2)
                dve.tensor_copy(dst, bank[1][:, :].rearrange("p (o l) -> p o l", o=2)).then_inc(vector_image_end.done("o"), 1)
                dve.tensor_copy(oT, bank[2][:, :].rearrange("p (l d) -> p l d", l=2)).then_inc(vector_image_end.done("oT"), 1)
                dve.wait_ge(tensor_image_end.sem, tensor_image_end.at(b, "ko"))
                dve.tensor_copy(ko, bank[4][:, :].rearrange("p (l d) -> p l d", l=2)).then_inc(vector_image_end.done("ko"), 1)
                dve.wait_ge(tensor_image_end.sem, tensor_image_end.at(b, "cov"))
                dve.wait_ge(vector_cov_zero.sem, vector_cov_zero.at(0, "zero"))
                if begun(b - 1):
                    dve.wait_ge(vector_image_end.sem, vector_image_end.at(b - 1, "cov"))
                dve.tensor_tensor(cov, cov, bank[5][:, :].rearrange("p (o d) -> p o d", o=2),
                                  op=ALU.add).then_inc(vector_image_end.done("cov"), 1)

            for s in range(TPB):
                pool1(0, s)
            image1(0)

            def image_step(b):
                for s in range(TPB):
                    pool1(b, s)
                    head1((b - 1) * TPB + s)
                finish1(b - 1)
                image1(b)

            image_step(1)
            with dve.Fori(2, B) as b:
                image_step(b)
            for s in range(TPB):
                head1((B - 1) * TPB + s)
            finish1(B - 1)

            dve.wait_ge(vector_image_end.sem, vector_image_end.at(B - 1, "cov"))
            dve.wait_ge(tensor_image_end.sem, tensor_image_end.at(B - 1, "cov"))
            dve.memset(ones, 1.0).then_inc(vector_bn.done("ones"), 1)
            for o in range(2):
                dve.tensor_reduce(omean[:, o:o + 1], oall[:, o, :, :].rearrange("p b l -> p (b l)"), axis=AX.X,
                                  op=ALU.add).then_inc(vector_bn.done(f"osum{o}"), 1)
            dve.wait_ge(vector_bn.sem, vector_bn.at(0, "osum1"))
            dve.tensor_scalar(omean, omean, 1.0 / (B * LOW), None, ALU.mult).then_inc(vector_bn.done("omean"), 1)
            dve.wait_ge(tensor_bn.sem, tensor_bn.at(0, "z"))
            for k in range(4):
                o, c = divmod(k, 2)
                s = slice(c * 512, c * 512 + 512)
                dve.tensor_tensor(zw[:, o, s], bank[k][:, :], wp[:, o, s], op=ALU.mult).then_inc(vector_bn.done(f"zw{k}"), 1)
            dve.wait_ge(vector_bn.sem, vector_bn.at(0, "omean"))
            for o in range(2):
                dve.tensor_scalar(wm[:, o, :], wp[:, o, :], omean[:, o:o + 1], None,
                                  ALU.mult).then_inc(vector_bn.done(f"wm{o}"), 1)
            dve.wait_ge(tensor_bn.sem, tensor_bn.at(0, "sq"))
            for c in range(2):
                dve.tensor_copy(bmean[:, c * 512:c * 512 + 512], bank[4 + c][:, :]).then_inc(vector_bn.done(f"mean{c}"), 1)
            for c in range(2):
                dve.tensor_scalar(bvar[:, c * 512:c * 512 + 512], bank[6 + c][:, :], 1.0 / (B * PIX), None,
                                  ALU.mult).then_inc(vector_bn.done(f"e{c}"), 1)
            dve.wait_ge(vector_bn.sem, vector_bn.at(0, "e1"))
            dve.tensor_tensor(ylow, bmean, bmean, op=ALU.mult).then_inc(vector_bn.done("msq"), 1)
            dve.wait_ge(vector_bn.sem, vector_bn.at(0, "msq"))
            dve.tensor_tensor(bvar, bvar, ylow, op=ALU.subtract).then_inc(vector_bn.done("var"), 1)
            dve.wait_ge(vector_bn.sem, vector_bn.at(0, "var"))
            dve.tensor_scalar(bvar, bvar, EPS, None, ALU.add).then_inc(vector_bn.done("eps"), 1)
            dve.wait_ge(scalar_bn.sem, scalar_bn.at(0, "std"))
            dve.reciprocal(bvar, bvar).then_inc(vector_bn.done("rstd"), 1)
            dve.wait_ge(vector_bn.sem, vector_bn.at(0, "rstd"))
            dve.wait_ge(bnl, 16 * (2))
            dve.tensor_tensor(bgam, bgam, bvar, op=ALU.mult).then_inc(vector_bn.done("scale"), 1)
            dve.wait_ge(vector_bn.sem, vector_bn.at(0, "scale"))
            dve.tensor_tensor(bmean, bmean, bgam, op=ALU.mult).then_inc(vector_bn.done("ms"), 1)
            dve.wait_ge(vector_bn.sem, vector_bn.at(0, "ms"))
            dve.tensor_tensor(bbet, bbet, bmean, op=ALU.subtract).then_inc(vector_bn.done("shift"), 1)
            dve.wait_ge(vector_bn.sem, vector_bn.at(0, "shift"))

            def low(b):
                if begun(b - 1):
                    dve.wait_ge(tensor_low.sem, tensor_low.at(b - 1, "y1"))
                src = oall[:, :, b, :] if isinstance(b, int) else oall[:, :, bass.ds(b, 1), :].squeeze(2)
                dve.tensor_copy(ob, src).then_inc(vector_low.done("ob"), 1)
                for k in range(2):
                    dve.wait_ge(tensor_low.sem, tensor_low.at(b, f"y{k}"))
                    if k == 0:
                        if begun(b - 1):
                            dve.wait_ge(vector_low.sem, vector_low.at(b - 1, "lo1"))
                    else:
                        dve.wait_ge(vector_low.sem, vector_low.at(b, "lo0"))
                    for c in range(2):
                        s = slice(c * 512, c * 512 + 512)
                        dve.tensor_tensor(ylow[:, s], bank[2 * k + c][:, :], bgam[:, s],
                                          op=ALU.mult).then_inc(vector_low.done(f"mul{c}{k}"), 1)
                    dve.wait_ge(vector_low.sem, vector_low.at(b, f"mul1{k}"))
                    dve.tensor_tensor(ylow, ylow, bbet, op=ALU.add).then_inc(vector_low.done(f"add{k}"), 1)
                    dve.wait_ge(vector_low.sem, vector_low.at(b, f"add{k}"))
                    if begun(b - 1):
                        dve.wait_ge(lows[k], 16 * (6 * b))
                    dve.tensor_copy(part[k][0], ylow).then_inc(vector_low.done(f"hi{k}"), 1)
                    dve.wait_ge(vector_low.sem, vector_low.at(b, f"hi{k}"))
                    dve.tensor_tensor(ylow, ylow, part[k][0], op=ALU.subtract).then_inc(vector_low.done(f"r1{k}"), 1)
                    dve.wait_ge(vector_low.sem, vector_low.at(b, f"r1{k}"))
                    dve.tensor_copy(part[k][1], ylow).then_inc(vector_low.done(f"mid{k}"), 1)
                    dve.wait_ge(vector_low.sem, vector_low.at(b, f"mid{k}"))
                    dve.tensor_tensor(part[k][2], ylow, part[k][1], op=ALU.subtract).then_inc(vector_low.done(f"lo{k}"), 1)

            low(0)
            with dve.Fori(1, B) as b:
                low(b)

            dve.wait_ge(lows[0], 16 * (6 * B))
            dve.wait_ge(lows[1], 16 * (6 * B))
            dve.wait_ge(vector_low.sem, vector_low.at(B - 1, "lo1"))
            dve.memset(EDGE, 0.0).then_inc(vector_pads.done("edge"), 1)

            def front(pr, u):
                i = 2 * pr + u
                par = PAR[u]
                dve.wait_ge(XL[u], 16 * (pr + 1))
                for q in range(8):
                    dve.wait_ge(tensor_front.sem, tensor_front.at(i, f"up{q}"))
                    s = slice(q * 512, q * 512 + 512)
                    dve.tensor_tensor(X[u][:, s], X[u][:, s], bank[q % 2][:, :], op=ALU.add).then_inc(vector_front.done(f"add{q}"), 1)
                dve.wait_ge(vector_front.sem, vector_front.at(i, "add7"))
                dve.tensor_reduce(RC[:, 0:64], X[u].rearrange("p (h w) -> p h w", h=64), axis=AX.X,
                                  op=ALU.add).then_inc(vector_front.done("rows"), 1)
                dve.wait_ge(vector_front.sem, vector_front.at(i, "rows"))
                dve.tensor_reduce(par[:, 0:1], RC[:, 0:64], axis=AX.X, op=ALU.add).then_inc(vector_front.done("total"), 1)
                dve.wait_ge(tensor_front.sem, tensor_front.at(i, "stats"))
                n = 1.0 / (GC * PIX)
                dve.tensor_scalar(par[:, 2:3], bank[7][:, 0:1], n, None, ALU.mult).then_inc(vector_front.done("mean"), 1)
                dve.wait_ge(vector_front.sem, vector_front.at(i, "mean"))
                dve.tensor_scalar(par[:, 3:4], par[:, 2:3], par[:, 2:3], -EPS, ALU.mult, ALU.add).then_inc(vector_front.done("msq"), 1)
                dve.wait_ge(vector_front.sem, vector_front.at(i, "msq"))
                dve.scalar_tensor_tensor(par[:, 4:5], bank[7][:, 1:2], n, par[:, 3:4], op0=ALU.mult,
                                         op1=ALU.subtract).then_inc(vector_front.done("var"), 1)
                dve.wait_ge(scalar_front.sem, scalar_front.at(i, "std"))
                dve.reciprocal(par[:, 6:7], par[:, 5:6]).then_inc(vector_front.done("rstd"), 1)
                dve.wait_ge(vector_front.sem, vector_front.at(i, "rstd"))
                dve.scalar_tensor_tensor(par[:, 7:8], par[:, 2:3], -1.0, par[:, 6:7], op0=ALU.mult,
                                         op1=ALU.mult).then_inc(vector_front.done("shift"), 1)
                dve.tensor_scalar(par[:, 8:9], par[:, 6:7], 1.0 / 64, None, ALU.mult).then_inc(vector_front.done("r64"), 1)
                dve.wait_ge(vector_front.sem, vector_front.at(i, "r64"))
                dve.wait_ge(pool_front.sem, pool_front.at(i, "col5"))
                dve.tensor_scalar(X[u], X[u], par[:, 6:7], par[:, 7:8], ALU.mult, ALU.add).then_inc(vector_front.done("gx"), 1)
                if begun(i - 2):
                    dve.wait_ge(tensor_gate.sem, tensor_gate.at(i - 2, "w1"))
                dve.tensor_scalar(CATS[u], RC, par[:, 8:9], par[:, 7:8], ALU.mult, ALU.add).then_inc(vector_front.done("cat"), 1)

            def gate(pr, u):
                i = 2 * pr + u
                cat = CATS[u]
                dve.wait_ge(scalar_gate.sem, scalar_gate.at(i, "sig"))
                if begun(i - 1):
                    dve.wait_ge(tensor_back.sem, tensor_back.at(i - 1, "gsum"))
                grid = X[u].rearrange("p (h w) -> p h w", h=64)
                ggrid = GT.rearrange("p (h w) -> p h w", h=64)
                dve.tensor_tensor(ggrid, grid, SHW[u][:, 64:128].unsqueeze(1).to_broadcast([P, 64, 64]),
                                  op=ALU.mult).then_inc(vector_gate.done("t1"), 1)
                dve.wait_ge(vector_gate.sem, vector_gate.at(i, "t1"))
                dve.scalar_tensor_tensor(ggrid, ggrid, 1.0, SHW[u][:, 0:64].unsqueeze(2).to_broadcast([P, 64, 64]),
                                         op0=ALU.mult, op1=ALU.mult, accum_out=SM[:, 0:1]).then_inc(vector_gate.done("gated"), 1)
                dve.tensor_reduce(SM[:, 20:21], cat[:, 0:64], axis=AX.X, op=ALU.add).then_inc(vector_gate.done("tot"), 1)
                dve.tensor_copy(EDGE[:, 2::-2], cat[:, 0:64:63]).then_inc(vector_gate.done("edges0"), 1)
                dve.tensor_copy(EDGE[:, 5:2:-2], cat[:, 64:128:63]).then_inc(vector_gate.done("edges1"), 1)
                dve.wait_ge(vector_gate.sem, vector_gate.at(i, "edges1"))
                fq = FR[:, 0:9].rearrange("p (a b) -> p a b", a=3)
                dve.tensor_tensor(fq, EDGE[:, 0:3].unsqueeze(2).to_broadcast([P, 3, 3]),
                                  EDGE[:, 3:6].unsqueeze(1).to_broadcast([P, 3, 3]), op=ALU.add).then_inc(vector_gate.done("f0"), 1)
                dve.wait_ge(vector_gate.sem, vector_gate.at(i, "f0"))
                dve.tensor_scalar(FR[:, 0:9], FR[:, 0:9], -1.0, SM[:, 20:21], ALU.mult, ALU.add).then_inc(vector_gate.done("f1"), 1)
                dve.wait_ge(vector_gate.sem, vector_gate.at(i, "f1"))
                corner = fq[:, ::2, ::2]
                dve.scalar_tensor_tensor(corner, grid[:, ::-63, ::-63], 1.0 / 64, corner, op0=ALU.mult,
                                         op1=ALU.add).then_inc(vector_gate.done("corner"), 1)
                dve.wait_ge(vector_gate.sem, vector_gate.at(i, "corner"))
                dve.tensor_tensor(FR[:, 16:25], FR[:, 0:9], wdw[:, :], op=ALU.mult).then_inc(vector_gate.done("fw"), 1)
                dve.wait_ge(vector_gate.sem, vector_gate.at(i, "fw"))
                dve.tensor_reduce(SM[:, 7:8], FR[:, 16:25], axis=AX.X, op=ALU.add).then_inc(vector_gate.done("dw"), 1)
                dve.wait_ge(vector_gate.sem, vector_gate.at(i, "dw"))
                dve.tensor_scalar(SM[:, 8:9], SM[:, 7:8], 1.0 / 64, colw[:, BDW:BDW + 1], ALU.mult,
                                  ALU.add).then_inc(vector_gate.done("dwb"), 1)
                dve.wait_ge(tensor_gate.sem, tensor_gate.at(i, "pw"))
                dve.tensor_tensor(SM[:, 9:10], bank[7][:, 64:65], colw[:, BPW:BPW + 1], op=ALU.add).then_inc(vector_gate.done("x2m"), 1)
                dve.wait_ge(vector_gate.sem, vector_gate.at(i, "x2m"))
                dve.tensor_scalar(FRL, csel[:, :], SM[:, 9:10], None, ALU.mult).then_inc(vector_gate.done("lsel"), 1)
                dve.wait_ge(tensor_gate.sem, tensor_gate.at(i, "lrow"))
                dve.tensor_reduce(SM[:, 10:11], bank[7][:, 320:352], axis=AX.X, op=ALU.max,
                                  negate=True).then_inc(vector_gate.done("max"), 1)
                dve.tensor_scalar(SM[:, 2:3], SM[:, 0:1], 1.0 / PIX, None, ALU.mult).then_inc(vector_gate.done("gmean"), 1)
                dve.wait_ge(vector_gate.sem, vector_gate.at(i, "gmean"))
                dve.tensor_scalar(SM[:, 3:4], SM[:, 2:3], SM[:, 2:3], -EPS, ALU.mult, ALU.add).then_inc(vector_gate.done("gmsq"), 1)
                dve.wait_ge(vector_gate.sem, vector_gate.at(i, "gmsq"))
                dve.wait_ge(scalar_gate.sem, scalar_gate.at(i, "sq"))
                dve.scalar_tensor_tensor(SM[:, 4:5], SM[:, 1:2], 1.0 / PIX, SM[:, 3:4], op0=ALU.mult,
                                         op1=ALU.subtract).then_inc(vector_gate.done("gvar"), 1)
                dve.wait_ge(scalar_gate.sem, scalar_gate.at(i, "expcol"))
                dve.reciprocal(SM[:, 6:7], SM[:, 5:6]).then_inc(vector_gate.done("grstd"), 1)
                dve.reciprocal(SM[:, 13:14], SM[:, 11:12]).then_inc(vector_gate.done("rsum"), 1)
                dve.wait_ge(vector_gate.sem, vector_gate.at(i, "rsum"))
                dve.tensor_tensor(SM[:, 14:15], SM[:, 12:13], SM[:, 13:14], op=ALU.mult).then_inc(vector_gate.done("s2"), 1)
                dve.tensor_tensor(SM[:, 15:16], colw[:, GAMMA:GAMMA + 1], SM[:, 6:7], op=ALU.mult).then_inc(vector_gate.done("sg"), 1)
                dve.wait_ge(vector_gate.sem, vector_gate.at(i, "sg"))
                dve.tensor_tensor(SM[:, 16:17], SM[:, 14:15], SM[:, 15:16], op=ALU.mult).then_inc(vector_gate.done("alpha"), 1)
                dve.wait_ge(vector_gate.sem, vector_gate.at(i, "alpha"))
                dve.tensor_scalar(ALG, gsel[:, :], SM[:, 16:17], None, ALU.mult).then_inc(vector_gate.done("alg"), 1)
                dve.tensor_tensor(SM[:, 17:18], SM[:, 16:17], SM[:, 2:3], op=ALU.mult).then_inc(vector_gate.done("am"), 1)
                dve.wait_ge(vector_gate.sem, vector_gate.at(i, "am"))
                dve.scalar_tensor_tensor(SM[:, 18:19], colw[:, BETA:BETA + 1], SM[:, 14:15], SM[:, 17:18],
                                         op0=ALU.mult, op1=ALU.subtract).then_inc(vector_gate.done("kc"), 1)
                dve.wait_ge(tensor_gate.sem, tensor_gate.at(i, "const"))
                dve.tensor_tensor(SM[:, 19:20], bank[7][:, 66:67], wts0[:, :], op=ALU.add).then_inc(vector_gate.done("kcon"), 1)

            def spectrum(pr, u):
                i = 2 * pr + u
                for k in range(8):
                    sign, half, octet = k // 4, (k // 2) % 2, k % 2
                    dve.wait_ge(scalar_spectrum.sem, scalar_spectrum.at(i, f"w{k}"))
                    if k == 0:
                        if begun(i - 1):
                            dve.wait_ge(tensor_spectrum.sem, tensor_spectrum.at(i - 1, "chan"))
                    else:
                        dve.wait_ge(vector_spectrum.sem, vector_spectrum.at(i, f"w{k - 1}"))
                    c = sign * 1024 + octet * 512
                    dve.tensor_tensor(MAG[64 * half:64 * half + 64, c:c + 512], SQ[k % 2][0:64, :], SQ[k % 2][64:128, :],
                                      op=ALU.add).then_inc(vector_spectrum.done(f"w{k}"), 1)
                dve.wait_ge(vector_spectrum.sem, vector_spectrum.at(i, "w7"))
                dve.wait_ge(tensor_spectrum.sem, tensor_spectrum.at(i, "chan"))
                dve.wait_ge(scalar_spectrum.sem, scalar_spectrum.at(i, "nyqroot"))
                if begun(i - 1):
                    dve.wait_ge(tensor_back.sem, tensor_back.at(i - 1, "fmap"))
                fm = bank[6][:, 256:320]
                dve.tensor_tensor(FM[:, 0:32], fm[:, 0:32], NYM[:, 0:32], op=ALU.add).then_inc(vector_spectrum.done("fm0"), 1)
                dve.tensor_tensor(FM[:, 32:64], fm[:, 63:31:-1], NYM[:, 32:64], op=ALU.add).then_inc(vector_spectrum.done("fm1"), 1)

            def back(pr, u):
                i = 2 * pr + u
                dve.wait_ge(tensor_back.sem, tensor_back.at(i, "gsum"))
                if begun(i - 1):
                    dve.wait_ge(tensor_back.sem, tensor_back.at(i - 1, "wmap"))
                dve.tensor_copy(TG, bank[4][:, 0:128]).then_inc(vector_back.done("gsum"), 1)
                dve.wait_ge(tensor_back.sem, tensor_back.at(i, "wmap"))
                dve.wait_ge(vector_gate.sem, vector_gate.at(i, "kcon"))
                if begun(i - 1):
                    dve.wait_ge(mapl, 16 * (8 * i))
                dve.tensor_scalar(MAP[:, 0, :], bank[5][:, 0:128], SM[:, 19:20], None, ALU.add).then_inc(vector_back.done("wmap"), 1)
                dve.wait_ge(tensor_back.sem, tensor_back.at(i, "fmap"))
                dve.tensor_copy(MAP[:, 1, :], bank[6][:, 0:128]).then_inc(vector_back.done("fmap"), 1)
                for q in range(4):
                    dve.wait_ge(scalar_back.sem, scalar_back.at(i, f"sig{2 * q + 1}"))
                    dve.scalar_tensor_tensor(SIG[q], SIG[q], PAR[u][:, 5:6], X[u][:, q * 1024:(q + 1) * 1024],
                                             op0=ALU.add, op1=ALU.mult).then_inc(vector_back.done(f"mul{q}"), 1)

            def step(pr, u):
                front(pr, u)
                gate(pr, u)
                spectrum(pr, u)
                back(pr, u)

            step(0, 0)
            step(0, 1)
            with dve.Fori(1, NT // 2) as pr:
                step(pr, 0)
                step(pr, 1)

        @block.tensor
        def _(pe):
            mm = pe.matmul
            pe.wait_ge(cst, 16 * N_CONST)
            pe.wait_ge(upl, 16 * 1)
            pe.wait_ge(blocks, 16 * (3 * NG))
            pe.wait_ge(vector_setup.sem, vector_setup.at(0, "selw"))
            mm(bank[0][0:8, 128:256], cw[:, 44:52], ident[:, :], start=True, stop=True).then_inc(tensor_setup.done("argw"), 1)
            pe.wait_ge(vector_setup.sem, vector_setup.at(0, "s1"))
            mm(bank[0][:, 0:1], wpbd[:, :], cw[:, 35:36], start=True, stop=True).then_inc(tensor_setup.done("p"), 1)
            pe.wait_ge(vector_setup.sem, vector_setup.at(0, "c1"))
            mm(bank[0][:, 1:2], gones[:, :], cw[:, 43:44], start=True, stop=True).then_inc(tensor_setup.done("const"), 1)
            pe.wait_ge(vector_setup.sem, vector_setup.at(0, "argw"))

            def image1(b):
                pe.wait_ge(vector_pool.sem, vector_pool.at(b * TPB + TPB - 1, "sum"))
                pe.wait_ge(scalar_squares.sem, scalar_squares.at(b * TPB + TPB - 1, "sq"))
                if begun(b - 1):
                    pe.wait_ge(vector_imagestats.sem, vector_imagestats.at(b - 1, "var0"))
                mm(bank[0][:, 0:16], gones[:, :], st, start=True, stop=True).then_inc(tensor_imagestats.done("stats"), 1)
                pe.wait_ge(vector_imagestats.sem, vector_imagestats.at(b, "xn7"))
                if begun(b - 1):
                    pe.wait_ge(vector_image_end.sem, vector_image_end.at(b - 1, "oT"))
                for o in range(4):
                    for t in range(TPB):
                        ins = mm(bank[1 + o // 2][:, (o % 2) * LOW:(o % 2 + 1) * LOW], wq[:, t, o * P:(o + 1) * P],
                                 xn[:, t, :], start=(t == 0), stop=(t == TPB - 1))
                ins.then_inc(tensor_qkv.done("qk"), 1)
                for m in range(2):
                    for t in range(TPB):
                        ins = mm(bank[3][:, m * TD:(m + 1) * TD], xn[:, t, m * P:(m + 1) * P],
                                 wq[:, t, 2 * TD:3 * TD], start=(t == 0), stop=(t == TPB - 1))
                ins.then_inc(tensor_qkv.done("v"), 1)
                pe.wait_ge(scalar_qkv.sem, scalar_qkv.at(b, "sq"))
                if begun(b - 1):
                    pe.wait_ge(vector_image_end.sem, vector_image_end.at(b - 1, "cov"))
                mm(bank[4][:, :], gones[:, :], qk2[:, 0:2, :], start=True, stop=True)
                mm(bank[5][:, :], gones[:, :], qk2[:, 2:4, :], start=True, stop=True).then_inc(tensor_qkv.done("norms"), 1)

            def head1(b, h):
                n = b * TPB + h
                lo, o = 32 * (h % 4), h // 4
                pe.wait_ge(vector_qkv.sem, vector_qkv.at(b, "kn"))
                if begun(n - 1):
                    pe.wait_ge(scalar_head.sem, scalar_head.at(n - 1, "exp1"))
                for l in range(2):
                    ins = mm(bank[6][:, l * LOW:(l + 1) * LOW], qk[lo:lo + 32, o, l * P:(l + 1) * P],
                             qk[lo:lo + 32, 2 + o, :], start=True, stop=True)
                ins.then_inc(tensor_head.done("scores"), 1)
                pe.wait_ge(vector_head.sem, vector_head.at(n, "scale1"))
                if begun(n - 1):
                    pe.wait_ge(vector_head.sem, vector_head.at(n - 1, "probT"))
                for m in range(2):
                    for l in range(2):
                        ins = pe.transpose(bank[7][:, m * LOW + l * P:m * LOW + (l + 1) * P],
                                           prob[:, l, m * P:(m + 1) * P], ident[:, :])
                ins.then_inc(tensor_head.done("transpose"), 1)
                pe.wait_ge(vector_head.sem, vector_head.at(n, "probT"))
                d = slice(DPH * h, DPH * h + DPH)
                for m in range(2):
                    mm(bank[1][lo:lo + 32, o * LOW:(o + 1) * LOW], vt[:, m, d], probT[:, m, :],
                       start=(m == 0), stop=(m == 1))
                for l in range(2):
                    for m in range(2):
                        ins = mm(bank[2][:, l * TD + DPH * h:l * TD + DPH * h + DPH], probT[:, m, l * P:(l + 1) * P],
                                 vt[:, m, d], start=(m == 0), stop=(m == 1))
                ins.then_inc(tensor_head.done("out"), 1)

            def finish1(b):
                pe.wait_ge(vector_image_end.sem, vector_image_end.at(b, "oT"))
                for l in range(2):
                    for k in range(2):
                        ins = mm(bank[4][:, l * TD:(l + 1) * TD], gram[:, k, l * P:(l + 1) * P], oT[:, k, :],
                                 start=(k == 0), stop=(k == 1))
                ins.then_inc(tensor_image_end.done("ko"), 1)
                pe.wait_ge(vector_image_end.sem, vector_image_end.at(b, "ko"))
                for o in range(2):
                    for k in range(2):
                        ins = mm(bank[5][:, o * TD:(o + 1) * TD], oT[:, k, o * P:(o + 1) * P], ko[:, k, :],
                                 start=(k == 0), stop=(k == 1))
                ins.then_inc(tensor_image_end.done("cov"), 1)

            image1(0)

            def image_step(b):
                for h in range(HEADS):
                    head1(b - 1, h)
                finish1(b - 1)
                image1(b)

            image_step(1)
            with pe.Fori(2, B) as b:
                image_step(b)
            for h in range(HEADS):
                head1(B - 1, h)
            finish1(B - 1)

            pe.wait_ge(vector_image_end.sem, vector_image_end.at(B - 1, "cov"))
            for o in range(2):
                for c in range(2):
                    for k in range(2):
                        ins = mm(bank[2 * o + c][:, :], cov[:, k, o * P:(o + 1) * P], wp[:, k, c * 512:(c + 1) * 512],
                                 start=(k == 0), stop=(k == 1))
            ins.then_inc(tensor_bn.done("z"), 1)
            pe.wait_ge(vector_bn.sem, vector_bn.at(0, "wm1"))
            for c in range(2):
                for o in range(2):
                    ins = mm(bank[4 + c][:, :], ones, wm[:, o, c * 512:(c + 1) * 512], start=(o == 0), stop=(o == 1))
            ins.then_inc(tensor_bn.done("mean"), 1)
            for c in range(2):
                for o in range(2):
                    ins = mm(bank[6 + c][:, :], ones, zw[:, o, c * 512:(c + 1) * 512], start=(o == 0), stop=(o == 1))
            ins.then_inc(tensor_bn.done("sq"), 1)

            def low(b):
                pe.wait_ge(vector_low.sem, vector_low.at(b, "ob"))
                for k in range(2):
                    if begun(b - 1):
                        pe.wait_ge(vector_low.sem, vector_low.at(b - 1, f"mul1{k}"))
                    for c in range(2):
                        for o in range(2):
                            ins = mm(bank[2 * k + c][:, :], ob[:, o, k * P:(k + 1) * P], wp[:, o, c * 512:(c + 1) * 512],
                                     start=(o == 0), stop=(o == 1))
                    ins.then_inc(tensor_low.done(f"y{k}"), 1)

            low(0)
            with pe.Fori(1, B) as b:
                low(b)
            pe.wait_ge(vector_low.sem, vector_low.at(B - 1, "mul11"))

            def front(pr, u):
                i = 2 * pr + u
                pe.wait_ge(YL[u], 16 * (6 * (pr + 1)))
                for q in range(8):
                    if q < 2:
                        if begun(i - 1):
                            pe.wait_ge(scalar_back.sem, scalar_back.at(i - 1, f"sig{6 + q}"))
                        if begun(i - 1):
                            pe.wait_ge(vector_front.sem, vector_front.at(i - 1, f"add{6 + q}"))
                    else:
                        pe.wait_ge(vector_front.sem, vector_front.at(i, f"add{q - 2}"))
                    mm(bank[q % 2][:, 0:128], YS[u][:, 2 * q, :], upmat[:, 128:256], start=True, stop=True)
                    mm(bank[q % 2][:, 128:384], YS[u][:, 2 * q + 1, :], upmat[:, :], start=True, stop=True)
                    mm(bank[q % 2][:, 384:512], YS[u][:, 2 * q + 2, :], upmat[:, 0:128], start=True,
                       stop=True).then_inc(tensor_front.done(f"up{q}"), 1)
                pe.wait_ge(vector_front.sem, vector_front.at(i, "total"))
                pe.wait_ge(scalar_front.sem, scalar_front.at(i, "sq"))
                if begun(i - 1):
                    pe.wait_ge(vector_gate.sem, vector_gate.at(i - 1, "kcon"))
                mm(bank[7][:, 0:2], gones[:, :], PAR[u][:, 0:2], start=True, stop=True).then_inc(tensor_front.done("stats"), 1)

            def gate(pr, u):
                i = 2 * pr + u
                pe.wait_ge(vector_front.sem, vector_front.at(i, "cat"))
                mm(bank[7][:, 128:256], w1bd[:, :], CATS[u], start=True, stop=True).then_inc(tensor_gate.done("w1"), 1)

            def taps2(pr, u):
                i = 2 * pr + u
                pe.wait_ge(vector_front.sem, vector_front.at(i, "gx"))
                for k, (c0, n) in enumerate(TAP_FILLS):
                    if k == 2:
                        pe.wait_ge(scalar_taps.sem, scalar_taps.at(i, "t0"))
                    else:
                        if begun(i - 1):
                            pe.wait_ge(vector_back.sem, vector_back.at(i - 1, ("gsum", "wmap")[k]))
                    for c in range(n):
                        ins = mm(bank[4 + k % 2][:, 36 * c:36 * c + 36], X[u][:, (c0 + c) * P:(c0 + c + 1) * P],
                                 taps[:, :], start=True, stop=True)
                    ins.then_inc(tensor_taps.done(f"t{k}"), 1)

            def logits(pr, u):
                i = 2 * pr + u
                pe.wait_ge(vector_gate.sem, vector_gate.at(i, "dwb"))
                pe.wait_ge(scalar_gate.sem, scalar_gate.at(i, "sig"))
                mm(bank[7][:, 64:65], wptbd[:, :], SM[:, 8:9], start=True, stop=True).then_inc(tensor_gate.done("pw"), 1)
                pe.wait_ge(vector_gate.sem, vector_gate.at(i, "lsel"))
                mm(bank[7][:, 320:352], gones[:, :], FRL, start=True, stop=True).then_inc(tensor_gate.done("lrow"), 1)
                pe.wait_ge(vector_gate.sem, vector_gate.at(i, "kc"))
                mm(bank[7][:, 66:67], gcols[:, :], SM[:, 18:19], start=True, stop=True).then_inc(tensor_gate.done("const"), 1)

            def spectrum(pr, u):
                i = 2 * pr + u
                pe.wait_ge(g2l, 16 * (2 * (i + 1)))
                for k in range(8):
                    if k < 2:
                        if begun(i - 1):
                            pe.wait_ge(scalar_spectrum.sem, scalar_spectrum.at(i - 1, f"w{6 + k}"))
                    else:
                        pe.wait_ge(scalar_spectrum.sem, scalar_spectrum.at(i, f"h{k - 2}"))
                    for c in range(4):
                        ins = mm(bank[2 + k % 2][:, c * P:(c + 1) * P], G2[:, (4 * k + c) * P:(4 * k + c + 1) * P],
                                 dft_h[:, :], start=True, stop=True)
                    ins.then_inc(tensor_spectrum.done(f"h{k}"), 1)
                pe.wait_ge(scalar_spectrum.sem, scalar_spectrum.at(i, "h7"))
                if begun(i - 1):
                    pe.wait_ge(vector_back.sem, vector_back.at(i - 1, "fmap"))
                for c in range(32):
                    ins = mm(bank[6][:, 384 + 2 * c:386 + 2 * c], AH[:, c * P:(c + 1) * P], nyq_w[:, :],
                             start=True, stop=True)
                ins.then_inc(tensor_spectrum.done("nyq"), 1)
                ah = AH.rearrange("p (c k) -> p c k", k=64)
                for k in range(8):
                    sign, half, octet = k // 4, (k // 2) % 2, k % 2
                    if k < 2:
                        pe.wait_ge(scalar_spectrum.sem, scalar_spectrum.at(i, f"h{6 + k}"))
                    else:
                        pe.wait_ge(scalar_spectrum.sem, scalar_spectrum.at(i, f"w{k - 2}"))
                    c0 = 2 * (half * 16 + octet * 8)
                    dst = bank[2 + k % 2][:, :].rearrange("p (c k) -> p c k", k=32)
                    mm(dst, dft_w[:, 0:P], ah[:, c0:c0 + 16, sign:sign + 32], start=True, stop=False)
                    mm(dst[:, :, 1 - sign:32 - sign], dft_w[:, (1 + sign) * P:(2 + sign) * P], ah[:, c0:c0 + 16, 33:64],
                       start=False, stop=True).then_inc(tensor_spectrum.done(f"w{k}"), 1)
                pe.wait_ge(scalar_spectrum.sem, scalar_spectrum.at(i, "nyqsq"))
                for j in range(2):
                    ins = mm(bank[6][64 * j:64 * j + 64, 448:512], SQN, nyq_comb[:, 64 * j:64 * j + 64],
                             start=True, stop=True)
                ins.then_inc(tensor_spectrum.done("nyqsum"), 1)
                pe.wait_ge(scalar_spectrum.sem, scalar_spectrum.at(i, "root"))
                pe.wait_ge(scalar_spectrum.sem, scalar_spectrum.at(i, "nyqroot"))
                mag = MAG.rearrange("p (s c k) -> p s c k", s=2, k=32)
                for c in range(32):
                    shift = (c % 2) * 64 + 2 * (c // 2)
                    ins = mm(bank[6][:, 256:320].rearrange("p (s k) -> p s k", s=2), spread[:, P - shift:2 * P - shift],
                             mag[:, :, c, :], start=(c == 0), stop=(c == 31))
                ins.then_inc(tensor_spectrum.done("chan"), 1)

            def back(pr, u):
                i = 2 * pr + u
                pe.wait_ge(vector_gate.sem, vector_gate.at(i, "alg"))
                pe.wait_ge(scalar_taps.sem, scalar_taps.at(i, "t2"))
                for c in range(32):
                    ins = mm(bank[4][:, NG * c:NG * c + NG], GT[:, c * P:(c + 1) * P], ALG, start=True, stop=True)
                ins.then_inc(tensor_back.done("gsum"), 1)
                pe.wait_ge(vector_back.sem, vector_back.at(i, "gsum"))
                for n, (tap, d) in enumerate(SHIFT_PLAN):
                    mm(bank[5][:, 0:128], TP[:, tap, 1 + d:33 + d, :], shifts[:, n * P:(n + 1) * P],
                       start=(n == 0), stop=False)
                mm(bank[5][:, 0:128], TG, ident[:, :], start=False, stop=True).then_inc(tensor_back.done("wmap"), 1)
                pe.wait_ge(vector_spectrum.sem, vector_spectrum.at(i, "fm1"))
                for k in range(2):
                    ins = mm(bank[6][:, 64 * k:64 + 64 * k], resize[:, k * P:(k + 1) * P], FM, start=True, stop=True)
                ins.then_inc(tensor_back.done("fmap"), 1)
                pe.wait_ge(mapl, 16 * (8 * (i + 1)))
                for q in range(8):
                    if q < 2:
                        pe.wait_ge(vector_front.sem, vector_front.at(i, f"add{6 + q}"))
                    else:
                        pe.wait_ge(scalar_back.sem, scalar_back.at(i, f"sig{q - 2}"))
                    mm(bank[q % 2][:, :], argw[:, :], ROWS[:, q * 512:(q + 1) * 512], start=True,
                       stop=True).then_inc(tensor_back.done(f"arg{q}"), 1)

            def step(pr, u):
                front(pr, u)
                gate(pr, u)
                taps2(pr, u)
                logits(pr, u)
                spectrum(pr, u)
                back(pr, u)

            step(0, 0)
            step(0, 1)
            with pe.Fori(1, NT // 2) as pr:
                step(pr, 0)
                step(pr, 1)


def laid_out(inputs):
    g = {k: np.ascontiguousarray(v) for k, v in inputs.items()}

    def col(v):
        return np.tile(v.reshape(GC, -1), (NG, 1))

    return {
        "x": g["x"],
        "w_qkv_t": g["L0_conv_w_qkv"].T,
        "w_proj_t": g["L0_conv_w_proj"].T,
        "temperature": np.repeat(g["L0_conv_temperature"].reshape(2, 4), DPH, axis=1).T,
        "bn_gamma": g["L0_conv_bn_gamma"], "bn_beta": g["L0_conv_bn_beta"],
        "w1_t": g["L1_conv_w1"].T, "w_pw": g["L1_conv_w_pw"], "w_pw_t": g["L1_conv_w_pw"].T,
        "b1": col(g["L1_conv_b1"]), "gn_gamma": col(g["L1_conv_gn_gamma"]), "gn_beta": col(g["L1_conv_gn_beta"]),
        "w_dw": col(g["L1_conv_w_dw"]), "b_dw": col(g["L1_conv_b_dw"]), "b_pw": col(g["L1_conv_b_pw"]),
        "w_fp": col(g["L1_conv_w_fp"]), "b_fp": col(g["L1_conv_b_fp"]),
        "beta_row": np.tile(g["L1_conv_gn_beta"].reshape(1, GC), (P, 1)),
    }


def kernel(**inputs):
    import concourse.bacc as bacc
    from concourse.bass_utils import run_bass_kernel_spmd

    nc = bacc.Bacc("TRN2", target_bir_lowering=False, num_devices=1)
    arrays, args = {}, {}
    for name, v in {**laid_out(inputs), **constants()}.items():
        v = np.ascontiguousarray(v)
        arrays[f"in_{name}"] = v
        args[name] = nc.dram_tensor(f"in_{name}", v.shape, mybir.dt.from_np(v.dtype), kind="ExternalInput").ap()
    out = nc.dram_tensor("out", (B, CH, H, W), F32, kind="ExternalOutput").ap()
    build(nc, args, out)
    r = run_bass_kernel_spmd(nc, [arrays], core_ids=[0])
    return r.results[0]["out"]
```

```python
import math
from contextlib import ExitStack

import numpy as np

import concourse.bass as bass
from concourse import mybir

F32 = mybir.dt.float32
BF16 = mybir.dt.bfloat16
ALU = mybir.AluOpType
ACT = mybir.ActivationFunctionType
AX = mybir.AxisListType

B, CH, H, W = 16, 1024, 64, 64
PIX = H * W
P = 128
TPB = CH // P
NT = B * TPB
GC = 32
NG = P // GC
HEADS, DPH = 8, 32
TD = HEADS * DPH
PH = PW = 16
LOW = PH * PW
EPS = 1e-5
KW = W // 2 + 1
HH = H // 2
PARTS = 3
ARG_ROWS = PARTS * NG * (1 + PARTS)


def constants():
    c = {}
    k = np.arange(64)
    ang = 2 * math.pi * np.outer(k, k) / 64
    cos, sin = np.cos(ang) / 8, np.sin(ang) / 8
    fh = np.concatenate([cos[:, :33], sin[:, 1:32]], axis=1)
    c["dft_h"] = np.kron(np.eye(2), fh)
    wc = np.zeros((2, 64, 2, 2, 32))
    ws = np.zeros((2, 64, 2, 2, 32))
    for j in range(2):
        wc[j, :, 0, j], wc[j, :, 1, j] = cos[:, :32], sin[:, :32]
        ws[j, :, 0, j], ws[j, :, 1, j] = -sin[:, :32], cos[:, :32]
    c["dft_w"] = np.stack([wc.reshape(P, P), ws.reshape(P, P), -ws.reshape(P, P)], 1).reshape(P, 3 * P)
    spread = np.zeros((P, P))
    for p in range(P):
        spread[p, 64 + (p // 64) * 32 + (p // 32) % 2] = 1
    c["spread"] = spread
    ures = np.zeros((2, 32, 32))
    for i in range(64):
        x = min(max((i + 0.5) * 0.5 - 0.5, 0.0), 31.0)
        i0 = int(math.floor(x))
        i1 = min(i0 + 1, 31)
        ures[i % 2, i0, i // 2] += 1 - (x - i0)
        ures[i % 2, i1, i // 2] += x - i0
    c["resize"] = np.concatenate([np.einsum("gk,ci->gcik", np.eye(NG), ures[a] / KW).reshape(P, P)
                                   for a in range(2)], axis=1)
    shifts = []
    for dh in (-1, 0, 1):
        for dw in (-1, 0, 1):
            for d in (-1, 0, 1):
                m = np.zeros((2, 64, 2, 64))
                for ho in range(2):
                    hi = ho + dh - 2 * d
                    if 0 <= hi < 2:
                        for wo in range(64):
                            if 0 <= wo + dw < 64:
                                m[hi, wo + dw, ho, wo] = 1
                if m.any():
                    shifts.append(m.reshape(P, P))
    c["shifts"] = np.concatenate(shifts, axis=1)
    up = np.zeros((64, 16))
    for o in range(64):
        s = (o + 0.5) / 4 - 0.5
        i0 = math.floor(s)
        up[o, min(max(i0, 0), 15)] += 1 - (s - i0)
        up[o, min(max(i0 + 1, 0), 15)] += s - i0
    wr = np.array([[7, 1], [5, 3], [3, 5], [1, 7]]) / 8.0
    u = np.einsum("dr,ws->rsdw", wr, up).reshape(2, 1, 16, 256)
    c["upsample"] = np.broadcast_to(u.transpose(1, 0, 2, 3), (3, 2, 16, 256)).reshape(96, 256)
    g = up.T @ up
    kk = np.kron(g, g)
    c["up_gram"] = np.concatenate([kk[:P], kk[P:]], axis=1)
    c["ident"] = np.eye(P)
    c["group_ones"] = np.kron(np.eye(NG), np.ones((GC, GC)))
    c["group_sel"] = np.kron(np.eye(NG), np.ones((GC, 1)))
    c["group_cols"] = np.tile(np.kron(np.eye(NG), np.ones((GC, 1))), (1, HH))
    c["chan_sel"] = np.tile(np.eye(GC), (NG, 1))
    return {"c_" + n: np.ascontiguousarray(a, dtype=np.float32) for n, a in c.items()}


TAP_FILLS = [(0, 11), (11, 11), (22, 10)]
SHIFT_PLAN = [(kh * 3 + kw, d) for kh in range(3) for kw in range(3) for d in (-1, 0, 1)
              if any(0 <= ho + (kh - 1) - 2 * d < 2 for ho in range(2))]


class Steps:

    def __init__(self, sem, names):
        self.sem, self.names, self.pos = sem, names, 0

    def done(self, name):
        assert self.names[self.pos] == name, (self.names[self.pos], name)
        self.pos = (self.pos + 1) % len(self.names)
        return self.sem

    def at(self, i, name):
        return i * len(self.names) + self.names.index(name) + 1


def begun(i):
    return not isinstance(i, int) or i >= 0


def build(nc, a, out):
    ctx = ExitStack()
    x_tiles = a["x"].rearrange("b (t p) h w -> (b t) p (h w)", p=P)
    out_tiles = out.rearrange("b (t p) h w -> (b t) p (h w)", p=P)
    low3 = nc.dram_tensor("low3", [NT, 3, 18 * PW, P], BF16, kind="Internal").ap()

    turn = nc.dram_tensor("turn", [2, P, PIX], F32, kind="Internal").ap()
    map_turn = nc.dram_tensor("map_turn", [2, 3, NG, HH, P], BF16, kind="Internal").ap()

    with ctx:
        def sb(name, cols, dt=F32, parts=P):
            return ctx.enter_context(nc.sbuf_tensor(name, [parts, cols], dt))

        def sem(name):
            return ctx.enter_context(nc.semaphore(name))

        def steps(name, names):
            return Steps(sem(name), names)

        bank = [ctx.enter_context(nc.psum_tensor(f"bank{k}", [P, 512], F32)) for k in range(8)]

        ident = sb("ident", P)
        gones = sb("group_ones", P)
        gsel = sb("group_sel", NG)
        gcols = sb("group_cols", P)
        csel = sb("chan_sel", GC)
        dft_h = sb("dft_h", P)
        dft_w = sb("dft_w", 3 * P)
        spread = sb("spread", P)
        resize_half = sb("resize_half", 4 * P, F32, 64)
        resize = sb("resize", 2 * P)
        shifts = sb("shifts", len(SHIFT_PLAN) * P)
        upmat = sb("upmat", 256, BF16, 96)
        w1bd = sb("w1bd", P)
        wpbd = sb("wpbd", P)
        wptbd = sb("wptbd", P)
        colw = sb("colw", 16)
        B1, GAMMA, BETA, BDW, BPW, BFP = range(6)
        wdw = sb("wdw", 9)
        taps = sb("taps", P)
        half = sb("half", 2)
        argw = sb("argw", P, BF16, ARG_ROWS)
        fpw = sb("fpw", 4, BF16)
        argw_t = sb("argw_t", ARG_ROWS)
        wts0 = sb("wts0", 1)
        beta_row = sb("beta_row", GC)
        cw = sb("cw", 64)
        consts = [(ident, "c_ident"), (gones, "c_group_ones"), (gsel, "c_group_sel"), (csel, "c_chan_sel"), (gcols, "c_group_cols"),
                  (dft_h, "c_dft_h"), (dft_w, "c_dft_w"), 
                  (spread, "c_spread"), (resize, "c_resize"), (shifts, "c_shifts")]

        ARENA = 46000
        arena = sb("arena", ARENA)
        at = [0]

        def carve(cols, dt=F32, parts=P):
            n = cols if dt == F32 else cols // 2
            v = arena[0:parts, at[0]:at[0] + n]
            at[0] += n
            assert at[0] <= ARENA, at[0]
            return v if dt == F32 else v.bitcast(BF16)

        XR = 4
        oall = carve(2 * B * LOW).rearrange("p (o b l) -> p o b l", o=2, b=B)
        gram = carve(2 * LOW).rearrange("p (k l) -> p k l", k=2)
        wp = carve(2 * CH).rearrange("p (o c) -> p o c", o=2)
        cov = carve(2 * TD).rearrange("p (o d) -> p o d", o=2)
        mark = at[0]
        xr = [carve(PIX) for _ in range(XR)]
        wq = carve(TPB * 3 * TD).rearrange("p (t o) -> p t o", t=TPB)
        pooled = [carve(TPB * LOW).rearrange("p (t l) -> p t l", t=TPB) for _ in range(1)] * 2
        xn = carve(TPB * LOW).rearrange("p (t l) -> p t l", t=TPB)
        st = carve(2 * TPB)
        gn = carve(8 * TPB)
        tempc = carve(2)
        qk = carve(4 * LOW).rearrange("p (o l) -> p o l", o=4)
        qk2 = carve(4 * LOW).rearrange("p (o l) -> p o l", o=4)
        vt = carve(2 * TD).rearrange("p (m d) -> p m d", m=2)
        prob = carve(2 * LOW).rearrange("p (l m) -> p l m", l=2)
        probT = carve(2 * LOW).rearrange("p (m l) -> p m l", m=2)
        hc = carve(8)
        oT = carve(2 * TD).rearrange("p (l d) -> p l d", l=2)
        ko = carve(2 * TD).rearrange("p (l d) -> p l d", l=2)
        junk1 = carve(PIX, BF16)
        at[0] = mark
        omean = carve(2)
        zw = carve(2 * CH).rearrange("p (o c) -> p o c", o=2)
        wm = carve(2 * CH).rearrange("p (o c) -> p o c", o=2)
        bmean, bvar, bgam, bbet = carve(CH), carve(CH), carve(CH), carve(CH)
        ob = carve(2 * LOW).rearrange("p (o l) -> p o l", o=2)
        ylow = carve(CH)
        part = [[carve(CH, BF16) for _ in range(3)] for _ in range(2)]
        ones = carve(P)

        at[0] = 0
        X = [carve(PIX) for _ in range(2)]
        YS = [carve(17 * P, BF16, 96).rearrange("p (i c) -> p i c", i=17) for _ in range(2)]
        GT = carve(PIX)
        G2 = carve(PIX)
        AH = carve(PIX)
        MAG = carve(2048)
        SQ = [carve(512) for _ in range(2)]
        SIG = [carve(1024) for _ in range(4)]
        TR = carve(2048)
        JUNK = carve(PIX, BF16)
        TP = carve(9 * NG * 34).rearrange("p (t h g) -> p t h g", t=9, g=NG)
        TG = carve(NG * HH)
        ROWS = carve(PIX, BF16, ARG_ROWS)
        RC = carve(P)
        CATS = [carve(P) for _ in range(2)]
        FRL = carve(GC)
        EDGE = carve(6)
        POWER = carve(1)
        SHW = [carve(P) for _ in range(2)]
        PAR = [carve(32) for _ in range(2)]
        SM = carve(64)
        FR = carve(32)
        ALG = carve(P)
        EO = carve(P)
        ALT = [carve(64) for _ in range(2)]
        ALTT = carve(P, F32, 64)
        SQN = carve(64)
        NYM = carve(64)
        FM = carve(P, F32, 64)
        MAP = carve(2 * PARTS * P, BF16).rearrange("p (m s x) -> p m s x", m=2, s=PARTS)
        REST = [carve(P) for _ in range(2)]

        cst = sem("consts_landed")
        upl = sem("upmat_landed")
        zeroed = sem("tables_zeroed")
        blocks = sem("blocks_landed")
        xl = [sem(f"x_slot{k}_landed") for k in range(XR)]
        vector_setup = steps("vector_setup", ["wfp", "sel", "hi", "hif", "r1", "mid", "midf", "lo", "selw0", "selw1", "selw2", "max", "rsum", "s1", "p", "wp9", "taps", "c0", "c1", "wts0", "argw", "half0", "half1"])
        scalar_setup = steps("scalar_setup", ["exprow", "expcol"])
        tensor_setup = steps("tensor_setup", ["argw", "p", "const"])
        vector_pool = steps("vector_pool", ["pool", "sum"])
        scalar_squares = steps("scalar_squares", ["sq"])
        tensor_imagestats = steps("tensor_imagestats", ["stats"])
        vector_imagestats = steps("vector_imagestats", ["mean", "msq", "var0", "var", "rstd", "r16", "shift"]
                      + [f"xn{t}" for t in range(TPB)])
        scalar_imagestats = steps("scalar_imagestats", ["std"])
        tensor_qkv = steps("tensor_qkv", ["qk", "v", "norms"])
        vector_qkv = steps("vector_qkv", ["copy", "v", "floor", "recip", "qn", "kn"])
        scalar_qkv = steps("scalar_qkv", ["sq", "norm"])
        tensor_head = steps("tensor_head", ["scores", "transpose", "out"])
        vector_head = steps("vector_head", ["max", "rsum", "scale0", "scale1", "probT"])
        scalar_head = steps("scalar_head", ["exp0", "exp1"])
        tensor_image_end = steps("tensor_image_end", ["ko", "cov"])
        vector_image_end = steps("vector_image_end", ["o", "oT", "ko", "cov"])
        vector_taps_zero = steps("vector_taps_zero", ["zero"])
        vector_cov_zero = steps("vector_cov_zero", ["zero"])
        bnl = sem("bn_rows_landed")
        vector_bn = steps("vector_bn", ["ones", "osum0", "osum1", "omean", "zw0", "zw1", "zw2", "zw3", "wm0", "wm1",
                                   "mean0", "mean1", "e0", "e1", "msq", "var", "eps", "rstd", "scale", "ms", "shift"])
        tensor_bn = steps("tensor_bn", ["z", "mean", "sq"])
        scalar_bn = steps("scalar_bn", ["std"])
        vector_low = steps("vector_low", ["ob"] + [f"{n}{k}" for k in range(2)
                                            for n in ("mul0", "mul1", "add", "hi", "r1", "mid", "lo")])
        tensor_low = steps("tensor_low", ["y0", "y1"])
        lows = [sem(f"low_parts{k}_stored") for k in range(2)]
        XL = [[sem(f"tile_slot{k}_quarter{q}_landed") for q in range(4)] for k in range(2)]
        YL = [sem(f"low_slot{k}_landed") for k in range(2)]
        tensor_front = steps("tensor_front", [f"up{q}" for q in range(8)] + ["stats"])
        vector_front = steps("vector_front", [f"add{q}" for q in range(8)]
                   + ["pairs", "rows", "alt", "total", "mean", "msq", "var", "shift", "std", "offset", "r64", "altn", "gx", "cat"])
        scalar_front = steps("scalar_front", ["sq"])
        pool_front = steps("pool_front", [f"col{k}" for k in range(6)] + ["rstd"])
        pool_gate = steps("pool_gate", ["rstd"])
        vector_pads = steps("vector_pads", ["edge", "alpha"])
        turned = sem("gx_in_dram")
        g2l = sem("rows_layout_landed")
        tensor_gate = steps("tensor_gate", ["w1", "pw", "lrow", "const"])
        scalar_gate = steps("scalar_gate", ["sig", "sq", "exprow", "expcol"])
        vector_gate = steps("vector_gate", ["tot", "edges0", "edges1", "f0", "f1", "corner", "fw", "dw",
                                   "dwb", "gates", "t1", "x2m", "lsel", "gated", "gmean", "gmsq", "max", "gvar", "rsum", "s2",
                                   "sg", "alpha", "alg", "am", "kc", "kcon"])
        tensor_taps = steps("tensor_taps", ["t0", "t1", "t2"])
        scalar_taps = steps("scalar_taps", ["t0", "t1", "t2"])
        tensor_spectrum = steps("tensor_spectrum", ["nyqt"] + [f"h{k}" for k in range(8)] + ["nyq"]
                                + [f"w{k}" for k in range(8)] + ["chan"])
        scalar_spectrum = steps("scalar_spectrum", ["nyqt"] + [f"h{k}" for k in range(8)] + ["nyqsq"]
                                + [f"w{k}" for k in range(4)] + ["nyqroot0", "nyqroot", "w4", "w5", "root0", "w6", "w7", "root1"])
        vector_spectrum = steps("vector_spectrum", ["nyq"] + [f"w{k}" for k in range(8)] + ["fm0", "fm1"])
        tensor_back = steps("tensor_back", ["gsum", "wmap", "fmap"] + [f"arg{q}" for q in range(8)])
        vector_back = steps("vector_back", ["gsum", "whi", "wrest", "wmid", "wmap", "fhi", "frest", "fmid", "fmap"] + [f"mul{q}" for q in range(4)])
        scalar_back = steps("scalar_back", [f"sig{q}" for q in range(8)] + [f"mean{q}" for q in range(4)])
        map_stored = sem("map_parts_stored")
        mapl = sem("map_rows_landed")
        stored = [sem(f"out_slot{k}_stored") for k in range(4)]
        pads = sem("pads_zeroed")

        block = ctx.enter_context(nc.Block())
        N_CONST = len(consts) + 7 + 8

        @block.sync
        def _(sp):
            for dst, name in consts:
                sp.dma_start(dst[:, :], a[name]).then_inc(cst, 16)
            for k, name in enumerate(["b1", "gn_gamma", "gn_beta", "b_dw", "b_pw", "b_fp"]):
                sp.dma_start(colw[:, k:k + 1], a[name]).then_inc(cst, 16)
            sp.dma_start(wdw[:, :], a["w_dw"]).then_inc(cst, 16)
            for j in range(2):
                sp.dma_start(resize_half[:, j * 2 * P:(j + 1) * 2 * P],
                             a["c_resize"][64 * j:64 * j + 64, :]).then_inc(cst, 16)
            sp.dma_start(gram, a["c_up_gram"].rearrange("p (k l) -> p k l", k=2)).then_inc(cst, 16)
            sp.dma_start(wp, a["w_proj_t"].rearrange("(o p) c -> p o c", p=P)).then_inc(cst, 16)
            sp.dma_start(wq, a["w_qkv_t"].rearrange("(t p) o -> p t o", p=P)).then_inc(cst, 16)
            sp.dma_start(tempc, a["temperature"]).then_inc(cst, 16)
            sp.dma_start(beta_row[:, :], a["beta_row"]).then_inc(cst, 16)
            sp.dma_start(cw[:, 0:32], a["w_fp"]).then_inc(cst, 16)
            sp.wait_ge(zeroed, 1)
            for g in range(NG):
                s = slice(g * GC, g * GC + GC)
                sp.dma_start(w1bd[s, s], a["w1_t"]).then_inc(blocks, 16)
                sp.dma_start(wpbd[s, s], a["w_pw"]).then_inc(blocks, 16)
                sp.dma_start(wptbd[s, s], a["w_pw_t"]).then_inc(blocks, 16)

            def load1(b, s):
                n = b * TPB + s - XR
                if begun(n):
                    sp.wait_ge(scalar_squares.sem, scalar_squares.at(n, "sq"))
                    sp.wait_ge(vector_pool.sem, vector_pool.at(n, "pool"))
                sp.dma_start(xr[s % XR], x_tiles[b * TPB + s]).then_inc(xl[s % XR], 16)

            for s in range(TPB):
                load1(0, s)
            with sp.Fori(1, B) as b:
                for s in range(TPB):
                    load1(b, s)

            sp.wait_ge(vector_image_end.sem, vector_image_end.at(B - 1, "cov"))
            sp.wait_ge(tensor_image_end.sem, tensor_image_end.at(B - 1, "cov"))
            sp.dma_start(bgam, a["bn_gamma"].partition_broadcast(P)).then_inc(bnl, 16)
            sp.dma_start(bbet, a["bn_beta"].partition_broadcast(P)).then_inc(bnl, 16)
            with sp.Fori(0, B) as b:
                for k in range(2):
                    for s in range(3):
                        sp.wait_ge(vector_low.sem, vector_low.at(b, ("hi", "mid", "lo")[s] + str(k)))
                        dst = low3[bass.ds(b * TPB, TPB), s]
                        dst = dst.rearrange("t q c -> q t c")
                        src = part[k][s].rearrange("p (t c) -> p t c", t=TPB)
                        sp.dma_start(dst[16 + k * P:16 + (k + 1) * P], src).then_inc(lows[k], 16)
                        if k == 0:
                            sp.dma_start(dst[0:16], src[0:16]).then_inc(lows[k], 16)
                        else:
                            sp.dma_start(dst[272:288], src[112:128]).then_inc(lows[k], 16)
            sp.wait_ge(lows[0], 16 * (6 * B))
            sp.wait_ge(lows[1], 16 * (6 * B))

            def load_low(i, u):
                if begun(i - 2):
                    sp.wait_ge(tensor_front.sem, tensor_front.at(i - 2, "up7"))
                for s in range(3):
                    for r in range(2):
                        p0 = s * 32 + r * 16
                        sp.dma_start(YS[u][p0:p0 + 16], low3[i, s, r * 16:r * 16 + 272, :].rearrange(
                            "(k q) c -> q k c", q=16)).then_inc(YL[u], 16)

            def load_quarter(i, u, q):
                if begun(i - 2):
                    sp.wait_ge(vector_back.sem, vector_back.at(i - 2, f"mul{q}"))
                s = slice(q * 1024, (q + 1) * 1024)
                sp.dma_start(X[u][:, s], x_tiles[i][:, s]).then_inc(XL[u][q], 16)

            def turn_out(i, u):
                sp.wait_ge(vector_front.sem, vector_front.at(i, "gx"))
                sp.dma_start(turn[u], X[u]).then_inc(turned, 16)

            def turn_in(i, u):
                sp.wait_ge(turned, 16 * (i + 1))
                if begun(i - 1):
                    sp.wait_ge(tensor_spectrum.sem, tensor_spectrum.at(i - 1, "h7"))
                for j in range(2):
                    sp.dma_start(G2[64 * j:64 * j + 64, :].rearrange("h (c w) -> h c w", c=64),
                                 turn[u, 64 * j:64 * j + 64, :].rearrange("c (h w) -> h c w", h=64)).then_inc(g2l, 16)

            def map_out(i, m):
                sp.wait_ge(vector_back.sem, vector_back.at(i, ("wmap", "fmap")[m]))
                if m == 0 and begun(i - 1):
                    sp.wait_ge(mapl, 16 * ((1 + PARTS) * i))
                for s in range(PARTS):
                    sp.dma_start(map_turn[m, s].rearrange("g h x -> h g x"), MAP[:, m, s, :]).then_inc(map_stored, 16)

            def map_in(i, m):
                sp.wait_ge(map_stored, 16 * (2 * PARTS * i + PARTS * (1 + m)))
                if m == 0 and begun(i - 1):
                    sp.wait_ge(tensor_back.sem, tensor_back.at(i - 1, "arg7"))
                n = PARTS * NG
                for j in range((1, PARTS)[m]):
                    r = n * (m + j)
                    sp.dma_start(ROWS[r:r + n, :], map_turn[m].rearrange("s g h x -> (s g) (h x)")).then_inc(mapl, 16)

            def store_quarter(i, q):
                sp.wait_ge(scalar_back.sem, scalar_back.at(i, f"mean{q}"))
                sp.dma_start(out_tiles[i][:, q * 1024:(q + 1) * 1024], SIG[q]).then_inc(stored[q], 16)

            def period(i, u, new=True, load=True):
                if load:
                    load_low(i + 2, u)
                map_out(i, 0)
                if new:
                    turn_out(i + 1, 1 - u)
                map_in(i, 0)
                if new:
                    turn_in(i + 1, 1 - u)
                map_out(i, 1)
                map_in(i, 1)
                if load:
                    for q in range(4):
                        load_quarter(i + 2, u, q)
                for q in range(4):
                    store_quarter(i, q)

            for u in range(2):
                load_low(u, u)
                for q in range(4):
                    load_quarter(u, u, q)
            turn_out(0, 0)
            turn_in(0, 0)
            period(0, 0)
            period(1, 1)
            with sp.Fori(1, NT // 2 - 1) as pr:
                period(2 * pr, 0)
                period(2 * pr + 1, 1)
            period(NT - 2, 0, load=False)
            period(NT - 1, 1, new=False, load=False)
            for q in range(4):
                sp.wait_ge(stored[q], 16 * NT)

        @block.gpsimd
        def _(pool):
            pool.memset(w1bd[:, :], 0.0)
            pool.memset(wpbd[:, :], 0.0)
            pool.memset(wptbd[:, :], 0.0).then_inc(zeroed, 1)
            pool.dma_start(upmat[:, :], a["c_upsample"]).then_inc(upl, 16)

            pool.wait_ge(lows[0], 16 * (6 * B))
            pool.wait_ge(lows[1], 16 * (6 * B))
            pool.wait_ge(vector_low.sem, vector_low.at(B - 1, "lo1"))
            pool.wait_ge(tensor_low.sem, tensor_low.at(B - 1, "y1"))
            pool.memset(POWER, -0.5).then_inc(pads, 1)
            pool.memset(TP, 0.0).then_inc(pads, 1)
            pool.wait_ge(pads, 2)

            def front(i, u):
                pool.wait_ge(vector_front.sem, vector_front.at(i, "add7"))
                if begun(i - 1):
                    pool.wait_ge(vector_front.sem, vector_front.at(i - 1, "cat"))
                pool.tensor_tensor(TR[:, 0:2048], X[u][:, 0:2048], X[u][:, 2048:4096],
                                   op=ALU.add).then_inc(pool_front.done("col0"), 1)
                n = 1024
                for k in range(1, 6):
                    pool.wait_ge(pool_front.sem, pool_front.at(i, f"col{k - 1}"))
                    dst = RC[:, 64:128] if n == 64 else TR[:, 0:n]
                    pool.tensor_tensor(dst, TR[:, 0:n], TR[:, n:2 * n], op=ALU.add).then_inc(pool_front.done(f"col{k}"), 1)
                    n //= 2
                pool.wait_ge(vector_front.sem, vector_front.at(i, "var"))
                pool.tensor_tensor(PAR[u][:, 6:7], PAR[u][:, 4:5], POWER, op=ALU.pow).then_inc(pool_front.done("rstd"), 1)
                pool.wait_ge(vector_gate.sem, vector_gate.at(i, "gvar"))
                pool.tensor_tensor(SM[:, 6:7], SM[:, 4:5], POWER, op=ALU.pow).then_inc(pool_gate.done("rstd"), 1)

            front(0, 0)
            front(1, 1)
            with pool.Fori(1, NT // 2) as pr:
                front(2 * pr, 0)
                front(2 * pr + 1, 1)

        @block.scalar
        def _(act):
            act.wait_ge(vector_setup.sem, vector_setup.at(0, "max"))
            act.activation(beta_row[:, :], beta_row[:, :], ACT.Exp, bias=cw[:, 33:34],
                           accum_out=cw[:, 40:41]).then_inc(scalar_setup.done("exprow"), 1)
            act.activation(cw[:, 41:42], colw[:, BETA:BETA + 1], ACT.Exp, bias=cw[:, 33:34]).then_inc(scalar_setup.done("expcol"), 1)

            def square1(b, s):
                act.wait_ge(xl[s % XR], 16 * (2 * b + s // XR + 1))
                if s == 0:
                    if begun(b - 1):
                        act.wait_ge(tensor_imagestats.sem, tensor_imagestats.at(b - 1, "stats"))
                if begun(b * TPB + s - 1):
                    act.wait_ge(scalar_squares.sem, scalar_squares.at(b * TPB + s - 1, "sq"))
                act.activation(junk1, xr[s % XR], ACT.Square, accum_out=st[:, TPB + s:TPB + s + 1]).then_inc(scalar_squares.done("sq"), 1)

            def image1(b):
                act.wait_ge(vector_imagestats.sem, vector_imagestats.at(b, "var"))
                act.activation(gn[:, 24:32], gn[:, 16:24], ACT.Sqrt).then_inc(scalar_imagestats.done("std"), 1)
                act.wait_ge(vector_qkv.sem, vector_qkv.at(b, "copy"))
                act.activation(qk2, qk, ACT.Square).then_inc(scalar_qkv.done("sq"), 1)
                act.wait_ge(tensor_qkv.sem, tensor_qkv.at(b, "norms"))
                act.activation(qk2[:, 0:2, :], bank[4][:, :].rearrange("p (o l) -> p o l", o=2), ACT.Sqrt)
                act.activation(qk2[:, 2:4, :], bank[5][:, :].rearrange("p (o l) -> p o l", o=2),
                               ACT.Sqrt).then_inc(scalar_qkv.done("norm"), 1)

            def head1(n):
                act.wait_ge(vector_head.sem, vector_head.at(n, "max"))
                for l in range(2):
                    act.activation(prob[:, l, :], bank[6][:, l * LOW:(l + 1) * LOW], ACT.Exp, bias=hc[:, l:l + 1],
                                   accum_out=hc[:, 2 + l:3 + l]).then_inc(scalar_head.done(f"exp{l}"), 1)

            for s in range(TPB):
                square1(0, s)
            image1(0)

            def image_step(b):
                for s in range(TPB):
                    square1(b, s)
                    head1((b - 1) * TPB + s)
                image1(b)

            image_step(1)
            with act.Fori(2, B) as b:
                image_step(b)
            for s in range(TPB):
                head1((B - 1) * TPB + s)

            act.wait_ge(vector_bn.sem, vector_bn.at(0, "eps"))
            act.activation(bvar, bvar, ACT.Sqrt).then_inc(scalar_bn.done("std"), 1)

            act.wait_ge(vector_setup.sem, vector_setup.at(0, "half1"))

            def front(i, u):
                act.wait_ge(vector_front.sem, vector_front.at(i, "add7"))
                if begun(i - 1):
                    act.wait_ge(tensor_front.sem, tensor_front.at(i - 1, "stats"))
                    act.wait_ge(scalar_gate.sem, scalar_gate.at(i - 1, "sq"))
                act.activation(JUNK, X[u], ACT.Square, accum_out=PAR[u][:, 1:2]).then_inc(scalar_front.done("sq"), 1)

            def gate(i, u):
                act.wait_ge(tensor_gate.sem, tensor_gate.at(i, "w1"))
                act.activation(SHW[u], bank[7][:, 128:256], ACT.Tanh, bias=half[:, 0:1],
                               scale=0.5).then_inc(scalar_gate.done("sig"), 1)

            def gate_stats(i):
                act.wait_ge(vector_gate.sem, vector_gate.at(i, "gated"))
                act.wait_ge(scalar_front.sem, scalar_front.at(i, "sq"))
                act.activation(JUNK, GT, ACT.Square, accum_out=SM[:, 1:2]).then_inc(scalar_gate.done("sq"), 1)

            def gate_softmax(i):
                act.wait_ge(vector_gate.sem, vector_gate.at(i, "max"))
                act.activation(FR, bank[7][:, 320:352], ACT.Exp, bias=SM[:, 10:11],
                               accum_out=SM[:, 11:12]).then_inc(scalar_gate.done("exprow"), 1)
                act.activation(SM[:, 12:13], SM[:, 9:10], ACT.Exp, bias=SM[:, 10:11]).then_inc(scalar_gate.done("expcol"), 1)

            def taps2(i):
                for k, (c0, n) in enumerate(TAP_FILLS):
                    act.wait_ge(tensor_taps.sem, tensor_taps.at(i, f"t{k}"))
                    if k == 0:
                        if begun(i - 1):
                            act.wait_ge(tensor_back.sem, tensor_back.at(i - 1, "wmap"))
                    act.activation(TP[:, :, 1 + c0:1 + c0 + n, :],
                                   bank[4 + k % 2][:, 0:36 * n].rearrange("p (c t g) -> p t c g", t=9, g=NG),
                                   ACT.Copy).then_inc(scalar_taps.done(f"t{k}"), 1)
                    if k == 0:
                        gate_stats(i)

            def nyquist_turned(i):
                act.wait_ge(tensor_spectrum.sem, tensor_spectrum.at(i, "nyqt"))
                if begun(i - 1):
                    act.wait_ge(tensor_spectrum.sem, tensor_spectrum.at(i - 1, "nyq"))
                act.activation(ALTT, bank[6][0:64, 384:512], ACT.Copy).then_inc(scalar_spectrum.done("nyqt"), 1)

            def rows_done(i, k):
                act.wait_ge(tensor_spectrum.sem, tensor_spectrum.at(i, f"h{k}"))
                if k == 0 and begun(i - 1):
                    act.wait_ge(tensor_spectrum.sem, tensor_spectrum.at(i - 1, "w7"))
                act.activation(AH[:, k * 512:(k + 1) * 512], bank[2 + k % 2][:, :],
                               ACT.Copy).then_inc(scalar_spectrum.done(f"h{k}"), 1)

            def spectrum(i, u, new):
                act.wait_ge(tensor_spectrum.sem, tensor_spectrum.at(i, "nyq"))
                if begun(i - 1):
                    act.wait_ge(scalar_spectrum.sem, scalar_spectrum.at(i - 1, "nyqroot"))
                act.activation(SQN, bank[6][:, 384:448], ACT.Square).then_inc(scalar_spectrum.done("nyqsq"), 1)
                for k in range(8):
                    act.wait_ge(tensor_spectrum.sem, tensor_spectrum.at(i, f"w{k}"))
                    if k >= 2:
                        act.wait_ge(vector_spectrum.sem, vector_spectrum.at(i, f"w{k - 2}"))
                    elif begun(i - 1):
                        act.wait_ge(vector_spectrum.sem, vector_spectrum.at(i - 1, f"w{k + 6}"))
                    act.activation(SQ[k % 2], bank[2 + k % 2][:, :], ACT.Square).then_inc(scalar_spectrum.done(f"w{k}"), 1)
                    if k == 1 and new:
                        gate(i + 1, 1 - u)
                    elif k == 3:
                        nyquist_root(i)
                    elif k == 5:
                        act.wait_ge(vector_spectrum.sem, vector_spectrum.at(i, "w3"))
                        act.activation(MAG[:, 0:1024], MAG[:, 0:1024], ACT.Sqrt).then_inc(scalar_spectrum.done("root0"), 1)
                act.wait_ge(vector_spectrum.sem, vector_spectrum.at(i, "w7"))
                act.activation(MAG[:, 1024:2048], MAG[:, 1024:2048], ACT.Sqrt).then_inc(scalar_spectrum.done("root1"), 1)

            def nyquist_root(i):
                act.wait_ge(vector_spectrum.sem, vector_spectrum.at(i, "nyq"))
                if begun(i - 1):
                    act.wait_ge(tensor_back.sem, tensor_back.at(i - 1, "fmap"))
                act.activation(NYM[:, 0:33], SQN[:, 0:33], ACT.Sqrt).then_inc(scalar_spectrum.done("nyqroot0"), 1)
                act.activation(NYM[:, 33:64], SQN[:, 31:0:-1], ACT.Sqrt).then_inc(scalar_spectrum.done("nyqroot"), 1)

            def back(i, u):
                for q in range(8):
                    act.wait_ge(tensor_back.sem, tensor_back.at(i, f"arg{q}"))
                    if q % 2 == 0:
                        if begun(i - 1):
                            act.wait_ge(stored[q // 2], 16 * (i))
                    act.activation(SIG[q // 2][:, (q % 2) * 512:(q % 2 + 1) * 512], bank[q % 4][:, :], ACT.Tanh,
                                   bias=half[:, 1:2], scale=0.5).then_inc(scalar_back.done(f"sig{q}"), 1)
                for q in range(4):
                    act.wait_ge(vector_back.sem, vector_back.at(i, f"mul{q}"))
                    act.activation(SIG[q], SIG[q], ACT.Identity, bias=PAR[u][:, 2:3],
                                   scale=0.5).then_inc(scalar_back.done(f"mean{q}"), 1)

            def period(i, u, new=True):
                nyquist_turned(i)
                for k in range(8):
                    rows_done(i, k)
                if new:
                    front(i + 1, 1 - u)
                spectrum(i, u, new)
                if new:
                    taps2(i + 1)
                    gate_softmax(i + 1)
                back(i, u)

            front(0, 0)
            gate(0, 0)
            taps2(0)
            gate_softmax(0)
            period(0, 0)
            period(1, 1)
            with act.Fori(1, NT // 2 - 1) as pr:
                period(2 * pr, 0)
                period(2 * pr + 1, 1)
            period(NT - 2, 0)
            period(NT - 1, 1, new=False)

        @block.vector
        def _(dve):
            dve.wait_ge(cst, 16 * N_CONST)
            dve.memset(taps[:, :], 0.0).then_inc(vector_taps_zero.done("zero"), 1)
            dve.memset(cov, 0.0).then_inc(vector_cov_zero.done("zero"), 1)
            dve.tensor_reduce(cw[:, 32:33], cw[:, 0:32], axis=AX.X, op=ALU.add).then_inc(vector_setup.done("wfp"), 1)
            dve.wait_ge(vector_setup.sem, vector_setup.at(0, "wfp"))
            by_group = gsel[:, :].unsqueeze(1).to_broadcast([P, PARTS, NG])
            aw = argw_t[:, :].rearrange("p (j s g) -> p j s g", j=1 + PARTS, s=PARTS)
            dve.tensor_copy(aw[:, 0], by_group).then_inc(vector_setup.done("sel"), 1)
            dve.tensor_copy(fpw[:, 0:1], cw[:, 32:33]).then_inc(vector_setup.done("hi"), 1)
            dve.wait_ge(vector_setup.sem, vector_setup.at(0, "hi"))
            dve.tensor_copy(cw[:, 44:45], fpw[:, 0:1]).then_inc(vector_setup.done("hif"), 1)
            dve.tensor_tensor(cw[:, 47:48], cw[:, 32:33], fpw[:, 0:1], op=ALU.subtract).then_inc(vector_setup.done("r1"), 1)
            dve.wait_ge(vector_setup.sem, vector_setup.at(0, "r1"))
            dve.tensor_copy(fpw[:, 1:2], cw[:, 47:48]).then_inc(vector_setup.done("mid"), 1)
            dve.wait_ge(vector_setup.sem, vector_setup.at(0, "mid"))
            dve.tensor_copy(cw[:, 45:46], fpw[:, 1:2]).then_inc(vector_setup.done("midf"), 1)
            dve.tensor_tensor(cw[:, 46:47], cw[:, 47:48], fpw[:, 1:2], op=ALU.subtract).then_inc(vector_setup.done("lo"), 1)
            dve.wait_ge(vector_setup.sem, vector_setup.at(0, "lo"))
            for j in range(PARTS):
                dve.tensor_scalar(aw[:, 1 + j], by_group, cw[:, 44 + j:45 + j], None,
                                  ALU.mult).then_inc(vector_setup.done(f"selw{j}"), 1)
            dve.tensor_reduce(cw[:, 33:34], beta_row[:, :], axis=AX.X, op=ALU.max,
                              negate=True).then_inc(vector_setup.done("max"), 1)
            dve.wait_ge(scalar_setup.sem, scalar_setup.at(0, "expcol"))
            dve.reciprocal(cw[:, 34:35], cw[:, 40:41]).then_inc(vector_setup.done("rsum"), 1)
            dve.wait_ge(vector_setup.sem, vector_setup.at(0, "rsum"))
            dve.tensor_tensor(cw[:, 35:36], cw[:, 41:42], cw[:, 34:35], op=ALU.mult).then_inc(vector_setup.done("s1"), 1)
            dve.wait_ge(tensor_setup.sem, tensor_setup.at(0, "p"))
            dve.tensor_copy(cw[:, 42:43], bank[0][:, 0:1]).then_inc(vector_setup.done("p"), 1)
            dve.wait_ge(vector_setup.sem, vector_setup.at(0, "p"))
            dve.tensor_scalar(cw[:, 52:61], wdw[:, :], cw[:, 42:43], None, ALU.mult).then_inc(vector_setup.done("wp9"), 1)
            dve.wait_ge(vector_setup.sem, vector_setup.at(0, "wp9"))
            dve.wait_ge(vector_taps_zero.sem, vector_taps_zero.at(0, "zero"))
            dve.tensor_tensor(taps[:, 0:36].rearrange("p (t g) -> p t g", g=NG),
                              cw[:, 52:61].unsqueeze(2).to_broadcast([P, 9, NG]),
                              gsel[:, :].unsqueeze(1).to_broadcast([P, 9, NG]), op=ALU.mult).then_inc(vector_setup.done("taps"), 1)
            dve.tensor_tensor(cw[:, 36:37], cw[:, 35:36], colw[:, BPW:BPW + 1], op=ALU.mult).then_inc(vector_setup.done("c0"), 1)
            dve.wait_ge(vector_setup.sem, vector_setup.at(0, "c0"))
            dve.scalar_tensor_tensor(cw[:, 43:44], colw[:, BDW:BDW + 1], cw[:, 42:43], cw[:, 36:37],
                                     op0=ALU.mult, op1=ALU.add).then_inc(vector_setup.done("c1"), 1)
            dve.wait_ge(tensor_setup.sem, tensor_setup.at(0, "const"))
            dve.tensor_copy(wts0[:, :], bank[0][:, 1:2]).then_inc(vector_setup.done("wts0"), 1)
            dve.tensor_copy(argw[:, :], bank[0][0:ARG_ROWS, 128:256]).then_inc(vector_setup.done("argw"), 1)
            dve.tensor_scalar(half[:, 0:1], colw[:, B1:B1 + 1], 0.5, None, ALU.mult).then_inc(vector_setup.done("half0"), 1)
            dve.tensor_scalar(half[:, 1:2], colw[:, BFP:BFP + 1], 0.5, None, ALU.mult).then_inc(vector_setup.done("half1"), 1)

            def pool1(b, s):
                dve.wait_ge(xl[s % XR], 16 * (2 * b + s // XR + 1))
                dve.tensor_reduce(pooled[0][:, s, :].rearrange("p (r c) -> p r c", r=PH),
                                  xr[s % XR].rearrange("p (r a c e) -> p r c a e", r=PH, a=4, c=PW),
                                  axis=AX.XY, op=ALU.add).then_inc(vector_pool.done("pool"), 1)
                dve.wait_ge(vector_pool.sem, vector_pool.at(b * TPB + s, "pool"))
                if s == 0:
                    if begun(b - 1):
                        dve.wait_ge(tensor_imagestats.sem, tensor_imagestats.at(b - 1, "stats"))
                dve.tensor_reduce(st[:, s:s + 1], pooled[0][:, s, :], axis=AX.X, op=ALU.add).then_inc(vector_pool.done("sum"), 1)

            def image1(b):
                dve.wait_ge(tensor_imagestats.sem, tensor_imagestats.at(b, "stats"))
                n = 1.0 / (GC * PIX)
                dve.tensor_scalar(gn[:, 0:8], bank[0][:, 0:8], n, None, ALU.mult).then_inc(vector_imagestats.done("mean"), 1)
                dve.wait_ge(vector_imagestats.sem, vector_imagestats.at(b, "mean"))
                dve.tensor_tensor(gn[:, 8:16], gn[:, 0:8], gn[:, 0:8], op=ALU.mult).then_inc(vector_imagestats.done("msq"), 1)
                dve.wait_ge(vector_imagestats.sem, vector_imagestats.at(b, "msq"))
                dve.scalar_tensor_tensor(gn[:, 16:24], bank[0][:, 8:16], n, gn[:, 8:16], op0=ALU.mult,
                                         op1=ALU.subtract).then_inc(vector_imagestats.done("var0"), 1)
                dve.wait_ge(vector_imagestats.sem, vector_imagestats.at(b, "var0"))
                dve.tensor_scalar(gn[:, 16:24], gn[:, 16:24], EPS, None, ALU.add).then_inc(vector_imagestats.done("var"), 1)
                dve.wait_ge(scalar_imagestats.sem, scalar_imagestats.at(b, "std"))
                dve.reciprocal(gn[:, 32:40], gn[:, 24:32]).then_inc(vector_imagestats.done("rstd"), 1)
                dve.wait_ge(vector_imagestats.sem, vector_imagestats.at(b, "rstd"))
                dve.tensor_scalar(gn[:, 40:48], gn[:, 32:40], 1.0 / 16, None, ALU.mult).then_inc(vector_imagestats.done("r16"), 1)
                dve.scalar_tensor_tensor(gn[:, 48:56], gn[:, 0:8], -1.0, gn[:, 32:40], op0=ALU.mult,
                                         op1=ALU.mult).then_inc(vector_imagestats.done("shift"), 1)
                dve.wait_ge(vector_imagestats.sem, vector_imagestats.at(b, "shift"))
                if begun(b - 1):
                    dve.wait_ge(tensor_qkv.sem, tensor_qkv.at(b - 1, "v"))
                for t in range(TPB):
                    dve.tensor_scalar(xn[:, t, :], pooled[0][:, t, :], gn[:, 40 + t:41 + t], gn[:, 48 + t:49 + t],
                                      ALU.mult, ALU.add).then_inc(vector_imagestats.done(f"xn{t}"), 1)
                dve.wait_ge(tensor_qkv.sem, tensor_qkv.at(b, "qk"))
                dve.tensor_copy(qk[:, 0:2, :], bank[1][:, :].rearrange("p (o l) -> p o l", o=2))
                dve.tensor_copy(qk[:, 2:4, :], bank[2][:, :].rearrange("p (o l) -> p o l", o=2)).then_inc(vector_qkv.done("copy"), 1)
                dve.wait_ge(tensor_qkv.sem, tensor_qkv.at(b, "v"))
                dve.tensor_copy(vt, bank[3][:, :].rearrange("p (m d) -> p m d", m=2)).then_inc(vector_qkv.done("v"), 1)
                dve.wait_ge(scalar_qkv.sem, scalar_qkv.at(b, "norm"))
                dve.tensor_scalar(qk2, qk2, 1e-12, None, ALU.max).then_inc(vector_qkv.done("floor"), 1)
                dve.wait_ge(vector_qkv.sem, vector_qkv.at(b, "floor"))
                dve.reciprocal(qk2, qk2).then_inc(vector_qkv.done("recip"), 1)
                dve.wait_ge(vector_qkv.sem, vector_qkv.at(b, "recip"))
                for o in range(2):
                    ins = dve.scalar_tensor_tensor(qk[:, o, :], qk[:, o, :], tempc[:, o:o + 1], qk2[:, o, :],
                                                   op0=ALU.mult, op1=ALU.mult)
                ins.then_inc(vector_qkv.done("qn"), 1)
                dve.tensor_tensor(qk[:, 2:4, :], qk[:, 2:4, :], qk2[:, 2:4, :], op=ALU.mult).then_inc(vector_qkv.done("kn"), 1)

            def head1(n):
                dve.wait_ge(tensor_head.sem, tensor_head.at(n, "scores"))
                dve.tensor_reduce(hc[:, 0:2], bank[6][:, :].rearrange("p (l m) -> p l m", l=2), axis=AX.X,
                                  op=ALU.max, negate=True).then_inc(vector_head.done("max"), 1)
                dve.wait_ge(scalar_head.sem, scalar_head.at(n, "exp1"))
                dve.reciprocal(hc[:, 4:6], hc[:, 2:4]).then_inc(vector_head.done("rsum"), 1)
                dve.wait_ge(vector_head.sem, vector_head.at(n, "rsum"))
                for l in range(2):
                    dve.tensor_scalar(prob[:, l, :], prob[:, l, :], hc[:, 4 + l:5 + l], None,
                                      ALU.mult).then_inc(vector_head.done(f"scale{l}"), 1)
                dve.wait_ge(tensor_head.sem, tensor_head.at(n, "transpose"))
                if begun(n - 1):
                    dve.wait_ge(tensor_head.sem, tensor_head.at(n - 1, "out"))
                dve.tensor_copy(probT, bank[7][:, :].rearrange("p (m l) -> p m l", m=2)).then_inc(vector_head.done("probT"), 1)

            def finish1(b):
                dve.wait_ge(tensor_head.sem, tensor_head.at(b * TPB + TPB - 1, "out"))
                dst = oall[:, :, b, :] if isinstance(b, int) else oall[:, :, bass.ds(b, 1), :].squeeze(2)
                dve.tensor_copy(dst, bank[1][:, :].rearrange("p (o l) -> p o l", o=2)).then_inc(vector_image_end.done("o"), 1)
                dve.tensor_copy(oT, bank[2][:, :].rearrange("p (l d) -> p l d", l=2)).then_inc(vector_image_end.done("oT"), 1)
                dve.wait_ge(tensor_image_end.sem, tensor_image_end.at(b, "ko"))
                dve.tensor_copy(ko, bank[4][:, :].rearrange("p (l d) -> p l d", l=2)).then_inc(vector_image_end.done("ko"), 1)
                dve.wait_ge(tensor_image_end.sem, tensor_image_end.at(b, "cov"))
                dve.wait_ge(vector_cov_zero.sem, vector_cov_zero.at(0, "zero"))
                if begun(b - 1):
                    dve.wait_ge(vector_image_end.sem, vector_image_end.at(b - 1, "cov"))
                dve.tensor_tensor(cov, cov, bank[5][:, :].rearrange("p (o d) -> p o d", o=2),
                                  op=ALU.add).then_inc(vector_image_end.done("cov"), 1)

            for s in range(TPB):
                pool1(0, s)
            image1(0)

            def image_step(b):
                for s in range(TPB):
                    pool1(b, s)
                    head1((b - 1) * TPB + s)
                finish1(b - 1)
                image1(b)

            image_step(1)
            with dve.Fori(2, B) as b:
                image_step(b)
            for s in range(TPB):
                head1((B - 1) * TPB + s)
            finish1(B - 1)

            dve.wait_ge(vector_image_end.sem, vector_image_end.at(B - 1, "cov"))
            dve.wait_ge(tensor_image_end.sem, tensor_image_end.at(B - 1, "cov"))
            dve.memset(ones, 1.0).then_inc(vector_bn.done("ones"), 1)
            for o in range(2):
                dve.tensor_reduce(omean[:, o:o + 1], oall[:, o, :, :].rearrange("p b l -> p (b l)"), axis=AX.X,
                                  op=ALU.add).then_inc(vector_bn.done(f"osum{o}"), 1)
            dve.wait_ge(vector_bn.sem, vector_bn.at(0, "osum1"))
            dve.tensor_scalar(omean, omean, 1.0 / (B * LOW), None, ALU.mult).then_inc(vector_bn.done("omean"), 1)
            dve.wait_ge(tensor_bn.sem, tensor_bn.at(0, "z"))
            for k in range(4):
                o, c = divmod(k, 2)
                s = slice(c * 512, c * 512 + 512)
                dve.tensor_tensor(zw[:, o, s], bank[k][:, :], wp[:, o, s], op=ALU.mult).then_inc(vector_bn.done(f"zw{k}"), 1)
            dve.wait_ge(vector_bn.sem, vector_bn.at(0, "omean"))
            for o in range(2):
                dve.tensor_scalar(wm[:, o, :], wp[:, o, :], omean[:, o:o + 1], None,
                                  ALU.mult).then_inc(vector_bn.done(f"wm{o}"), 1)
            dve.wait_ge(tensor_bn.sem, tensor_bn.at(0, "sq"))
            for c in range(2):
                dve.tensor_copy(bmean[:, c * 512:c * 512 + 512], bank[4 + c][:, :]).then_inc(vector_bn.done(f"mean{c}"), 1)
            for c in range(2):
                dve.tensor_scalar(bvar[:, c * 512:c * 512 + 512], bank[6 + c][:, :], 1.0 / (B * PIX), None,
                                  ALU.mult).then_inc(vector_bn.done(f"e{c}"), 1)
            dve.wait_ge(vector_bn.sem, vector_bn.at(0, "e1"))
            dve.tensor_tensor(ylow, bmean, bmean, op=ALU.mult).then_inc(vector_bn.done("msq"), 1)
            dve.wait_ge(vector_bn.sem, vector_bn.at(0, "msq"))
            dve.tensor_tensor(bvar, bvar, ylow, op=ALU.subtract).then_inc(vector_bn.done("var"), 1)
            dve.wait_ge(vector_bn.sem, vector_bn.at(0, "var"))
            dve.tensor_scalar(bvar, bvar, EPS, None, ALU.add).then_inc(vector_bn.done("eps"), 1)
            dve.wait_ge(scalar_bn.sem, scalar_bn.at(0, "std"))
            dve.reciprocal(bvar, bvar).then_inc(vector_bn.done("rstd"), 1)
            dve.wait_ge(vector_bn.sem, vector_bn.at(0, "rstd"))
            dve.wait_ge(bnl, 16 * (2))
            dve.tensor_tensor(bgam, bgam, bvar, op=ALU.mult).then_inc(vector_bn.done("scale"), 1)
            dve.wait_ge(vector_bn.sem, vector_bn.at(0, "scale"))
            dve.tensor_tensor(bmean, bmean, bgam, op=ALU.mult).then_inc(vector_bn.done("ms"), 1)
            dve.wait_ge(vector_bn.sem, vector_bn.at(0, "ms"))
            dve.tensor_tensor(bbet, bbet, bmean, op=ALU.subtract).then_inc(vector_bn.done("shift"), 1)
            dve.wait_ge(vector_bn.sem, vector_bn.at(0, "shift"))

            def low(b):
                if begun(b - 1):
                    dve.wait_ge(tensor_low.sem, tensor_low.at(b - 1, "y1"))
                src = oall[:, :, b, :] if isinstance(b, int) else oall[:, :, bass.ds(b, 1), :].squeeze(2)
                dve.tensor_copy(ob, src).then_inc(vector_low.done("ob"), 1)
                for k in range(2):
                    dve.wait_ge(tensor_low.sem, tensor_low.at(b, f"y{k}"))
                    if k == 0:
                        if begun(b - 1):
                            dve.wait_ge(vector_low.sem, vector_low.at(b - 1, "lo1"))
                    else:
                        dve.wait_ge(vector_low.sem, vector_low.at(b, "lo0"))
                    for c in range(2):
                        s = slice(c * 512, c * 512 + 512)
                        dve.tensor_tensor(ylow[:, s], bank[2 * k + c][:, :], bgam[:, s],
                                          op=ALU.mult).then_inc(vector_low.done(f"mul{c}{k}"), 1)
                    dve.wait_ge(vector_low.sem, vector_low.at(b, f"mul1{k}"))
                    dve.tensor_tensor(ylow, ylow, bbet, op=ALU.add).then_inc(vector_low.done(f"add{k}"), 1)
                    dve.wait_ge(vector_low.sem, vector_low.at(b, f"add{k}"))
                    if begun(b - 1):
                        dve.wait_ge(lows[k], 16 * (6 * b))
                    dve.tensor_copy(part[k][0], ylow).then_inc(vector_low.done(f"hi{k}"), 1)
                    dve.wait_ge(vector_low.sem, vector_low.at(b, f"hi{k}"))
                    dve.tensor_tensor(ylow, ylow, part[k][0], op=ALU.subtract).then_inc(vector_low.done(f"r1{k}"), 1)
                    dve.wait_ge(vector_low.sem, vector_low.at(b, f"r1{k}"))
                    dve.tensor_copy(part[k][1], ylow).then_inc(vector_low.done(f"mid{k}"), 1)
                    dve.wait_ge(vector_low.sem, vector_low.at(b, f"mid{k}"))
                    dve.tensor_tensor(part[k][2], ylow, part[k][1], op=ALU.subtract).then_inc(vector_low.done(f"lo{k}"), 1)

            low(0)
            with dve.Fori(1, B) as b:
                low(b)

            dve.wait_ge(lows[0], 16 * (6 * B))
            dve.wait_ge(lows[1], 16 * (6 * B))
            dve.wait_ge(vector_low.sem, vector_low.at(B - 1, "lo1"))
            dve.memset(EDGE, 0.0).then_inc(vector_pads.done("edge"), 1)
            dve.memset(ALG, 0.0).then_inc(vector_pads.done("alpha"), 1)

            def add_low(i, u, n):
                for q in range(8):
                    if q % 2 == 0:
                        dve.wait_ge(XL[u][q // 2], 16 * (n + 1))
                    dve.wait_ge(tensor_front.sem, tensor_front.at(i, f"up{q}"))
                    s = slice(q * 512, q * 512 + 512)
                    dve.tensor_tensor(X[u][:, s], X[u][:, s], bank[q % 2][:, :], op=ALU.add).then_inc(vector_front.done(f"add{q}"), 1)

            def sums(i, u):
                dve.wait_ge(vector_front.sem, vector_front.at(i, "add7"))
                dve.tensor_reduce(EO.rearrange("p (h e) -> p h e", e=2), X[u].rearrange("p (h w e) -> p h e w", h=64, e=2),
                                  axis=AX.X, op=ALU.add).then_inc(vector_front.done("pairs"), 1)
                dve.wait_ge(vector_front.sem, vector_front.at(i, "pairs"))
                dve.tensor_tensor(RC[:, 0:64], EO[:, 0:P:2], EO[:, 1:P:2], op=ALU.add).then_inc(vector_front.done("rows"), 1)
                if begun(i - 2):
                    dve.wait_ge(tensor_spectrum.sem, tensor_spectrum.at(i - 2, "nyqt"))
                dve.tensor_tensor(ALT[u], EO[:, 0:P:2], EO[:, 1:P:2], op=ALU.subtract).then_inc(vector_front.done("alt"), 1)
                dve.wait_ge(vector_front.sem, vector_front.at(i, "rows"))
                if begun(i - 2):
                    dve.wait_ge(scalar_back.sem, scalar_back.at(i - 2, "mean3"))
                dve.tensor_reduce(PAR[u][:, 0:1], RC[:, 0:64], axis=AX.X, op=ALU.add).then_inc(vector_front.done("total"), 1)

            def variance(i, u):
                par = PAR[u]
                dve.wait_ge(tensor_front.sem, tensor_front.at(i, "stats"))
                n = 1.0 / (GC * PIX)
                dve.tensor_scalar(par[:, 2:3], bank[7][:, 0:1], n, None, ALU.mult).then_inc(vector_front.done("mean"), 1)
                dve.wait_ge(vector_front.sem, vector_front.at(i, "mean"))
                dve.tensor_scalar(par[:, 3:4], par[:, 2:3], par[:, 2:3], -EPS, ALU.mult, ALU.add).then_inc(vector_front.done("msq"), 1)
                dve.wait_ge(vector_front.sem, vector_front.at(i, "msq"))
                dve.scalar_tensor_tensor(par[:, 4:5], bank[7][:, 1:2], n, par[:, 3:4], op0=ALU.mult,
                                         op1=ALU.subtract).then_inc(vector_front.done("var"), 1)

            def normalise(i, u):
                par = PAR[u]
                dve.wait_ge(pool_front.sem, pool_front.at(i, "rstd"))
                dve.scalar_tensor_tensor(par[:, 7:8], par[:, 2:3], -1.0, par[:, 6:7], op0=ALU.mult,
                                         op1=ALU.mult).then_inc(vector_front.done("shift"), 1)
                dve.tensor_tensor(par[:, 5:6], par[:, 4:5], par[:, 6:7], op=ALU.mult).then_inc(vector_front.done("std"), 1)
                dve.wait_ge(vector_front.sem, vector_front.at(i, "std"))
                dve.tensor_scalar(par[:, 9:10], par[:, 5:6], 2.0, 1.0, ALU.mult, ALU.add).then_inc(vector_front.done("offset"), 1)
                dve.tensor_scalar(par[:, 8:9], par[:, 6:7], 1.0 / 64, None, ALU.mult).then_inc(vector_front.done("r64"), 1)
                dve.wait_ge(vector_front.sem, vector_front.at(i, "r64"))
                dve.tensor_scalar(ALT[u], ALT[u], par[:, 6:7], 0.125, ALU.mult, ALU.mult).then_inc(vector_front.done("altn"), 1)
                dve.tensor_scalar(X[u], X[u], par[:, 6:7], par[:, 7:8], ALU.mult, ALU.add).then_inc(vector_front.done("gx"), 1)
                if begun(i - 2):
                    dve.wait_ge(tensor_gate.sem, tensor_gate.at(i - 2, "w1"))
                dve.tensor_scalar(CATS[u], RC, par[:, 8:9], par[:, 7:8], ALU.mult, ALU.add).then_inc(vector_front.done("cat"), 1)

            ggrid = GT.rearrange("p (h w) -> p h w", h=64)

            def filter_mean(i, u):
                cat = CATS[u]
                grid = X[u].rearrange("p (h w) -> p h w", h=64)
                dve.wait_ge(vector_front.sem, vector_front.at(i, "cat"))
                if begun(i - 1):
                    dve.wait_ge(scalar_gate.sem, scalar_gate.at(i - 1, "expcol"))
                dve.tensor_reduce(SM[:, 20:21], cat[:, 0:64], axis=AX.X, op=ALU.add).then_inc(vector_gate.done("tot"), 1)
                dve.tensor_copy(EDGE[:, 2::-2], cat[:, 0:64:63]).then_inc(vector_gate.done("edges0"), 1)
                dve.tensor_copy(EDGE[:, 5:2:-2], cat[:, 64:128:63]).then_inc(vector_gate.done("edges1"), 1)
                dve.wait_ge(vector_gate.sem, vector_gate.at(i, "edges1"))
                fq = FR[:, 0:9].rearrange("p (a b) -> p a b", a=3)
                dve.tensor_tensor(fq, EDGE[:, 0:3].unsqueeze(2).to_broadcast([P, 3, 3]),
                                  EDGE[:, 3:6].unsqueeze(1).to_broadcast([P, 3, 3]), op=ALU.add).then_inc(vector_gate.done("f0"), 1)
                dve.wait_ge(vector_gate.sem, vector_gate.at(i, "f0"))
                dve.tensor_scalar(FR[:, 0:9], FR[:, 0:9], -1.0, SM[:, 20:21], ALU.mult, ALU.add).then_inc(vector_gate.done("f1"), 1)
                dve.wait_ge(vector_gate.sem, vector_gate.at(i, "f1"))
                corner = fq[:, ::2, ::2]
                dve.scalar_tensor_tensor(corner, grid[:, ::-63, ::-63], 1.0 / 64, corner, op0=ALU.mult,
                                         op1=ALU.add).then_inc(vector_gate.done("corner"), 1)
                dve.wait_ge(vector_gate.sem, vector_gate.at(i, "corner"))
                dve.tensor_tensor(FR[:, 16:25], FR[:, 0:9], wdw[:, :], op=ALU.mult).then_inc(vector_gate.done("fw"), 1)
                dve.wait_ge(vector_gate.sem, vector_gate.at(i, "fw"))
                dve.tensor_reduce(SM[:, 7:8], FR[:, 16:25], axis=AX.X, op=ALU.add).then_inc(vector_gate.done("dw"), 1)
                dve.wait_ge(vector_gate.sem, vector_gate.at(i, "dw"))
                dve.tensor_scalar(SM[:, 8:9], SM[:, 7:8], 1.0 / 64, colw[:, BDW:BDW + 1], ALU.mult,
                                  ALU.add).then_inc(vector_gate.done("dwb"), 1)

            def logits(i):
                dve.wait_ge(tensor_gate.sem, tensor_gate.at(i, "pw"))
                dve.tensor_tensor(SM[:, 9:10], bank[7][:, 64:65], colw[:, BPW:BPW + 1], op=ALU.add).then_inc(vector_gate.done("x2m"), 1)
                dve.wait_ge(vector_gate.sem, vector_gate.at(i, "x2m"))
                dve.tensor_scalar(FRL, csel[:, :], SM[:, 9:10], None, ALU.mult).then_inc(vector_gate.done("lsel"), 1)

            def gate_columns(i, u):
                dve.wait_ge(scalar_gate.sem, scalar_gate.at(i, "sig"))
                dve.tensor_scalar(SHW[u], SHW[u], 0.5, 0.5, ALU.mult, ALU.add).then_inc(vector_gate.done("gates"), 1)
                dve.wait_ge(vector_gate.sem, vector_gate.at(i, "gates"))
                if begun(i - 1):
                    dve.wait_ge(tensor_back.sem, tensor_back.at(i - 1, "gsum"))
                grid = X[u].rearrange("p (h w) -> p h w", h=64)
                dve.tensor_tensor(ggrid, grid, SHW[u][:, 64:128].unsqueeze(1).to_broadcast([P, 64, 64]),
                                  op=ALU.mult).then_inc(vector_gate.done("t1"), 1)

            def gate_rows(i, u):
                dve.wait_ge(vector_gate.sem, vector_gate.at(i, "t1"))
                dve.scalar_tensor_tensor(ggrid, ggrid, 1.0, SHW[u][:, 0:64].unsqueeze(2).to_broadcast([P, 64, 64]),
                                         op0=ALU.mult, op1=ALU.mult, accum_out=SM[:, 0:1]).then_inc(vector_gate.done("gated"), 1)

            def gate_small(i):
                dve.wait_ge(vector_gate.sem, vector_gate.at(i, "gated"))
                dve.tensor_scalar(SM[:, 2:3], SM[:, 0:1], 1.0 / PIX, None, ALU.mult).then_inc(vector_gate.done("gmean"), 1)
                dve.wait_ge(vector_gate.sem, vector_gate.at(i, "gmean"))
                dve.tensor_scalar(SM[:, 3:4], SM[:, 2:3], SM[:, 2:3], -EPS, ALU.mult, ALU.add).then_inc(vector_gate.done("gmsq"), 1)
                dve.wait_ge(tensor_gate.sem, tensor_gate.at(i, "lrow"))
                dve.tensor_reduce(SM[:, 10:11], bank[7][:, 320:352], axis=AX.X, op=ALU.max,
                                  negate=True).then_inc(vector_gate.done("max"), 1)

            def weights(i):
                dve.wait_ge(vector_gate.sem, vector_gate.at(i, "gmsq"))
                dve.wait_ge(scalar_gate.sem, scalar_gate.at(i, "sq"))
                dve.scalar_tensor_tensor(SM[:, 4:5], SM[:, 1:2], 1.0 / PIX, SM[:, 3:4], op0=ALU.mult,
                                         op1=ALU.subtract).then_inc(vector_gate.done("gvar"), 1)
                dve.wait_ge(scalar_gate.sem, scalar_gate.at(i, "expcol"))
                dve.reciprocal(SM[:, 13:14], SM[:, 11:12]).then_inc(vector_gate.done("rsum"), 1)
                dve.wait_ge(vector_gate.sem, vector_gate.at(i, "rsum"))
                dve.wait_ge(pool_gate.sem, pool_gate.at(i, "rstd"))
                dve.tensor_tensor(SM[:, 14:15], SM[:, 12:13], SM[:, 13:14], op=ALU.mult).then_inc(vector_gate.done("s2"), 1)
                dve.tensor_tensor(SM[:, 15:16], colw[:, GAMMA:GAMMA + 1], SM[:, 6:7], op=ALU.mult).then_inc(vector_gate.done("sg"), 1)
                dve.wait_ge(vector_gate.sem, vector_gate.at(i, "sg"))
                dve.tensor_tensor(SM[:, 16:17], SM[:, 14:15], SM[:, 15:16], op=ALU.mult).then_inc(vector_gate.done("alpha"), 1)
                dve.wait_ge(vector_gate.sem, vector_gate.at(i, "alpha"))
                dve.tensor_scalar(ALG[:, 0:NG], gsel[:, :], SM[:, 16:17], None, ALU.mult).then_inc(vector_gate.done("alg"), 1)
                dve.tensor_tensor(SM[:, 17:18], SM[:, 16:17], SM[:, 2:3], op=ALU.mult).then_inc(vector_gate.done("am"), 1)
                dve.wait_ge(vector_gate.sem, vector_gate.at(i, "am"))
                dve.scalar_tensor_tensor(SM[:, 18:19], colw[:, BETA:BETA + 1], SM[:, 14:15], SM[:, 17:18],
                                         op0=ALU.mult, op1=ALU.subtract).then_inc(vector_gate.done("kc"), 1)

            def constant(i):
                dve.wait_ge(tensor_gate.sem, tensor_gate.at(i, "const"))
                dve.tensor_tensor(SM[:, 19:20], bank[7][:, 66:67], wts0[:, :], op=ALU.add).then_inc(vector_gate.done("kcon"), 1)

            def nyquist(i):
                dve.wait_ge(scalar_spectrum.sem, scalar_spectrum.at(i, "nyqsq"))
                dve.tensor_tensor(SQN[:, 1:32], SQN[:, 1:32], SQN[:, 33:64], op=ALU.add).then_inc(vector_spectrum.done("nyq"), 1)

            def squares(i, k):
                sign, half_, octet = k // 4, (k // 2) % 2, k % 2
                dve.wait_ge(scalar_spectrum.sem, scalar_spectrum.at(i, f"w{k}"))
                if k == 0 and begun(i - 1):
                    dve.wait_ge(tensor_spectrum.sem, tensor_spectrum.at(i - 1, "chan"))
                c = sign * 1024 + octet * 512
                dve.tensor_tensor(MAG[64 * half_:64 * half_ + 64, c:c + 512], SQ[k % 2][0:64, :], SQ[k % 2][64:128, :],
                                  op=ALU.add).then_inc(vector_spectrum.done(f"w{k}"), 1)
                dve.wait_ge(vector_spectrum.sem, vector_spectrum.at(i, f"w{k}"))

            def frequency_map(i):
                dve.wait_ge(tensor_spectrum.sem, tensor_spectrum.at(i, "chan"))
                if begun(i - 1):
                    dve.wait_ge(tensor_back.sem, tensor_back.at(i - 1, "fmap"))
                fm = bank[6][0:64, 128:256].rearrange("p (s j k) -> p s j k", s=2, j=2)
                dst = FM.rearrange("p (j f) -> p j f", j=2)
                dve.tensor_copy(dst[:, :, 0:32], fm[:, 0]).then_inc(vector_spectrum.done("fm0"), 1)
                dve.tensor_copy(dst[:, :, 32:64], fm[:, 1, :, ::-1]).then_inc(vector_spectrum.done("fm1"), 1)
                dve.wait_ge(tensor_back.sem, tensor_back.at(i, "fmap"))
                src = bank[6][:, 0:128]
                dve.tensor_copy(MAP[:, 1, 0, :], src).then_inc(vector_back.done("fhi"), 1)
                dve.wait_ge(vector_back.sem, vector_back.at(i, "fhi"))
                dve.tensor_tensor(REST[1], src, MAP[:, 1, 0, :], op=ALU.subtract).then_inc(vector_back.done("frest"), 1)
                dve.wait_ge(vector_back.sem, vector_back.at(i, "frest"))
                dve.tensor_copy(MAP[:, 1, 1, :], REST[1]).then_inc(vector_back.done("fmid"), 1)
                dve.wait_ge(vector_back.sem, vector_back.at(i, "fmid"))
                dve.tensor_tensor(MAP[:, 1, 2, :], REST[1], MAP[:, 1, 1, :], op=ALU.subtract).then_inc(vector_back.done("fmap"), 1)

            def group_sum(i):
                dve.wait_ge(tensor_back.sem, tensor_back.at(i, "gsum"))
                if begun(i - 1):
                    dve.wait_ge(tensor_back.sem, tensor_back.at(i - 1, "wmap"))
                dve.tensor_copy(TG, bank[4][:, 0:128]).then_inc(vector_back.done("gsum"), 1)

            def weight_map(i):
                dve.wait_ge(tensor_back.sem, tensor_back.at(i, "wmap"))
                dve.wait_ge(vector_gate.sem, vector_gate.at(i, "kcon"))
                if begun(i - 1):
                    dve.wait_ge(map_stored, 16 * (2 * PARTS * i))
                src, k = bank[5][:, 0:128], SM[:, 19:20]
                dve.tensor_scalar(MAP[:, 0, 0, :], src, k, None, ALU.add).then_inc(vector_back.done("whi"), 1)
                dve.wait_ge(vector_back.sem, vector_back.at(i, "whi"))
                dve.scalar_tensor_tensor(REST[0], src, k, MAP[:, 0, 0, :], op0=ALU.add,
                                         op1=ALU.subtract).then_inc(vector_back.done("wrest"), 1)
                dve.wait_ge(vector_back.sem, vector_back.at(i, "wrest"))
                dve.tensor_copy(MAP[:, 0, 1, :], REST[0]).then_inc(vector_back.done("wmid"), 1)
                dve.wait_ge(vector_back.sem, vector_back.at(i, "wmid"))
                dve.tensor_tensor(MAP[:, 0, 2, :], REST[0], MAP[:, 0, 1, :], op=ALU.subtract).then_inc(vector_back.done("wmap"), 1)

            def multiply(i, u):
                for q in range(4):
                    dve.wait_ge(scalar_back.sem, scalar_back.at(i, f"sig{2 * q + 1}"))
                    dve.scalar_tensor_tensor(SIG[q], SIG[q], PAR[u][:, 9:10], X[u][:, q * 1024:(q + 1) * 1024],
                                             op0=ALU.add, op1=ALU.mult).then_inc(vector_back.done(f"mul{q}"), 1)

            def period(i, u, n, new=True):
                constant(i)
                if new:
                    add_low(i + 1, 1 - u, n)
                    sums(i + 1, 1 - u)
                group_sum(i)
                if new:
                    variance(i + 1, 1 - u)
                weight_map(i)
                if new:
                    normalise(i + 1, 1 - u)
                nyquist(i)
                squares(i, 0)
                squares(i, 1)
                if new:
                    filter_mean(i + 1, 1 - u)
                squares(i, 2)
                if new:
                    gate_columns(i + 1, 1 - u)
                squares(i, 3)
                if new:
                    logits(i + 1)
                squares(i, 4)
                if new:
                    gate_rows(i + 1, 1 - u)
                squares(i, 5)
                squares(i, 6)
                squares(i, 7)
                if new:
                    gate_small(i + 1)
                frequency_map(i)
                if new:
                    weights(i + 1)
                multiply(i, u)

            add_low(0, 0, 0)
            sums(0, 0)
            variance(0, 0)
            normalise(0, 0)
            filter_mean(0, 0)
            gate_columns(0, 0)
            logits(0)
            gate_rows(0, 0)
            gate_small(0)
            weights(0)
            period(0, 0, 0)
            period(1, 1, 1)
            with dve.Fori(1, NT // 2 - 1) as pr:
                period(2 * pr, 0, pr)
                period(2 * pr + 1, 1, pr + 1)
            period(NT - 2, 0, NT // 2 - 1)
            period(NT - 1, 1, 0, new=False)

        @block.tensor
        def _(pe):
            mm = pe.matmul
            pe.wait_ge(cst, 16 * N_CONST)
            pe.wait_ge(upl, 16 * 1)
            pe.wait_ge(blocks, 16 * (3 * NG))
            pe.wait_ge(vector_setup.sem, vector_setup.at(0, "selw2"))
            mm(bank[0][0:ARG_ROWS, 128:256], argw_t[:, :], ident[:, :], start=True, stop=True).then_inc(tensor_setup.done("argw"), 1)
            pe.wait_ge(vector_setup.sem, vector_setup.at(0, "s1"))
            mm(bank[0][:, 0:1], wpbd[:, :], cw[:, 35:36], start=True, stop=True).then_inc(tensor_setup.done("p"), 1)
            pe.wait_ge(vector_setup.sem, vector_setup.at(0, "c1"))
            mm(bank[0][:, 1:2], gones[:, :], cw[:, 43:44], start=True, stop=True).then_inc(tensor_setup.done("const"), 1)
            pe.wait_ge(vector_setup.sem, vector_setup.at(0, "argw"))

            def image1(b):
                pe.wait_ge(vector_pool.sem, vector_pool.at(b * TPB + TPB - 1, "sum"))
                pe.wait_ge(scalar_squares.sem, scalar_squares.at(b * TPB + TPB - 1, "sq"))
                if begun(b - 1):
                    pe.wait_ge(vector_imagestats.sem, vector_imagestats.at(b - 1, "var0"))
                mm(bank[0][:, 0:16], gones[:, :], st, start=True, stop=True).then_inc(tensor_imagestats.done("stats"), 1)
                pe.wait_ge(vector_imagestats.sem, vector_imagestats.at(b, "xn7"))
                if begun(b - 1):
                    pe.wait_ge(vector_image_end.sem, vector_image_end.at(b - 1, "oT"))
                for o in range(4):
                    for t in range(TPB):
                        ins = mm(bank[1 + o // 2][:, (o % 2) * LOW:(o % 2 + 1) * LOW], wq[:, t, o * P:(o + 1) * P],
                                 xn[:, t, :], start=(t == 0), stop=(t == TPB - 1))
                ins.then_inc(tensor_qkv.done("qk"), 1)
                for m in range(2):
                    for t in range(TPB):
                        ins = mm(bank[3][:, m * TD:(m + 1) * TD], xn[:, t, m * P:(m + 1) * P],
                                 wq[:, t, 2 * TD:3 * TD], start=(t == 0), stop=(t == TPB - 1))
                ins.then_inc(tensor_qkv.done("v"), 1)
                pe.wait_ge(scalar_qkv.sem, scalar_qkv.at(b, "sq"))
                if begun(b - 1):
                    pe.wait_ge(vector_image_end.sem, vector_image_end.at(b - 1, "cov"))
                mm(bank[4][:, :], gones[:, :], qk2[:, 0:2, :], start=True, stop=True)
                mm(bank[5][:, :], gones[:, :], qk2[:, 2:4, :], start=True, stop=True).then_inc(tensor_qkv.done("norms"), 1)

            def head1(b, h):
                n = b * TPB + h
                lo, o = 32 * (h % 4), h // 4
                pe.wait_ge(vector_qkv.sem, vector_qkv.at(b, "kn"))
                if begun(n - 1):
                    pe.wait_ge(scalar_head.sem, scalar_head.at(n - 1, "exp1"))
                for l in range(2):
                    ins = mm(bank[6][:, l * LOW:(l + 1) * LOW], qk[lo:lo + 32, o, l * P:(l + 1) * P],
                             qk[lo:lo + 32, 2 + o, :], start=True, stop=True)
                ins.then_inc(tensor_head.done("scores"), 1)
                pe.wait_ge(vector_head.sem, vector_head.at(n, "scale1"))
                if begun(n - 1):
                    pe.wait_ge(vector_head.sem, vector_head.at(n - 1, "probT"))
                for m in range(2):
                    for l in range(2):
                        ins = pe.transpose(bank[7][:, m * LOW + l * P:m * LOW + (l + 1) * P],
                                           prob[:, l, m * P:(m + 1) * P], ident[:, :])
                ins.then_inc(tensor_head.done("transpose"), 1)
                pe.wait_ge(vector_head.sem, vector_head.at(n, "probT"))
                d = slice(DPH * h, DPH * h + DPH)
                for m in range(2):
                    mm(bank[1][lo:lo + 32, o * LOW:(o + 1) * LOW], vt[:, m, d], probT[:, m, :],
                       start=(m == 0), stop=(m == 1))
                for l in range(2):
                    for m in range(2):
                        ins = mm(bank[2][:, l * TD + DPH * h:l * TD + DPH * h + DPH], probT[:, m, l * P:(l + 1) * P],
                                 vt[:, m, d], start=(m == 0), stop=(m == 1))
                ins.then_inc(tensor_head.done("out"), 1)

            def finish1(b):
                pe.wait_ge(vector_image_end.sem, vector_image_end.at(b, "oT"))
                for l in range(2):
                    for k in range(2):
                        ins = mm(bank[4][:, l * TD:(l + 1) * TD], gram[:, k, l * P:(l + 1) * P], oT[:, k, :],
                                 start=(k == 0), stop=(k == 1))
                ins.then_inc(tensor_image_end.done("ko"), 1)
                pe.wait_ge(vector_image_end.sem, vector_image_end.at(b, "ko"))
                for o in range(2):
                    for k in range(2):
                        ins = mm(bank[5][:, o * TD:(o + 1) * TD], oT[:, k, o * P:(o + 1) * P], ko[:, k, :],
                                 start=(k == 0), stop=(k == 1))
                ins.then_inc(tensor_image_end.done("cov"), 1)

            image1(0)

            def image_step(b):
                for h in range(HEADS):
                    head1(b - 1, h)
                finish1(b - 1)
                image1(b)

            image_step(1)
            with pe.Fori(2, B) as b:
                image_step(b)
            for h in range(HEADS):
                head1(B - 1, h)
            finish1(B - 1)

            pe.wait_ge(vector_image_end.sem, vector_image_end.at(B - 1, "cov"))
            for o in range(2):
                for c in range(2):
                    for k in range(2):
                        ins = mm(bank[2 * o + c][:, :], cov[:, k, o * P:(o + 1) * P], wp[:, k, c * 512:(c + 1) * 512],
                                 start=(k == 0), stop=(k == 1))
            ins.then_inc(tensor_bn.done("z"), 1)
            pe.wait_ge(vector_bn.sem, vector_bn.at(0, "wm1"))
            for c in range(2):
                for o in range(2):
                    ins = mm(bank[4 + c][:, :], ones, wm[:, o, c * 512:(c + 1) * 512], start=(o == 0), stop=(o == 1))
            ins.then_inc(tensor_bn.done("mean"), 1)
            for c in range(2):
                for o in range(2):
                    ins = mm(bank[6 + c][:, :], ones, zw[:, o, c * 512:(c + 1) * 512], start=(o == 0), stop=(o == 1))
            ins.then_inc(tensor_bn.done("sq"), 1)

            def low(b):
                pe.wait_ge(vector_low.sem, vector_low.at(b, "ob"))
                for k in range(2):
                    if begun(b - 1):
                        pe.wait_ge(vector_low.sem, vector_low.at(b - 1, f"mul1{k}"))
                    for c in range(2):
                        for o in range(2):
                            ins = mm(bank[2 * k + c][:, :], ob[:, o, k * P:(k + 1) * P], wp[:, o, c * 512:(c + 1) * 512],
                                     start=(o == 0), stop=(o == 1))
                    ins.then_inc(tensor_low.done(f"y{k}"), 1)

            low(0)
            with pe.Fori(1, B) as b:
                low(b)
            pe.wait_ge(vector_low.sem, vector_low.at(B - 1, "mul11"))

            def up(i, u, q):
                if q < 2:
                    if begun(i - 2):
                        pe.wait_ge(scalar_back.sem, scalar_back.at(i - 2, f"sig{4 + q}"))
                    if begun(i - 1):
                        pe.wait_ge(vector_front.sem, vector_front.at(i - 1, f"add{6 + q}"))
                else:
                    pe.wait_ge(vector_front.sem, vector_front.at(i, f"add{q - 2}"))
                mm(bank[q % 2][:, 0:128], YS[u][:, 2 * q, :], upmat[:, 128:256], start=True, stop=True)
                mm(bank[q % 2][:, 128:384], YS[u][:, 2 * q + 1, :], upmat[:, :], start=True, stop=True)
                mm(bank[q % 2][:, 384:512], YS[u][:, 2 * q + 2, :], upmat[:, 0:128], start=True,
                   stop=True).then_inc(tensor_front.done(f"up{q}"), 1)

            def stats(i, u):
                pe.wait_ge(vector_front.sem, vector_front.at(i, "total"))
                pe.wait_ge(scalar_front.sem, scalar_front.at(i, "sq"))
                if begun(i - 1):
                    pe.wait_ge(vector_gate.sem, vector_gate.at(i - 1, "kcon"))
                mm(bank[7][:, 0:2], gones[:, :], PAR[u][:, 0:2], start=True, stop=True).then_inc(tensor_front.done("stats"), 1)

            def gate(i, u):
                pe.wait_ge(vector_front.sem, vector_front.at(i, "cat"))
                mm(bank[7][:, 128:256], w1bd[:, :], CATS[u], start=True, stop=True).then_inc(tensor_gate.done("w1"), 1)

            def taps2(i, u, fills):
                pe.wait_ge(vector_front.sem, vector_front.at(i, "gx"))
                for k in fills:
                    c0, n = TAP_FILLS[k]
                    if k == 2:
                        pe.wait_ge(scalar_taps.sem, scalar_taps.at(i, "t0"))
                    else:
                        if begun(i - 1):
                            pe.wait_ge(vector_back.sem, vector_back.at(i - 1, ("gsum", "wmap")[k]))
                    for c in range(n):
                        ins = mm(bank[4 + k % 2][:, 36 * c:36 * c + P], X[u][:, (c0 + c) * P:(c0 + c + 1) * P],
                                 taps[:, :], start=True, stop=True)
                    ins.then_inc(tensor_taps.done(f"t{k}"), 1)

            def pointwise(i):
                pe.wait_ge(vector_gate.sem, vector_gate.at(i, "dwb"))
                pe.wait_ge(scalar_gate.sem, scalar_gate.at(i, "sig"))
                mm(bank[7][:, 64:65], wptbd[:, :], SM[:, 8:9], start=True, stop=True).then_inc(tensor_gate.done("pw"), 1)

            def logits(i):
                pe.wait_ge(vector_gate.sem, vector_gate.at(i, "lsel"))
                mm(bank[7][:, 320:352], gones[:, :], FRL, start=True, stop=True).then_inc(tensor_gate.done("lrow"), 1)

            def constant(i):
                pe.wait_ge(vector_gate.sem, vector_gate.at(i, "kc"))
                mm(bank[7][:, 66:67], gcols[:, :], SM[:, 18:19], start=True, stop=True).then_inc(tensor_gate.done("const"), 1)

            def row_transform(i, k):
                if k == 0:
                    pe.wait_ge(g2l, 16 * (2 * (i + 1)))
                if k >= 2:
                    pe.wait_ge(scalar_spectrum.sem, scalar_spectrum.at(i, f"h{k - 2}"))
                elif begun(i - 1):
                    pe.wait_ge(scalar_back.sem, scalar_back.at(i - 1, f"sig{6 + k}"))
                for c in range(4):
                    ins = mm(bank[2 + k % 2][:, c * P:(c + 1) * P], G2[:, (4 * k + c) * P:(4 * k + c + 1) * P],
                             dft_h[:, :], start=True, stop=True)
                ins.then_inc(tensor_spectrum.done(f"h{k}"), 1)

            def nyquist_turn(i, u):
                pe.wait_ge(vector_front.sem, vector_front.at(i, "altn"))
                if begun(i - 1):
                    pe.wait_ge(vector_back.sem, vector_back.at(i - 1, "fmap"))
                mm(bank[6][0:64, 384:512], ALT[u], ident[:, :], start=True, stop=True).then_inc(tensor_spectrum.done("nyqt"), 1)

            def nyquist(i):
                pe.wait_ge(scalar_spectrum.sem, scalar_spectrum.at(i, "nyqt"))
                mm(bank[6][:, 384:448], ALTT, dft_h[0:64, 0:64], start=True, stop=True).then_inc(tensor_spectrum.done("nyq"), 1)

            def column_transform(i, k):
                ah = AH.rearrange("p (c k) -> p c k", k=64)
                sign, half_, octet = k // 4, (k // 2) % 2, k % 2
                if k < 2:
                    pe.wait_ge(scalar_spectrum.sem, scalar_spectrum.at(i, f"h{6 + k}"))
                else:
                    pe.wait_ge(scalar_spectrum.sem, scalar_spectrum.at(i, f"w{k - 2}"))
                c0 = 2 * (half_ * 16 + octet * 8)
                dst = bank[2 + k % 2][:, :].rearrange("p (c k) -> p c k", k=32)
                mm(dst, dft_w[:, 0:P], ah[:, c0:c0 + 16, sign:sign + 32], start=True, stop=False)
                mm(dst[:, :, 1 - sign:32 - sign], dft_w[:, (1 + sign) * P:(2 + sign) * P], ah[:, c0:c0 + 16, 33:64],
                   start=False, stop=True).then_inc(tensor_spectrum.done(f"w{k}"), 1)

            def channel_sum(i):
                pe.wait_ge(scalar_spectrum.sem, scalar_spectrum.at(i, "root1"))
                pe.wait_ge(scalar_spectrum.sem, scalar_spectrum.at(i, "nyqsq"))
                mag = MAG.rearrange("p (s c k) -> p s c k", s=2, k=64)
                dst = bank[6][0:64, 128:256].rearrange("p (s k) -> p s k", s=2)
                for c in range(16):
                    ins = mm(dst, spread[:, 64 - 2 * c:P - 2 * c], mag[:, :, c, :], start=(c == 0), stop=(c == 15))
                ins.then_inc(tensor_spectrum.done("chan"), 1)

            def group_sum(i):
                pe.wait_ge(vector_gate.sem, vector_gate.at(i, "alg"))
                pe.wait_ge(scalar_taps.sem, scalar_taps.at(i, "t2"))
                for c in range(32):
                    ins = mm(bank[4][:, NG * c:NG * c + P], GT[:, c * P:(c + 1) * P], ALG, start=True, stop=True)
                ins.then_inc(tensor_back.done("gsum"), 1)

            def weight_map(i):
                pe.wait_ge(vector_back.sem, vector_back.at(i, "gsum"))
                for n, (tap, d) in enumerate(SHIFT_PLAN):
                    mm(bank[5][:, 0:128], TP[:, tap, 1 + d:33 + d, :], shifts[:, n * P:(n + 1) * P],
                       start=(n == 0), stop=False)
                mm(bank[5][:, 0:128], TG, ident[:, :], start=False, stop=True).then_inc(tensor_back.done("wmap"), 1)

            def frequency_map(i):
                pe.wait_ge(vector_spectrum.sem, vector_spectrum.at(i, "fm1"))
                pe.wait_ge(scalar_spectrum.sem, scalar_spectrum.at(i, "nyqroot"))
                for k in range(2):
                    dst = bank[6][:, 64 * k:64 + 64 * k]
                    mm(dst, resize[:, k * P:(k + 1) * P], NYM, start=True, stop=False)
                    for j in range(2):
                        ins = mm(dst, resize_half[:, (2 * j + k) * P:(2 * j + k + 1) * P], FM[:, 64 * j:64 * j + 64],
                                 start=False, stop=(j == 1))
                ins.then_inc(tensor_back.done("fmap"), 1)

            def arguments(i, new):
                pe.wait_ge(mapl, 16 * ((1 + PARTS) * (i + 1)))
                for q in range(8):
                    if q < 2:
                        pe.wait_ge(vector_front.sem, vector_front.at(i + 1 if new else i, f"add{6 + q}"))
                    elif q < 4:
                        pe.wait_ge(scalar_spectrum.sem, scalar_spectrum.at(i, f"w{4 + q}"))
                    else:
                        pe.wait_ge(scalar_back.sem, scalar_back.at(i, f"sig{q - 4}"))
                    mm(bank[q % 4][:, :], argw[:, :], ROWS[:, q * 512:(q + 1) * 512], start=True,
                       stop=True).then_inc(tensor_back.done(f"arg{q}"), 1)

            def period(i, u, n, new=True):
                constant(i)
                if new:
                    pe.wait_ge(YL[1 - u], 16 * (6 * (n + 1)))
                nyquist_turn(i, u)
                for k in range(8):
                    row_transform(i, k)
                    if new:
                        up(i + 1, 1 - u, k)
                group_sum(i)
                if new:
                    stats(i + 1, 1 - u)
                weight_map(i)
                nyquist(i)
                for k in range(8):
                    column_transform(i, k)
                    if new and k == 1:
                        gate(i + 1, 1 - u)
                    elif new and k == 3:
                        pointwise(i + 1)
                    elif new and k == 5:
                        logits(i + 1)
                if new:
                    taps2(i + 1, 1 - u, (0,))
                channel_sum(i)
                frequency_map(i)
                if new:
                    taps2(i + 1, 1 - u, (1, 2))
                arguments(i, new)

            pe.wait_ge(YL[0], 16 * 6)
            for k in range(8):
                up(0, 0, k)
            stats(0, 0)
            gate(0, 0)
            taps2(0, 0, (0, 1, 2))
            pointwise(0)
            logits(0)
            period(0, 0, 0)
            period(1, 1, 1)
            with pe.Fori(1, NT // 2 - 1) as pr:
                period(2 * pr, 0, pr)
                period(2 * pr + 1, 1, pr + 1)
            period(NT - 2, 0, NT // 2 - 1)
            period(NT - 1, 1, 0, new=False)


def laid_out(inputs):
    g = {k: np.ascontiguousarray(v) for k, v in inputs.items()}

    def col(v):
        return np.tile(v.reshape(GC, -1), (NG, 1))

    return {
        "x": g["x"],
        "w_qkv_t": g["L0_conv_w_qkv"].T,
        "w_proj_t": g["L0_conv_w_proj"].T,
        "temperature": np.repeat(g["L0_conv_temperature"].reshape(2, 4), DPH, axis=1).T,
        "bn_gamma": g["L0_conv_bn_gamma"], "bn_beta": g["L0_conv_bn_beta"],
        "w1_t": g["L1_conv_w1"].T, "w_pw": g["L1_conv_w_pw"], "w_pw_t": g["L1_conv_w_pw"].T,
        "b1": col(g["L1_conv_b1"]), "gn_gamma": col(g["L1_conv_gn_gamma"]), "gn_beta": col(g["L1_conv_gn_beta"]),
        "w_dw": col(g["L1_conv_w_dw"]), "b_dw": col(g["L1_conv_b_dw"]), "b_pw": col(g["L1_conv_b_pw"]),
        "w_fp": col(g["L1_conv_w_fp"]), "b_fp": col(g["L1_conv_b_fp"]),
        "beta_row": np.tile(g["L1_conv_gn_beta"].reshape(1, GC), (P, 1)),
    }


def kernel(**inputs):
    import concourse.bacc as bacc
    from concourse.bass_utils import run_bass_kernel_spmd

    nc = bacc.Bacc("TRN2", target_bir_lowering=False, num_devices=1)
    arrays, args = {}, {}
    for name, v in {**laid_out(inputs), **constants()}.items():
        v = np.ascontiguousarray(v)
        arrays[f"in_{name}"] = v
        args[name] = nc.dram_tensor(f"in_{name}", v.shape, mybir.dt.from_np(v.dtype), kind="ExternalInput").ap()
    out = nc.dram_tensor("out", (B, CH, H, W), F32, kind="ExternalOutput").ap()
    build(nc, args, out)
    r = run_bass_kernel_spmd(nc, [arrays], core_ids=[0])
    return r.results[0]["out"]
```

```python
import math
from contextlib import ExitStack

import numpy as np

import concourse.bass as bass
from concourse import mybir

F32 = mybir.dt.float32
BF16 = mybir.dt.bfloat16
ALU = mybir.AluOpType
ACT = mybir.ActivationFunctionType
AX = mybir.AxisListType

B, CH, H, W = 16, 1024, 64, 64
PIX = H * W
P = 128
TPB = CH // P
NT = B * TPB
GC = 32
NG = P // GC
HEADS, DPH = 8, 32
TD = HEADS * DPH
PH = PW = 16
LOW = PH * PW
EPS = 1e-5
KW = W // 2 + 1
HH = H // 2
PARTS = 3
ARG_ROWS = PARTS * NG * (1 + PARTS)


def constants():
    c = {}
    k = np.arange(64)
    ang = 2 * math.pi * np.outer(k, k) / 64
    cos, sin = np.cos(ang) / 8, np.sin(ang) / 8
    fh = np.concatenate([cos[:, :33], sin[:, 1:32]], axis=1)
    c["dft_h"] = np.kron(np.eye(2), fh)
    wc = np.zeros((2, 64, 2, 2, 32))
    ws = np.zeros((2, 64, 2, 2, 32))
    for j in range(2):
        wc[j, :, 0, j], wc[j, :, 1, j] = cos[:, :32], sin[:, :32]
        ws[j, :, 0, j], ws[j, :, 1, j] = -sin[:, :32], cos[:, :32]
    c["dft_w"] = np.stack([wc.reshape(P, P), ws.reshape(P, P), -ws.reshape(P, P)], 1).reshape(P, 3 * P)
    spread = np.zeros((P, P))
    for p in range(P):
        spread[p, 64 + (p // 64) * 32 + (p // 32) % 2] = 1
    c["spread"] = spread
    ures = np.zeros((2, 32, 32))
    for i in range(64):
        x = min(max((i + 0.5) * 0.5 - 0.5, 0.0), 31.0)
        i0 = int(math.floor(x))
        i1 = min(i0 + 1, 31)
        ures[i % 2, i0, i // 2] += 1 - (x - i0)
        ures[i % 2, i1, i // 2] += x - i0
    c["resize"] = np.concatenate([np.einsum("gk,ci->gcik", np.eye(NG), ures[a] / KW).reshape(P, P)
                                   for a in range(2)], axis=1)
    shifts = []
    for dh in (-1, 0, 1):
        for dw in (-1, 0, 1):
            for d in (-1, 0, 1):
                m = np.zeros((2, 64, 2, 64))
                for ho in range(2):
                    hi = ho + dh - 2 * d
                    if 0 <= hi < 2:
                        for wo in range(64):
                            if 0 <= wo + dw < 64:
                                m[hi, wo + dw, ho, wo] = 1
                if m.any():
                    shifts.append(m.reshape(P, P))
    c["shifts"] = np.concatenate(shifts, axis=1)
    up = np.zeros((64, 16))
    for o in range(64):
        s = (o + 0.5) / 4 - 0.5
        i0 = math.floor(s)
        up[o, min(max(i0, 0), 15)] += 1 - (s - i0)
        up[o, min(max(i0 + 1, 0), 15)] += s - i0
    wr = np.array([[7, 1], [5, 3], [3, 5], [1, 7]]) / 8.0
    u = np.einsum("dr,ws->rsdw", wr, up).reshape(2, 1, 16, 256)
    c["upsample"] = np.broadcast_to(u.transpose(1, 0, 2, 3), (3, 2, 16, 256)).reshape(96, 256)
    g = up.T @ up
    kk = np.kron(g, g)
    c["up_gram"] = np.concatenate([kk[:P], kk[P:]], axis=1)
    c["ident"] = np.eye(P)
    c["group_ones"] = np.kron(np.eye(NG), np.ones((GC, GC)))
    c["group_sel"] = np.kron(np.eye(NG), np.ones((GC, 1)))
    c["group_cols"] = np.tile(np.kron(np.eye(NG), np.ones((GC, 1))), (1, HH))
    c["chan_sel"] = np.tile(np.eye(GC), (NG, 1))
    return {"c_" + n: np.ascontiguousarray(a, dtype=np.float32) for n, a in c.items()}


ARG_BANKS = [0, 1, 2, 3, 5, 4, 0, 1]
SCORE_BANKS = [6, 3]
EARLY = 4
TAP_FILLS = [(0, 11), (11, 11), (22, 10)]
SHIFT_PLAN = [(kh * 3 + kw, d) for kh in range(3) for kw in range(3) for d in (-1, 0, 1)
              if any(0 <= ho + (kh - 1) - 2 * d < 2 for ho in range(2))]


class Steps:

    def __init__(self, sem, names):
        self.sem, self.names, self.pos = sem, names, 0

    def done(self, name):
        assert self.names[self.pos] == name, (self.names[self.pos], name)
        self.pos = (self.pos + 1) % len(self.names)
        return self.sem

    def at(self, i, name):
        return i * len(self.names) + self.names.index(name) + 1


def begun(i):
    return not isinstance(i, int) or i >= 0


def build(nc, a, out):
    ctx = ExitStack()
    x_tiles = a["x"].rearrange("b (t p) h w -> (b t) p (h w)", p=P)
    out_tiles = out.rearrange("b (t p) h w -> (b t) p (h w)", p=P)
    low3 = nc.dram_tensor("low3", [NT, 3, 18 * PW, P], BF16, kind="Internal").ap()

    turn = nc.dram_tensor("turn", [2, P, PIX], F32, kind="Internal").ap()
    map_turn = nc.dram_tensor("map_turn", [2, HH, NG, PARTS, P], BF16, kind="Internal").ap()

    with ctx:
        def sb(name, cols, dt=F32, parts=P):
            return ctx.enter_context(nc.sbuf_tensor(name, [parts, cols], dt))

        def sem(name):
            return ctx.enter_context(nc.semaphore(name))

        def steps(name, names):
            return Steps(sem(name), names)

        bank = [ctx.enter_context(nc.psum_tensor(f"bank{k}", [P, 512], F32)) for k in range(8)]

        ident = sb("ident", P)
        gones = sb("group_ones", P)
        gsel = sb("group_sel", NG)
        gcols = sb("group_cols", P)
        csel = sb("chan_sel", GC)
        dft_h = sb("dft_h", P)
        dft_w = sb("dft_w", 3 * P)
        spread = sb("spread", P)
        resize_half = sb("resize_half", 4 * P, F32, 64)
        resize = sb("resize", 2 * P)
        shifts = sb("shifts", len(SHIFT_PLAN) * P)
        upmat = sb("upmat", 256, BF16, 96)
        w1bd = sb("w1bd", P)
        wpbd = sb("wpbd", P)
        wptbd = sb("wptbd", P)
        colw = sb("colw", 16)
        B1, GAMMA, BETA, BDW, BPW, BFP = range(6)
        wdw = sb("wdw", 9)
        taps = sb("taps", P)
        half = sb("half", 2)
        argw = sb("argw", P, BF16, ARG_ROWS)
        fpw = sb("fpw", 4, BF16)
        argw_t = sb("argw_t", ARG_ROWS)
        wts0 = sb("wts0", 1)
        beta_row = sb("beta_row", GC)
        cw = sb("cw", 64)
        consts = [(ident, "c_ident"), (gones, "c_group_ones"), (gsel, "c_group_sel"), (csel, "c_chan_sel"), (gcols, "c_group_cols"),
                  (dft_h, "c_dft_h"), (dft_w, "c_dft_w"),
                  (spread, "c_spread"), (resize, "c_resize"), (shifts, "c_shifts")]

        ARENA = 46000
        arena = sb("arena", ARENA)
        at = [0]

        def carve(cols, dt=F32, parts=P):
            n = cols if dt == F32 else cols // 2
            v = arena[0:parts, at[0]:at[0] + n]
            at[0] += n
            assert at[0] <= ARENA, at[0]
            return v if dt == F32 else v.bitcast(BF16)

        XR = 4
        oall = carve(2 * B * LOW).rearrange("p (o b l) -> p o b l", o=2, b=B)
        gram = carve(2 * LOW).rearrange("p (k l) -> p k l", k=2)
        wp = carve(2 * CH).rearrange("p (o c) -> p o c", o=2)
        cov = carve(2 * TD).rearrange("p (o d) -> p o d", o=2)
        mark = at[0]
        xr = [carve(PIX) for _ in range(XR)]
        wq = carve(TPB * 3 * TD).rearrange("p (t o) -> p t o", t=TPB)
        pooled = carve(TPB * LOW).rearrange("p (t l) -> p t l", t=TPB)
        xn = carve(TPB * LOW).rearrange("p (t l) -> p t l", t=TPB)
        st = carve(2 * TPB)
        gn = carve(8 * TPB)
        tempc = carve(2)
        qk = carve(4 * LOW).rearrange("p (o l) -> p o l", o=4)
        qk2 = carve(4 * LOW).rearrange("p (o l) -> p o l", o=4)
        vt = carve(2 * TD).rearrange("p (m d) -> p m d", m=2)
        prob = carve(2 * LOW).rearrange("p (l m) -> p l m", l=2)
        probT = carve(2 * LOW).rearrange("p (m l) -> p m l", m=2)
        hc = carve(8)
        oT = carve(2 * TD).rearrange("p (l d) -> p l d", l=2)
        ko = carve(2 * TD).rearrange("p (l d) -> p l d", l=2)
        junk1 = carve(PIX, BF16)
        at[0] = mark
        omean = carve(2)
        zw = carve(2 * CH).rearrange("p (o c) -> p o c", o=2)
        wm = carve(2 * CH).rearrange("p (o c) -> p o c", o=2)
        bmean, bvar, bgam, bbet = carve(CH), carve(CH), carve(CH), carve(CH)
        ob = carve(2 * LOW).rearrange("p (o l) -> p o l", o=2)
        ylow = [carve(CH) for _ in range(2)]
        part = [[carve(CH, BF16) for _ in range(3)] for _ in range(2)]
        ones = carve(P)

        at[0] = 0
        XS = carve(PIX)
        X = [carve(PIX) for _ in range(2)]
        YS = [carve(17 * P, BF16, 96).rearrange("p (i c) -> p i c", i=17) for _ in range(2)]
        GT = carve(PIX)
        G2 = carve(PIX)
        AH = carve(PIX)
        MAG = carve(2048)
        SQ = [carve(512) for _ in range(2)]
        SIG = [carve(1024) for _ in range(4)]
        TR = carve(2048)
        JUNK = carve(PIX, BF16)
        TP = carve(9 * NG * 34).rearrange("p (t h g) -> p t h g", t=9, g=NG)
        TG = carve(NG * HH)
        ROWS = carve(PIX, BF16, ARG_ROWS)
        RC = carve(P)
        CATS = [carve(P) for _ in range(2)]
        FRL = carve(GC)
        EDGE = carve(6)
        POWER = carve(1)
        SHW = [carve(P) for _ in range(2)]
        PAR = [carve(32) for _ in range(2)]
        SM = carve(64)
        FR = carve(32)
        ALG = carve(P)
        EO = carve(P)
        ALT = [carve(64) for _ in range(2)]
        ALTT = carve(P, F32, 64)
        SQN = carve(64)
        NYM = carve(64)
        FM = carve(P, F32, 64)
        MAP = carve(2 * PARTS * P, BF16).rearrange("p (m s x) -> p m s x", m=2, s=PARTS)
        REST = [carve(P) for _ in range(2)]

        cst = sem("consts_landed")
        upl = sem("upmat_landed")
        zeroed = sem("tables_zeroed")
        blocks = sem("blocks_landed")
        xl = [sem(f"x_slot{k}_landed") for k in range(XR)]
        vector_setup = steps("vector_setup", ["wfp", "sel", "hi", "hif", "r1", "mid", "midf", "lo", "selw0", "selw1", "selw2", "max", "rsum", "s1", "p", "wp9", "taps", "c0", "c1", "wts0", "argw", "half0", "half1"])
        scalar_setup = steps("scalar_setup", ["exprow", "expcol"])
        tensor_setup = steps("tensor_setup", ["argw", "p", "const"])
        vector_pool = steps("vector_pool", ["pool", "sum"])
        scalar_squares = steps("scalar_squares", ["sq"])
        tensor_imagestats = steps("tensor_imagestats", ["stats"])
        vector_imagestats = steps("vector_imagestats", ["mean", "msq", "var0", "var", "rstd", "r16", "shift"]
                      + [f"xn{t}" for t in range(TPB)])
        scalar_imagestats = steps("scalar_imagestats", ["std"])
        tensor_qkv = steps("tensor_qkv", ["qk", "v", "norms"])
        vector_qkv = steps("vector_qkv", ["copy", "v", "floor", "recip", "qn", "kn"])
        scalar_qkv = steps("scalar_qkv", ["sq", "norm"])
        tensor_scores = steps("tensor_scores", ["scores"])
        tensor_head = steps("tensor_head", ["transpose", "out"])
        vector_head = steps("vector_head", ["max", "rsum", "scale0", "scale1", "probT"])
        scalar_head = steps("scalar_head", ["exp0", "exp1"])
        tensor_image_end = steps("tensor_image_end", ["ko", "cov"])
        vector_image_end = steps("vector_image_end", ["o", "oT", "ko", "cov"])
        vector_taps_zero = steps("vector_taps_zero", ["zero"])
        vector_cov_zero = steps("vector_cov_zero", ["zero"])
        bnl = sem("bn_rows_landed")
        vector_bn = steps("vector_bn", ["ones", "osum0", "osum1", "omean", "zw0", "zw1", "zw2", "zw3", "wm0", "wm1",
                                   "mean0", "mean1", "e0", "e1", "msq", "var", "eps", "rstd", "scale", "ms", "shift", "wscale0", "wscale1"])
        tensor_bn = steps("tensor_bn", ["z", "mean", "sq"])
        scalar_bn = steps("scalar_bn", ["std"])
        vector_ob = steps("vector_ob", ["ob"])
        vector_low = steps("vector_low", [f"{n}{k}" for k in range(2) for n in ("add0", "add1", "hi", "rest", "mid")])
        pool_low = steps("pool_low", ["lo0", "lo1"])
        tensor_low = steps("tensor_low", ["y0", "y1"])
        lows = [sem(f"low_parts{k}_stored") for k in range(2)]
        x_landed = sem("tile_landed")
        YL = [sem(f"low_slot{k}_landed") for k in range(2)]
        tensor_front = steps("tensor_front", [f"up{q}" for q in range(8)] + ["stats"])
        vector_front = steps("vector_front", [f"add{q}" for q in range(8)]
                   + ["pairs", "rows", "alt", "total", "mean", "msq", "var", "shift", "std", "offset", "r64", "altn", "gx", "cat"])
        scalar_front = steps("scalar_front", ["sq"])
        pool_front = steps("pool_front", ["col0", "rstd"] + [f"col{k}" for k in range(1, 6)])
        pool_gate = steps("pool_gate", ["rstd"])
        vector_pads = steps("vector_pads", ["edge", "alpha"])
        turned = sem("gx_in_dram")
        g2l = sem("rows_layout_landed")
        tensor_gate = steps("tensor_gate", ["w1", "pw", "lrow", "const"])
        scalar_gate = steps("scalar_gate", ["sig", "sq", "exprow", "expcol"])
        vector_gate = steps("vector_gate", ["tot", "edges0", "edges1", "f0", "f1", "corner", "fw", "dw",
                                   "dwb", "gates", "t1", "x2m", "lsel", "gated", "gmean", "gmsq", "max", "gvar", "rsum", "s2",
                                   "sg", "alpha", "alg", "am", "kc", "kcon"])
        tensor_taps = steps("tensor_taps", ["t0", "t1", "t2"])
        scalar_taps = steps("scalar_taps", ["t0", "t1", "t2"])
        tensor_spectrum = steps("tensor_spectrum", ["nyqt"] + [f"h{k}" for k in range(8)] + ["nyq"]
                                + [f"w{k}" for k in range(8)] + ["chan"])
        scalar_spectrum = steps("scalar_spectrum", ["nyqt"] + [f"h{k}" for k in range(8)] + ["nyqsq"]
                                + [f"w{k}" for k in range(4)] + ["nyqroot0", "nyqroot", "w4", "w5", "root0", "w6", "w7", "root1", "fm0", "fm1"])
        vector_spectrum = steps("vector_spectrum", ["nyq"] + [f"w{k}" for k in range(8)])
        tensor_back = steps("tensor_back", ["gsum0", "gsum1", "wmap", "fmap"] + [f"arg{q}" for q in range(8)])
        vector_back = steps("vector_back", ["gsum", "whi", "wrest", "wmid", "wmap", "fhi", "frest", "fmid", "fmap"] + [f"mul{q}" for q in range(4)])
        scalar_back = steps("scalar_back", [f"sig{q}" for q in range(8)] + [f"mean{q}" for q in range(4)])
        map_stored = sem("map_parts_stored")
        mapl = sem("map_rows_landed")
        stored = [sem(f"out_slot{k}_stored") for k in range(4)]
        pads = sem("pads_zeroed")

        block = ctx.enter_context(nc.Block())
        N_CONST = len(consts) + 7 + 8

        @block.sync
        def _(sp):
            for dst, name in consts:
                sp.dma_start(dst[:, :], a[name]).then_inc(cst, 16)
            for k, name in enumerate(["b1", "gn_gamma", "gn_beta", "b_dw", "b_pw", "b_fp"]):
                sp.dma_start(colw[:, k:k + 1], a[name]).then_inc(cst, 16)
            sp.dma_start(wdw[:, :], a["w_dw"]).then_inc(cst, 16)
            for j in range(2):
                sp.dma_start(resize_half[:, j * 2 * P:(j + 1) * 2 * P],
                             a["c_resize"][64 * j:64 * j + 64, :]).then_inc(cst, 16)
            sp.dma_start(gram, a["c_up_gram"].rearrange("p (k l) -> p k l", k=2)).then_inc(cst, 16)
            sp.dma_start(wp, a["w_proj_t"].rearrange("(o p) c -> p o c", p=P)).then_inc(cst, 16)
            sp.dma_start(wq, a["w_qkv_t"].rearrange("(t p) o -> p t o", p=P)).then_inc(cst, 16)
            sp.dma_start(tempc, a["temperature"]).then_inc(cst, 16)
            sp.dma_start(beta_row[:, :], a["beta_row"]).then_inc(cst, 16)
            sp.dma_start(cw[:, 0:32], a["w_fp"]).then_inc(cst, 16)
            sp.wait_ge(zeroed, 1)
            for g in range(NG):
                s = slice(g * GC, g * GC + GC)
                sp.dma_start(w1bd[s, s], a["w1_t"]).then_inc(blocks, 16)
                sp.dma_start(wpbd[s, s], a["w_pw"]).then_inc(blocks, 16)
                sp.dma_start(wptbd[s, s], a["w_pw_t"]).then_inc(blocks, 16)

            def load1(b, s):
                n = b * TPB + s - XR
                if begun(n):
                    sp.wait_ge(scalar_squares.sem, scalar_squares.at(n, "sq"))
                    sp.wait_ge(vector_pool.sem, vector_pool.at(n, "pool"))
                sp.dma_start(xr[s % XR], x_tiles[b * TPB + s]).then_inc(xl[s % XR], 16)

            for s in range(TPB):
                load1(0, s)
            with sp.Fori(1, B) as b:
                for s in range(TPB):
                    load1(b, s)

            sp.wait_ge(vector_image_end.sem, vector_image_end.at(B - 1, "cov"))
            sp.wait_ge(tensor_image_end.sem, tensor_image_end.at(B - 1, "cov"))
            sp.dma_start(bgam, a["bn_gamma"].partition_broadcast(P)).then_inc(bnl, 16)
            sp.dma_start(bbet, a["bn_beta"].partition_broadcast(P)).then_inc(bnl, 16)
            with sp.Fori(0, B) as b:
                for k in range(2):
                    for s in range(3):
                        if s < 2:
                            sp.wait_ge(vector_low.sem, vector_low.at(b, ("hi", "mid")[s] + str(k)))
                        else:
                            sp.wait_ge(pool_low.sem, pool_low.at(b, f"lo{k}"))
                        dst = low3[bass.ds(b * TPB, TPB), s]
                        dst = dst.rearrange("t q c -> q t c")
                        src = part[k][s].rearrange("p (t c) -> p t c", t=TPB)
                        sp.dma_start(dst[16 + k * P:16 + (k + 1) * P], src).then_inc(lows[k], 16)
                        if k == 0:
                            sp.dma_start(dst[0:16], src[0:16]).then_inc(lows[k], 16)
                        else:
                            sp.dma_start(dst[272:288], src[112:128]).then_inc(lows[k], 16)
            sp.wait_ge(lows[0], 16 * (6 * B))
            sp.wait_ge(lows[1], 16 * (6 * B))

            def load_low(i, u):
                if begun(i - 2):
                    sp.wait_ge(tensor_front.sem, tensor_front.at(i - 2, "up7"))
                for s in range(3):
                    for r in range(2):
                        p0 = s * 32 + r * 16
                        sp.dma_start(YS[u][p0:p0 + 16], low3[i, s, r * 16:r * 16 + 272, :].rearrange(
                            "(k q) c -> q k c", q=16)).then_inc(YL[u], 16)

            def load_x(i):
                if begun(i - 1):
                    sp.wait_ge(vector_front.sem, vector_front.at(i - 1, "add7"))
                sp.dma_start(XS, x_tiles[i]).then_inc(x_landed, 16)

            def turn_out(i, u):
                sp.wait_ge(vector_front.sem, vector_front.at(i, "gx"))
                sp.dma_start(turn[u], X[u]).then_inc(turned, 16)

            def turn_in(i, u):
                sp.wait_ge(turned, 16 * (i + 1))
                if begun(i - 1):
                    sp.wait_ge(tensor_spectrum.sem, tensor_spectrum.at(i - 1, "h7"))
                for j in range(2):
                    sp.dma_start(G2[64 * j:64 * j + 64, :].rearrange("h (c w) -> h c w", c=64),
                                 turn[u, 64 * j:64 * j + 64, :].rearrange("c (h w) -> h c w", h=64)).then_inc(g2l, 16)

            def map_out(i, m):
                sp.wait_ge(vector_back.sem, vector_back.at(i, ("wmap", "fmap")[m]))
                if m == 0 and begun(i - 1):
                    sp.wait_ge(mapl, 16 * ((1 + PARTS) * i))
                sp.dma_start(map_turn[m].rearrange("h g s x -> (h g) (s x)"),
                             MAP[:, m].rearrange("p s x -> p (s x)")).then_inc(map_stored, 16)

            def map_in(i, m):
                sp.wait_ge(map_stored, 16 * (2 * i + 1 + m))
                if m == 0 and begun(i - 1):
                    sp.wait_ge(tensor_back.sem, tensor_back.at(i - 1, "arg7"))
                n = PARTS * NG
                for j in range((1, PARTS)[m]):
                    r = n * (m + j)
                    sp.dma_start(ROWS[r:r + n, :].rearrange("r (h x) -> r h x", h=HH),
                                 map_turn[m].rearrange("h g s x -> (g s) h x")).then_inc(mapl, 16)

            def store_quarter(i, q):
                sp.wait_ge(scalar_back.sem, scalar_back.at(i, f"mean{q}"))
                sp.dma_start(out_tiles[i][:, q * 1024:(q + 1) * 1024], SIG[q]).then_inc(stored[q], 16)

            def period(i, u, new=True, load=True):
                if load:
                    load_low(i + 2, u)
                    load_x(i + 2)
                if new:
                    turn_out(i + 1, 1 - u)
                    turn_in(i + 1, 1 - u)
                for m in range(2):
                    map_out(i, m)
                    map_in(i, m)
                for q in range(4):
                    store_quarter(i, q)

            for u in range(2):
                load_low(u, u)
                load_x(u)
            turn_out(0, 0)
            turn_in(0, 0)
            period(0, 0)
            period(1, 1)
            with sp.Fori(1, NT // 2 - 1) as pr:
                period(2 * pr, 0)
                period(2 * pr + 1, 1)
            period(NT - 2, 0, load=False)
            period(NT - 1, 1, new=False, load=False)
            for q in range(4):
                sp.wait_ge(stored[q], 16 * NT)

        @block.gpsimd
        def _(pool):
            pool.memset(w1bd[:, :], 0.0)
            pool.memset(wpbd[:, :], 0.0)
            pool.memset(wptbd[:, :], 0.0).then_inc(zeroed, 1)
            pool.dma_start(upmat[:, :], a["c_upsample"]).then_inc(upl, 16)

            def low(b):
                for k in range(2):
                    pool.wait_ge(vector_low.sem, vector_low.at(b, f"mid{k}"))
                    pool.tensor_tensor(part[k][2], ylow[k], part[k][1], op=ALU.subtract).then_inc(pool_low.done(f"lo{k}"), 1)

            low(0)
            with pool.Fori(1, B) as b:
                low(b)

            pool.wait_ge(lows[0], 16 * (6 * B))
            pool.wait_ge(lows[1], 16 * (6 * B))
            pool.wait_ge(pool_low.sem, pool_low.at(B - 1, "lo1"))
            pool.wait_ge(tensor_low.sem, tensor_low.at(B - 1, "y1"))
            pool.memset(POWER, -0.5).then_inc(pads, 1)
            pool.memset(TP, 0.0).then_inc(pads, 1)
            pool.wait_ge(pads, 2)

            def front(i, u):
                pool.wait_ge(vector_front.sem, vector_front.at(i, "add7"))
                if begun(i - 1):
                    pool.wait_ge(vector_front.sem, vector_front.at(i - 1, "cat"))
                pool.tensor_tensor(TR[:, 0:2048], X[u][:, 0:2048], X[u][:, 2048:4096],
                                   op=ALU.add).then_inc(pool_front.done("col0"), 1)
                pool.wait_ge(vector_front.sem, vector_front.at(i, "var"))
                pool.tensor_tensor(PAR[u][:, 6:7], PAR[u][:, 4:5], POWER, op=ALU.pow).then_inc(pool_front.done("rstd"), 1)
                n = 1024
                for k in range(1, 6):
                    pool.wait_ge(pool_front.sem, pool_front.at(i, f"col{k - 1}"))
                    dst = RC[:, 64:128] if n == 64 else TR[:, 0:n]
                    pool.tensor_tensor(dst, TR[:, 0:n], TR[:, n:2 * n], op=ALU.add).then_inc(pool_front.done(f"col{k}"), 1)
                    n //= 2
                pool.wait_ge(vector_gate.sem, vector_gate.at(i, "gvar"))
                pool.tensor_tensor(SM[:, 6:7], SM[:, 4:5], POWER, op=ALU.pow).then_inc(pool_gate.done("rstd"), 1)

            front(0, 0)
            front(1, 1)
            with pool.Fori(1, NT // 2) as pr:
                front(2 * pr, 0)
                front(2 * pr + 1, 1)

        @block.scalar
        def _(act):
            act.wait_ge(vector_setup.sem, vector_setup.at(0, "max"))
            act.activation(beta_row[:, :], beta_row[:, :], ACT.Exp, bias=cw[:, 33:34],
                           accum_out=cw[:, 40:41]).then_inc(scalar_setup.done("exprow"), 1)
            act.activation(cw[:, 41:42], colw[:, BETA:BETA + 1], ACT.Exp, bias=cw[:, 33:34]).then_inc(scalar_setup.done("expcol"), 1)

            def square1(b, s):
                act.wait_ge(xl[s % XR], 16 * (2 * b + s // XR + 1))
                if s == 0:
                    if begun(b - 1):
                        act.wait_ge(tensor_imagestats.sem, tensor_imagestats.at(b - 1, "stats"))
                if begun(b * TPB + s - 1):
                    act.wait_ge(scalar_squares.sem, scalar_squares.at(b * TPB + s - 1, "sq"))
                act.activation(junk1, xr[s % XR], ACT.Square, accum_out=st[:, TPB + s:TPB + s + 1]).then_inc(scalar_squares.done("sq"), 1)

            def image1(b):
                act.wait_ge(vector_imagestats.sem, vector_imagestats.at(b, "var"))
                act.activation(gn[:, 24:32], gn[:, 16:24], ACT.Sqrt).then_inc(scalar_imagestats.done("std"), 1)

            def lengths1(b):
                act.wait_ge(vector_qkv.sem, vector_qkv.at(b, "copy"))
                act.activation(qk2, qk, ACT.Square).then_inc(scalar_qkv.done("sq"), 1)
                act.wait_ge(tensor_qkv.sem, tensor_qkv.at(b, "norms"))
                act.activation(qk2[:, 0:2, :], bank[4][:, :].rearrange("p (o l) -> p o l", o=2), ACT.Sqrt)
                act.activation(qk2[:, 2:4, :], bank[5][:, :].rearrange("p (o l) -> p o l", o=2),
                               ACT.Sqrt).then_inc(scalar_qkv.done("norm"), 1)

            def head1(n, h):
                act.wait_ge(vector_head.sem, vector_head.at(n, "max"))
                for l in range(2):
                    act.activation(prob[:, l, :], bank[SCORE_BANKS[h % 2]][:, l * LOW:(l + 1) * LOW], ACT.Exp, bias=hc[:, l:l + 1],
                                   accum_out=hc[:, 2 + l:3 + l]).then_inc(scalar_head.done(f"exp{l}"), 1)

            def next_tiles(b):
                for s in range(EARLY):
                    square1(b, s)

            def image_step(b, more=True):
                for h in range(HEADS):
                    head1((b - 1) * HEADS + h, h)
                    if EARLY + h < TPB:
                        square1(b, EARLY + h)
                image1(b)
                if more:
                    next_tiles(b + 1)
                lengths1(b)

            for s in range(TPB):
                square1(0, s)
            image1(0)
            next_tiles(1)
            lengths1(0)
            image_step(1)
            with act.Fori(2, B - 1) as b:
                image_step(b)
            image_step(B - 1, more=False)
            for h in range(HEADS):
                head1((B - 1) * HEADS + h, h)

            act.wait_ge(vector_bn.sem, vector_bn.at(0, "eps"))
            act.activation(bvar, bvar, ACT.Sqrt).then_inc(scalar_bn.done("std"), 1)

            act.wait_ge(vector_setup.sem, vector_setup.at(0, "half1"))

            def front(i, u):
                act.wait_ge(vector_front.sem, vector_front.at(i, "add7"))
                if begun(i - 1):
                    act.wait_ge(tensor_front.sem, tensor_front.at(i - 1, "stats"))
                    act.wait_ge(scalar_gate.sem, scalar_gate.at(i - 1, "sq"))
                act.activation(JUNK, X[u], ACT.Square, accum_out=PAR[u][:, 1:2]).then_inc(scalar_front.done("sq"), 1)

            def gate(i, u):
                act.wait_ge(tensor_gate.sem, tensor_gate.at(i, "w1"))
                act.activation(SHW[u], bank[7][:, 128:256], ACT.Tanh, bias=half[:, 0:1],
                               scale=0.5).then_inc(scalar_gate.done("sig"), 1)

            def gate_stats(i):
                act.wait_ge(vector_gate.sem, vector_gate.at(i, "gated"))
                act.wait_ge(scalar_front.sem, scalar_front.at(i, "sq"))
                act.activation(JUNK, GT, ACT.Square, accum_out=SM[:, 1:2]).then_inc(scalar_gate.done("sq"), 1)

            def gate_softmax(i):
                act.wait_ge(vector_gate.sem, vector_gate.at(i, "max"))
                act.activation(FR, bank[7][:, 320:352], ACT.Exp, bias=SM[:, 10:11],
                               accum_out=SM[:, 11:12]).then_inc(scalar_gate.done("exprow"), 1)
                act.activation(SM[:, 12:13], SM[:, 9:10], ACT.Exp, bias=SM[:, 10:11]).then_inc(scalar_gate.done("expcol"), 1)

            def taps2(i):
                for k, (c0, n) in enumerate(TAP_FILLS):
                    act.wait_ge(tensor_taps.sem, tensor_taps.at(i, f"t{k}"))
                    if k == 0:
                        if begun(i - 1):
                            act.wait_ge(tensor_back.sem, tensor_back.at(i - 1, "wmap"))
                    act.activation(TP[:, :, 1 + c0:1 + c0 + n, :],
                                   bank[4 + k % 2][:, 0:36 * n].rearrange("p (c t g) -> p t c g", t=9, g=NG),
                                   ACT.Copy).then_inc(scalar_taps.done(f"t{k}"), 1)
                    if k == 1:
                        gate_softmax(i)

            def nyquist_turned(i):
                act.wait_ge(tensor_spectrum.sem, tensor_spectrum.at(i, "nyqt"))
                if begun(i - 1):
                    act.wait_ge(tensor_spectrum.sem, tensor_spectrum.at(i - 1, "nyq"))
                act.activation(ALTT, bank[6][0:64, 384:512], ACT.Copy).then_inc(scalar_spectrum.done("nyqt"), 1)

            def rows_done(i, k):
                act.wait_ge(tensor_spectrum.sem, tensor_spectrum.at(i, f"h{k}"))
                if k == 0 and begun(i - 1):
                    act.wait_ge(tensor_spectrum.sem, tensor_spectrum.at(i - 1, "w7"))
                act.activation(AH[:, k * 512:(k + 1) * 512], bank[2 + k % 2][:, :],
                               ACT.Copy).then_inc(scalar_spectrum.done(f"h{k}"), 1)

            def spectrum(i, u, new):
                act.wait_ge(tensor_spectrum.sem, tensor_spectrum.at(i, "nyq"))
                if begun(i - 1):
                    act.wait_ge(scalar_spectrum.sem, scalar_spectrum.at(i - 1, "nyqroot"))
                act.activation(SQN, bank[6][:, 384:448], ACT.Square).then_inc(scalar_spectrum.done("nyqsq"), 1)
                for k in range(8):
                    act.wait_ge(tensor_spectrum.sem, tensor_spectrum.at(i, f"w{k}"))
                    if k >= 2:
                        act.wait_ge(vector_spectrum.sem, vector_spectrum.at(i, f"w{k - 2}"))
                    elif begun(i - 1):
                        act.wait_ge(vector_spectrum.sem, vector_spectrum.at(i - 1, f"w{k + 6}"))
                    act.activation(SQ[k % 2], bank[2 + k % 2][:, :], ACT.Square).then_inc(scalar_spectrum.done(f"w{k}"), 1)
                    if k == 3:
                        if new:
                            gate(i + 1, 1 - u)
                        nyquist_root(i)
                    elif k == 5:
                        act.wait_ge(vector_spectrum.sem, vector_spectrum.at(i, "w3"))
                        act.activation(MAG[:, 0:1024], MAG[:, 0:1024], ACT.Sqrt).then_inc(scalar_spectrum.done("root0"), 1)
                act.wait_ge(vector_spectrum.sem, vector_spectrum.at(i, "w7"))
                act.activation(MAG[:, 1024:2048], MAG[:, 1024:2048], ACT.Sqrt).then_inc(scalar_spectrum.done("root1"), 1)

            def frequencies(i):
                act.wait_ge(tensor_spectrum.sem, tensor_spectrum.at(i, "chan"))
                if begun(i - 1):
                    act.wait_ge(tensor_back.sem, tensor_back.at(i - 1, "fmap"))
                fm = bank[6][0:64, 128:256].rearrange("p (s j k) -> p s j k", s=2, j=2)
                dst = FM.rearrange("p (j f) -> p j f", j=2)
                act.activation(dst[:, :, 0:32], fm[:, 0], ACT.Copy).then_inc(scalar_spectrum.done("fm0"), 1)
                act.activation(dst[:, :, 32:64], fm[:, 1, :, ::-1], ACT.Copy).then_inc(scalar_spectrum.done("fm1"), 1)

            def nyquist_root(i):
                act.wait_ge(vector_spectrum.sem, vector_spectrum.at(i, "nyq"))
                if begun(i - 1):
                    act.wait_ge(tensor_back.sem, tensor_back.at(i - 1, "fmap"))
                act.activation(NYM[:, 0:33], SQN[:, 0:33], ACT.Sqrt).then_inc(scalar_spectrum.done("nyqroot0"), 1)
                act.activation(NYM[:, 33:64], SQN[:, 31:0:-1], ACT.Sqrt).then_inc(scalar_spectrum.done("nyqroot"), 1)

            def back(i):
                for q in range(8):
                    act.wait_ge(tensor_back.sem, tensor_back.at(i, f"arg{q}"))
                    if q % 2 == 0:
                        if begun(i - 1):
                            act.wait_ge(stored[q // 2], 16 * (i))
                    act.activation(SIG[q // 2][:, (q % 2) * 512:(q % 2 + 1) * 512], bank[ARG_BANKS[q]][:, :], ACT.Tanh,
                                   bias=half[:, 1:2], scale=0.5).then_inc(scalar_back.done(f"sig{q}"), 1)

            def add_mean(i, u, q):
                act.wait_ge(vector_back.sem, vector_back.at(i, f"mul{q}"))
                act.activation(SIG[q], SIG[q], ACT.Identity, bias=PAR[u][:, 2:3],
                               scale=0.5).then_inc(scalar_back.done(f"mean{q}"), 1)

            def period(i, u, new=True):
                nyquist_turned(i)
                for k in range(8):
                    rows_done(i, k)
                    if k % 2 and begun(i - 1):
                        add_mean(i - 1, 1 - u, k // 2)
                if new:
                    front(i + 1, 1 - u)
                spectrum(i, u, new)
                frequencies(i)
                if new:
                    gate_stats(i + 1)
                    taps2(i + 1)
                back(i)

            front(0, 0)
            gate(0, 0)
            gate_stats(0)
            taps2(0)
            period(0, 0)
            period(1, 1)
            with act.Fori(1, NT // 2 - 1) as pr:
                period(2 * pr, 0)
                period(2 * pr + 1, 1)
            period(NT - 2, 0)
            period(NT - 1, 1, new=False)
            for q in range(4):
                add_mean(NT - 1, 1, q)

        @block.vector
        def _(dve):
            dve.wait_ge(cst, 16 * N_CONST)
            dve.memset(taps[:, :], 0.0).then_inc(vector_taps_zero.done("zero"), 1)
            dve.memset(cov, 0.0).then_inc(vector_cov_zero.done("zero"), 1)
            dve.tensor_reduce(cw[:, 32:33], cw[:, 0:32], axis=AX.X, op=ALU.add).then_inc(vector_setup.done("wfp"), 1)
            dve.wait_ge(vector_setup.sem, vector_setup.at(0, "wfp"))
            by_group = gsel[:, :].unsqueeze(2).to_broadcast([P, NG, PARTS])
            aw = argw_t[:, :].rearrange("p (j g s) -> p j g s", j=1 + PARTS, s=PARTS)
            dve.tensor_copy(aw[:, 0], by_group).then_inc(vector_setup.done("sel"), 1)
            dve.tensor_copy(fpw[:, 0:1], cw[:, 32:33]).then_inc(vector_setup.done("hi"), 1)
            dve.wait_ge(vector_setup.sem, vector_setup.at(0, "hi"))
            dve.tensor_copy(cw[:, 44:45], fpw[:, 0:1]).then_inc(vector_setup.done("hif"), 1)
            dve.tensor_tensor(cw[:, 47:48], cw[:, 32:33], fpw[:, 0:1], op=ALU.subtract).then_inc(vector_setup.done("r1"), 1)
            dve.wait_ge(vector_setup.sem, vector_setup.at(0, "r1"))
            dve.tensor_copy(fpw[:, 1:2], cw[:, 47:48]).then_inc(vector_setup.done("mid"), 1)
            dve.wait_ge(vector_setup.sem, vector_setup.at(0, "mid"))
            dve.tensor_copy(cw[:, 45:46], fpw[:, 1:2]).then_inc(vector_setup.done("midf"), 1)
            dve.tensor_tensor(cw[:, 46:47], cw[:, 47:48], fpw[:, 1:2], op=ALU.subtract).then_inc(vector_setup.done("lo"), 1)
            dve.wait_ge(vector_setup.sem, vector_setup.at(0, "lo"))
            for j in range(PARTS):
                dve.tensor_scalar(aw[:, 1 + j], by_group, cw[:, 44 + j:45 + j], None,
                                  ALU.mult).then_inc(vector_setup.done(f"selw{j}"), 1)
            dve.tensor_reduce(cw[:, 33:34], beta_row[:, :], axis=AX.X, op=ALU.max,
                              negate=True).then_inc(vector_setup.done("max"), 1)
            dve.wait_ge(scalar_setup.sem, scalar_setup.at(0, "expcol"))
            dve.reciprocal(cw[:, 34:35], cw[:, 40:41]).then_inc(vector_setup.done("rsum"), 1)
            dve.wait_ge(vector_setup.sem, vector_setup.at(0, "rsum"))
            dve.tensor_tensor(cw[:, 35:36], cw[:, 41:42], cw[:, 34:35], op=ALU.mult).then_inc(vector_setup.done("s1"), 1)
            dve.wait_ge(tensor_setup.sem, tensor_setup.at(0, "p"))
            dve.tensor_copy(cw[:, 42:43], bank[0][:, 0:1]).then_inc(vector_setup.done("p"), 1)
            dve.wait_ge(vector_setup.sem, vector_setup.at(0, "p"))
            dve.tensor_scalar(cw[:, 52:61], wdw[:, :], cw[:, 42:43], None, ALU.mult).then_inc(vector_setup.done("wp9"), 1)
            dve.wait_ge(vector_setup.sem, vector_setup.at(0, "wp9"))
            dve.wait_ge(vector_taps_zero.sem, vector_taps_zero.at(0, "zero"))
            dve.tensor_tensor(taps[:, 0:36].rearrange("p (t g) -> p t g", g=NG),
                              cw[:, 52:61].unsqueeze(2).to_broadcast([P, 9, NG]),
                              gsel[:, :].unsqueeze(1).to_broadcast([P, 9, NG]), op=ALU.mult).then_inc(vector_setup.done("taps"), 1)
            dve.tensor_tensor(cw[:, 36:37], cw[:, 35:36], colw[:, BPW:BPW + 1], op=ALU.mult).then_inc(vector_setup.done("c0"), 1)
            dve.wait_ge(vector_setup.sem, vector_setup.at(0, "c0"))
            dve.scalar_tensor_tensor(cw[:, 43:44], colw[:, BDW:BDW + 1], cw[:, 42:43], cw[:, 36:37],
                                     op0=ALU.mult, op1=ALU.add).then_inc(vector_setup.done("c1"), 1)
            dve.wait_ge(tensor_setup.sem, tensor_setup.at(0, "const"))
            dve.tensor_copy(wts0[:, :], bank[0][:, 1:2]).then_inc(vector_setup.done("wts0"), 1)
            dve.tensor_copy(argw[:, :], bank[0][0:ARG_ROWS, 128:256]).then_inc(vector_setup.done("argw"), 1)
            dve.tensor_scalar(half[:, 0:1], colw[:, B1:B1 + 1], 0.5, None, ALU.mult).then_inc(vector_setup.done("half0"), 1)
            dve.tensor_scalar(half[:, 1:2], colw[:, BFP:BFP + 1], 0.5, None, ALU.mult).then_inc(vector_setup.done("half1"), 1)

            def pool1(b, s):
                dve.wait_ge(xl[s % XR], 16 * (2 * b + s // XR + 1))
                if s == 0 and begun(b - 1):
                    dve.wait_ge(vector_imagestats.sem, vector_imagestats.at(b - 1, f"xn{TPB - 1}"))
                dve.tensor_reduce(pooled[:, s, :].rearrange("p (r c) -> p r c", r=PH),
                                  xr[s % XR].rearrange("p (r a c e) -> p r c a e", r=PH, a=4, c=PW),
                                  axis=AX.XY, op=ALU.add).then_inc(vector_pool.done("pool"), 1)
                dve.wait_ge(vector_pool.sem, vector_pool.at(b * TPB + s, "pool"))
                if s == 0:
                    if begun(b - 1):
                        dve.wait_ge(tensor_imagestats.sem, tensor_imagestats.at(b - 1, "stats"))
                dve.tensor_reduce(st[:, s:s + 1], pooled[:, s, :], axis=AX.X, op=ALU.add).then_inc(vector_pool.done("sum"), 1)

            def image1(b):
                dve.wait_ge(tensor_imagestats.sem, tensor_imagestats.at(b, "stats"))
                n = 1.0 / (GC * PIX)
                dve.tensor_scalar(gn[:, 0:8], bank[0][:, 0:8], n, None, ALU.mult).then_inc(vector_imagestats.done("mean"), 1)
                dve.wait_ge(vector_imagestats.sem, vector_imagestats.at(b, "mean"))
                dve.tensor_tensor(gn[:, 8:16], gn[:, 0:8], gn[:, 0:8], op=ALU.mult).then_inc(vector_imagestats.done("msq"), 1)
                dve.wait_ge(vector_imagestats.sem, vector_imagestats.at(b, "msq"))
                dve.scalar_tensor_tensor(gn[:, 16:24], bank[0][:, 8:16], n, gn[:, 8:16], op0=ALU.mult,
                                         op1=ALU.subtract).then_inc(vector_imagestats.done("var0"), 1)
                dve.wait_ge(vector_imagestats.sem, vector_imagestats.at(b, "var0"))
                dve.tensor_scalar(gn[:, 16:24], gn[:, 16:24], EPS, None, ALU.add).then_inc(vector_imagestats.done("var"), 1)
                dve.wait_ge(scalar_imagestats.sem, scalar_imagestats.at(b, "std"))
                dve.reciprocal(gn[:, 32:40], gn[:, 24:32]).then_inc(vector_imagestats.done("rstd"), 1)
                dve.wait_ge(vector_imagestats.sem, vector_imagestats.at(b, "rstd"))
                dve.tensor_scalar(gn[:, 40:48], gn[:, 32:40], 1.0 / 16, None, ALU.mult).then_inc(vector_imagestats.done("r16"), 1)
                dve.scalar_tensor_tensor(gn[:, 48:56], gn[:, 0:8], -1.0, gn[:, 32:40], op0=ALU.mult,
                                         op1=ALU.mult).then_inc(vector_imagestats.done("shift"), 1)
                dve.wait_ge(vector_imagestats.sem, vector_imagestats.at(b, "shift"))
                if begun(b - 1):
                    dve.wait_ge(tensor_qkv.sem, tensor_qkv.at(b - 1, "v"))
                for t in range(TPB):
                    dve.tensor_scalar(xn[:, t, :], pooled[:, t, :], gn[:, 40 + t:41 + t], gn[:, 48 + t:49 + t],
                                      ALU.mult, ALU.add).then_inc(vector_imagestats.done(f"xn{t}"), 1)

            def lengths1(b):
                dve.wait_ge(tensor_qkv.sem, tensor_qkv.at(b, "qk"))
                dve.tensor_copy(qk[:, 0:2, :], bank[1][:, :].rearrange("p (o l) -> p o l", o=2))
                dve.tensor_copy(qk[:, 2:4, :], bank[2][:, :].rearrange("p (o l) -> p o l", o=2)).then_inc(vector_qkv.done("copy"), 1)
                dve.wait_ge(tensor_qkv.sem, tensor_qkv.at(b, "v"))
                dve.tensor_copy(vt, bank[3][:, :].rearrange("p (m d) -> p m d", m=2)).then_inc(vector_qkv.done("v"), 1)
                dve.wait_ge(scalar_qkv.sem, scalar_qkv.at(b, "norm"))
                dve.tensor_scalar(qk2, qk2, 1e-12, None, ALU.max).then_inc(vector_qkv.done("floor"), 1)
                dve.wait_ge(vector_qkv.sem, vector_qkv.at(b, "floor"))
                dve.reciprocal(qk2, qk2).then_inc(vector_qkv.done("recip"), 1)
                dve.wait_ge(vector_qkv.sem, vector_qkv.at(b, "recip"))
                for o in range(2):
                    ins = dve.scalar_tensor_tensor(qk[:, o, :], qk[:, o, :], tempc[:, o:o + 1], qk2[:, o, :],
                                                   op0=ALU.mult, op1=ALU.mult)
                ins.then_inc(vector_qkv.done("qn"), 1)
                dve.tensor_tensor(qk[:, 2:4, :], qk[:, 2:4, :], qk2[:, 2:4, :], op=ALU.mult).then_inc(vector_qkv.done("kn"), 1)

            def head_max(n, h):
                dve.wait_ge(tensor_scores.sem, tensor_scores.at(n, "scores"))
                dve.tensor_reduce(hc[:, 0:2], bank[SCORE_BANKS[h % 2]][:, :].rearrange("p (l m) -> p l m", l=2), axis=AX.X,
                                  op=ALU.max, negate=True).then_inc(vector_head.done("max"), 1)

            def head_scale(n):
                dve.wait_ge(scalar_head.sem, scalar_head.at(n, "exp1"))
                dve.reciprocal(hc[:, 4:6], hc[:, 2:4]).then_inc(vector_head.done("rsum"), 1)
                dve.wait_ge(vector_head.sem, vector_head.at(n, "rsum"))
                for l in range(2):
                    dve.tensor_scalar(prob[:, l, :], prob[:, l, :], hc[:, 4 + l:5 + l], None,
                                      ALU.mult).then_inc(vector_head.done(f"scale{l}"), 1)
                dve.wait_ge(tensor_head.sem, tensor_head.at(n, "transpose"))
                if begun(n - 1):
                    dve.wait_ge(tensor_head.sem, tensor_head.at(n - 1, "out"))
                dve.tensor_copy(probT, bank[7][:, :].rearrange("p (m l) -> p m l", m=2)).then_inc(vector_head.done("probT"), 1)

            def finish1(b):
                dve.wait_ge(tensor_head.sem, tensor_head.at(b * TPB + TPB - 1, "out"))
                dst = oall[:, :, b, :] if isinstance(b, int) else oall[:, :, bass.ds(b, 1), :].squeeze(2)
                dve.tensor_copy(dst, bank[1][:, :].rearrange("p (o l) -> p o l", o=2)).then_inc(vector_image_end.done("o"), 1)
                dve.tensor_copy(oT, bank[2][:, :].rearrange("p (l d) -> p l d", l=2)).then_inc(vector_image_end.done("oT"), 1)
                dve.wait_ge(tensor_image_end.sem, tensor_image_end.at(b, "ko"))
                dve.tensor_copy(ko, bank[4][:, :].rearrange("p (l d) -> p l d", l=2)).then_inc(vector_image_end.done("ko"), 1)
                dve.wait_ge(tensor_image_end.sem, tensor_image_end.at(b, "cov"))
                dve.wait_ge(vector_cov_zero.sem, vector_cov_zero.at(0, "zero"))
                if begun(b - 1):
                    dve.wait_ge(vector_image_end.sem, vector_image_end.at(b - 1, "cov"))
                dve.tensor_tensor(cov, cov, bank[5][:, :].rearrange("p (o d) -> p o d", o=2),
                                  op=ALU.add).then_inc(vector_image_end.done("cov"), 1)

            def next_tiles(b):
                for s in range(EARLY):
                    pool1(b, s)

            def image_step(b, more=True):
                for h in range(HEADS):
                    head_max((b - 1) * HEADS + h, h)
                    if EARLY + h < TPB:
                        pool1(b, EARLY + h)
                    head_scale((b - 1) * HEADS + h)
                finish1(b - 1)
                image1(b)
                if more:
                    next_tiles(b + 1)
                lengths1(b)

            for s in range(TPB):
                pool1(0, s)
            image1(0)
            next_tiles(1)
            lengths1(0)
            image_step(1)
            with dve.Fori(2, B - 1) as b:
                image_step(b)
            image_step(B - 1, more=False)
            for h in range(HEADS):
                head_max((B - 1) * HEADS + h, h)
                head_scale((B - 1) * HEADS + h)
            finish1(B - 1)

            dve.wait_ge(vector_image_end.sem, vector_image_end.at(B - 1, "cov"))
            dve.wait_ge(tensor_image_end.sem, tensor_image_end.at(B - 1, "cov"))
            dve.memset(ones, 1.0).then_inc(vector_bn.done("ones"), 1)
            for o in range(2):
                dve.tensor_reduce(omean[:, o:o + 1], oall[:, o, :, :].rearrange("p b l -> p (b l)"), axis=AX.X,
                                  op=ALU.add).then_inc(vector_bn.done(f"osum{o}"), 1)
            dve.wait_ge(vector_bn.sem, vector_bn.at(0, "osum1"))
            dve.tensor_scalar(omean, omean, 1.0 / (B * LOW), None, ALU.mult).then_inc(vector_bn.done("omean"), 1)
            dve.wait_ge(tensor_bn.sem, tensor_bn.at(0, "z"))
            for k in range(4):
                o, c = divmod(k, 2)
                s = slice(c * 512, c * 512 + 512)
                dve.tensor_tensor(zw[:, o, s], bank[k][:, :], wp[:, o, s], op=ALU.mult).then_inc(vector_bn.done(f"zw{k}"), 1)
            dve.wait_ge(vector_bn.sem, vector_bn.at(0, "omean"))
            for o in range(2):
                dve.tensor_scalar(wm[:, o, :], wp[:, o, :], omean[:, o:o + 1], None,
                                  ALU.mult).then_inc(vector_bn.done(f"wm{o}"), 1)
            dve.wait_ge(tensor_bn.sem, tensor_bn.at(0, "sq"))
            for c in range(2):
                dve.tensor_copy(bmean[:, c * 512:c * 512 + 512], bank[4 + c][:, :]).then_inc(vector_bn.done(f"mean{c}"), 1)
            for c in range(2):
                dve.tensor_scalar(bvar[:, c * 512:c * 512 + 512], bank[6 + c][:, :], 1.0 / (B * PIX), None,
                                  ALU.mult).then_inc(vector_bn.done(f"e{c}"), 1)
            dve.wait_ge(vector_bn.sem, vector_bn.at(0, "e1"))
            dve.tensor_tensor(ylow[0], bmean, bmean, op=ALU.mult).then_inc(vector_bn.done("msq"), 1)
            dve.wait_ge(vector_bn.sem, vector_bn.at(0, "msq"))
            dve.tensor_tensor(bvar, bvar, ylow[0], op=ALU.subtract).then_inc(vector_bn.done("var"), 1)
            dve.wait_ge(vector_bn.sem, vector_bn.at(0, "var"))
            dve.tensor_scalar(bvar, bvar, EPS, None, ALU.add).then_inc(vector_bn.done("eps"), 1)
            dve.wait_ge(scalar_bn.sem, scalar_bn.at(0, "std"))
            dve.reciprocal(bvar, bvar).then_inc(vector_bn.done("rstd"), 1)
            dve.wait_ge(vector_bn.sem, vector_bn.at(0, "rstd"))
            dve.wait_ge(bnl, 16 * (2))
            dve.tensor_tensor(bgam, bgam, bvar, op=ALU.mult).then_inc(vector_bn.done("scale"), 1)
            dve.wait_ge(vector_bn.sem, vector_bn.at(0, "scale"))
            dve.tensor_tensor(bmean, bmean, bgam, op=ALU.mult).then_inc(vector_bn.done("ms"), 1)
            dve.wait_ge(vector_bn.sem, vector_bn.at(0, "ms"))
            dve.tensor_tensor(bbet, bbet, bmean, op=ALU.subtract).then_inc(vector_bn.done("shift"), 1)
            dve.wait_ge(vector_bn.sem, vector_bn.at(0, "shift"))

            for o in range(2):
                dve.tensor_tensor(wp[:, o, :], wp[:, o, :], bgam, op=ALU.mult).then_inc(vector_bn.done(f"wscale{o}"), 1)
            dve.wait_ge(vector_bn.sem, vector_bn.at(0, "wscale1"))
            dve.tensor_copy(ob, oall[:, :, 0, :]).then_inc(vector_ob.done("ob"), 1)

            def low(b, more=True):
                for k in range(2):
                    dve.wait_ge(tensor_low.sem, tensor_low.at(b, f"y{k}"))
                    if k == 1 and more:
                        nxt = oall[:, :, b + 1, :] if isinstance(b, int) else oall[:, :, bass.ds(b + 1, 1), :].squeeze(2)
                        dve.tensor_copy(ob, nxt).then_inc(vector_ob.done("ob"), 1)
                    if begun(b - 1):
                        dve.wait_ge(pool_low.sem, pool_low.at(b - 1, f"lo{k}"))
                    for c in range(2):
                        s = slice(c * 512, c * 512 + 512)
                        dve.tensor_tensor(ylow[k][:, s], bank[2 * k + c][:, :], bbet[:, s],
                                          op=ALU.add).then_inc(vector_low.done(f"add{c}{k}"), 1)
                    dve.wait_ge(vector_low.sem, vector_low.at(b, f"add1{k}"))
                    if begun(b - 1):
                        dve.wait_ge(lows[k], 16 * (6 * b))
                    dve.tensor_copy(part[k][0], ylow[k]).then_inc(vector_low.done(f"hi{k}"), 1)
                    dve.wait_ge(vector_low.sem, vector_low.at(b, f"hi{k}"))
                    dve.tensor_tensor(ylow[k], ylow[k], part[k][0], op=ALU.subtract).then_inc(vector_low.done(f"rest{k}"), 1)
                    dve.wait_ge(vector_low.sem, vector_low.at(b, f"rest{k}"))
                    dve.tensor_copy(part[k][1], ylow[k]).then_inc(vector_low.done(f"mid{k}"), 1)

            low(0)
            with dve.Fori(1, B - 1) as b:
                low(b)
            low(B - 1, more=False)

            dve.wait_ge(lows[0], 16 * (6 * B))
            dve.wait_ge(lows[1], 16 * (6 * B))
            dve.wait_ge(vector_low.sem, vector_low.at(B - 1, "mid1"))
            dve.wait_ge(pool_low.sem, pool_low.at(B - 1, "lo1"))
            dve.memset(EDGE, 0.0).then_inc(vector_pads.done("edge"), 1)
            dve.memset(ALG, 0.0).then_inc(vector_pads.done("alpha"), 1)

            def add_low(i, u):
                dve.wait_ge(x_landed, 16 * (i + 1))
                if begun(i - 2):
                    dve.wait_ge(vector_back.sem, vector_back.at(i - 2, "mul3"))
                for q in range(8):
                    dve.wait_ge(tensor_front.sem, tensor_front.at(i, f"up{q}"))
                    s = slice(q * 512, q * 512 + 512)
                    dve.tensor_tensor(X[u][:, s], XS[:, s], bank[q % 2][:, :], op=ALU.add).then_inc(vector_front.done(f"add{q}"), 1)

            def sums(i, u):
                dve.wait_ge(vector_front.sem, vector_front.at(i, "add7"))
                dve.tensor_reduce(EO.rearrange("p (h e) -> p h e", e=2), X[u].rearrange("p (h w e) -> p h e w", h=64, e=2),
                                  axis=AX.X, op=ALU.add).then_inc(vector_front.done("pairs"), 1)
                dve.wait_ge(vector_front.sem, vector_front.at(i, "pairs"))
                dve.tensor_tensor(RC[:, 0:64], EO[:, 0:P:2], EO[:, 1:P:2], op=ALU.add).then_inc(vector_front.done("rows"), 1)
                if begun(i - 2):
                    dve.wait_ge(tensor_spectrum.sem, tensor_spectrum.at(i - 2, "nyqt"))
                dve.tensor_tensor(ALT[u], EO[:, 0:P:2], EO[:, 1:P:2], op=ALU.subtract).then_inc(vector_front.done("alt"), 1)
                dve.wait_ge(vector_front.sem, vector_front.at(i, "rows"))
                if begun(i - 2):
                    dve.wait_ge(scalar_back.sem, scalar_back.at(i - 2, "mean3"))
                dve.tensor_reduce(PAR[u][:, 0:1], RC[:, 0:64], axis=AX.X, op=ALU.add).then_inc(vector_front.done("total"), 1)

            def variance(i, u):
                par = PAR[u]
                dve.wait_ge(tensor_front.sem, tensor_front.at(i, "stats"))
                n = 1.0 / (GC * PIX)
                dve.tensor_scalar(par[:, 2:3], bank[7][:, 0:1], n, None, ALU.mult).then_inc(vector_front.done("mean"), 1)
                dve.wait_ge(vector_front.sem, vector_front.at(i, "mean"))
                dve.tensor_scalar(par[:, 3:4], par[:, 2:3], par[:, 2:3], -EPS, ALU.mult, ALU.add).then_inc(vector_front.done("msq"), 1)
                dve.wait_ge(vector_front.sem, vector_front.at(i, "msq"))
                dve.scalar_tensor_tensor(par[:, 4:5], bank[7][:, 1:2], n, par[:, 3:4], op0=ALU.mult,
                                         op1=ALU.subtract).then_inc(vector_front.done("var"), 1)

            def normalise(i, u):
                par = PAR[u]
                dve.wait_ge(pool_front.sem, pool_front.at(i, "rstd"))
                dve.scalar_tensor_tensor(par[:, 7:8], par[:, 2:3], -1.0, par[:, 6:7], op0=ALU.mult,
                                         op1=ALU.mult).then_inc(vector_front.done("shift"), 1)
                dve.tensor_tensor(par[:, 5:6], par[:, 4:5], par[:, 6:7], op=ALU.mult).then_inc(vector_front.done("std"), 1)
                dve.wait_ge(vector_front.sem, vector_front.at(i, "std"))
                dve.tensor_scalar(par[:, 9:10], par[:, 5:6], 2.0, 1.0, ALU.mult, ALU.add).then_inc(vector_front.done("offset"), 1)
                dve.tensor_scalar(par[:, 8:9], par[:, 6:7], 1.0 / 64, None, ALU.mult).then_inc(vector_front.done("r64"), 1)
                dve.wait_ge(vector_front.sem, vector_front.at(i, "r64"))
                dve.tensor_scalar(ALT[u], ALT[u], par[:, 6:7], 0.125, ALU.mult, ALU.mult).then_inc(vector_front.done("altn"), 1)
                dve.tensor_scalar(X[u], X[u], par[:, 6:7], par[:, 7:8], ALU.mult, ALU.add).then_inc(vector_front.done("gx"), 1)

            def gate_input(i, u):
                par = PAR[u]
                dve.wait_ge(pool_front.sem, pool_front.at(i, "col5"))
                if begun(i - 2):
                    dve.wait_ge(tensor_gate.sem, tensor_gate.at(i - 2, "w1"))
                dve.tensor_scalar(CATS[u], RC, par[:, 8:9], par[:, 7:8], ALU.mult, ALU.add).then_inc(vector_front.done("cat"), 1)

            ggrid = GT.rearrange("p (h w) -> p h w", h=64)

            def filter_mean(i, u):
                cat = CATS[u]
                grid = X[u].rearrange("p (h w) -> p h w", h=64)
                dve.wait_ge(vector_front.sem, vector_front.at(i, "cat"))
                if begun(i - 1):
                    dve.wait_ge(scalar_gate.sem, scalar_gate.at(i - 1, "expcol"))
                dve.tensor_reduce(SM[:, 20:21], cat[:, 0:64], axis=AX.X, op=ALU.add).then_inc(vector_gate.done("tot"), 1)
                dve.tensor_copy(EDGE[:, 2::-2], cat[:, 0:64:63]).then_inc(vector_gate.done("edges0"), 1)
                dve.tensor_copy(EDGE[:, 5:2:-2], cat[:, 64:128:63]).then_inc(vector_gate.done("edges1"), 1)
                dve.wait_ge(vector_gate.sem, vector_gate.at(i, "edges1"))
                fq = FR[:, 0:9].rearrange("p (a b) -> p a b", a=3)
                dve.tensor_tensor(fq, EDGE[:, 0:3].unsqueeze(2).to_broadcast([P, 3, 3]),
                                  EDGE[:, 3:6].unsqueeze(1).to_broadcast([P, 3, 3]), op=ALU.add).then_inc(vector_gate.done("f0"), 1)
                dve.wait_ge(vector_gate.sem, vector_gate.at(i, "f0"))
                dve.tensor_scalar(FR[:, 0:9], FR[:, 0:9], -1.0, SM[:, 20:21], ALU.mult, ALU.add).then_inc(vector_gate.done("f1"), 1)
                dve.wait_ge(vector_gate.sem, vector_gate.at(i, "f1"))
                corner = fq[:, ::2, ::2]
                dve.scalar_tensor_tensor(corner, grid[:, ::-63, ::-63], 1.0 / 64, corner, op0=ALU.mult,
                                         op1=ALU.add).then_inc(vector_gate.done("corner"), 1)
                dve.wait_ge(vector_gate.sem, vector_gate.at(i, "corner"))
                dve.tensor_tensor(FR[:, 16:25], FR[:, 0:9], wdw[:, :], op=ALU.mult).then_inc(vector_gate.done("fw"), 1)
                dve.wait_ge(vector_gate.sem, vector_gate.at(i, "fw"))
                dve.tensor_reduce(SM[:, 7:8], FR[:, 16:25], axis=AX.X, op=ALU.add).then_inc(vector_gate.done("dw"), 1)
                dve.wait_ge(vector_gate.sem, vector_gate.at(i, "dw"))
                dve.tensor_scalar(SM[:, 8:9], SM[:, 7:8], 1.0 / 64, colw[:, BDW:BDW + 1], ALU.mult,
                                  ALU.add).then_inc(vector_gate.done("dwb"), 1)

            def logits(i):
                dve.wait_ge(tensor_gate.sem, tensor_gate.at(i, "pw"))
                dve.tensor_tensor(SM[:, 9:10], bank[7][:, 64:65], colw[:, BPW:BPW + 1], op=ALU.add).then_inc(vector_gate.done("x2m"), 1)
                dve.wait_ge(vector_gate.sem, vector_gate.at(i, "x2m"))
                dve.tensor_scalar(FRL, csel[:, :], SM[:, 9:10], None, ALU.mult).then_inc(vector_gate.done("lsel"), 1)

            def gate_columns(i, u):
                dve.wait_ge(scalar_gate.sem, scalar_gate.at(i, "sig"))
                dve.tensor_scalar(SHW[u], SHW[u], 0.5, 0.5, ALU.mult, ALU.add).then_inc(vector_gate.done("gates"), 1)
                dve.wait_ge(vector_gate.sem, vector_gate.at(i, "gates"))
                if begun(i - 1):
                    dve.wait_ge(tensor_back.sem, tensor_back.at(i - 1, "gsum1"))
                grid = X[u].rearrange("p (h w) -> p h w", h=64)
                dve.tensor_tensor(ggrid, grid, SHW[u][:, 64:128].unsqueeze(1).to_broadcast([P, 64, 64]),
                                  op=ALU.mult).then_inc(vector_gate.done("t1"), 1)

            def gate_rows(i, u):
                dve.wait_ge(vector_gate.sem, vector_gate.at(i, "t1"))
                dve.scalar_tensor_tensor(ggrid, ggrid, 1.0, SHW[u][:, 0:64].unsqueeze(2).to_broadcast([P, 64, 64]),
                                         op0=ALU.mult, op1=ALU.mult, accum_out=SM[:, 0:1]).then_inc(vector_gate.done("gated"), 1)

            def gate_small(i):
                dve.wait_ge(vector_gate.sem, vector_gate.at(i, "gated"))
                dve.tensor_scalar(SM[:, 2:3], SM[:, 0:1], 1.0 / PIX, None, ALU.mult).then_inc(vector_gate.done("gmean"), 1)
                dve.wait_ge(vector_gate.sem, vector_gate.at(i, "gmean"))
                dve.tensor_scalar(SM[:, 3:4], SM[:, 2:3], SM[:, 2:3], -EPS, ALU.mult, ALU.add).then_inc(vector_gate.done("gmsq"), 1)
                dve.wait_ge(tensor_gate.sem, tensor_gate.at(i, "lrow"))
                dve.tensor_reduce(SM[:, 10:11], bank[7][:, 320:352], axis=AX.X, op=ALU.max,
                                  negate=True).then_inc(vector_gate.done("max"), 1)

            def weights(i):
                dve.wait_ge(vector_gate.sem, vector_gate.at(i, "gmsq"))
                dve.wait_ge(scalar_gate.sem, scalar_gate.at(i, "sq"))
                dve.scalar_tensor_tensor(SM[:, 4:5], SM[:, 1:2], 1.0 / PIX, SM[:, 3:4], op0=ALU.mult,
                                         op1=ALU.subtract).then_inc(vector_gate.done("gvar"), 1)
                dve.wait_ge(scalar_gate.sem, scalar_gate.at(i, "expcol"))
                dve.reciprocal(SM[:, 13:14], SM[:, 11:12]).then_inc(vector_gate.done("rsum"), 1)
                dve.wait_ge(vector_gate.sem, vector_gate.at(i, "rsum"))
                dve.wait_ge(pool_gate.sem, pool_gate.at(i, "rstd"))
                dve.tensor_tensor(SM[:, 14:15], SM[:, 12:13], SM[:, 13:14], op=ALU.mult).then_inc(vector_gate.done("s2"), 1)
                dve.tensor_tensor(SM[:, 15:16], colw[:, GAMMA:GAMMA + 1], SM[:, 6:7], op=ALU.mult).then_inc(vector_gate.done("sg"), 1)
                dve.wait_ge(vector_gate.sem, vector_gate.at(i, "sg"))
                dve.tensor_tensor(SM[:, 16:17], SM[:, 14:15], SM[:, 15:16], op=ALU.mult).then_inc(vector_gate.done("alpha"), 1)
                dve.wait_ge(vector_gate.sem, vector_gate.at(i, "alpha"))
                dve.tensor_scalar(ALG[:, 0:NG], gsel[:, :], SM[:, 16:17], None, ALU.mult).then_inc(vector_gate.done("alg"), 1)
                dve.tensor_tensor(SM[:, 17:18], SM[:, 16:17], SM[:, 2:3], op=ALU.mult).then_inc(vector_gate.done("am"), 1)
                dve.wait_ge(vector_gate.sem, vector_gate.at(i, "am"))
                dve.scalar_tensor_tensor(SM[:, 18:19], colw[:, BETA:BETA + 1], SM[:, 14:15], SM[:, 17:18],
                                         op0=ALU.mult, op1=ALU.subtract).then_inc(vector_gate.done("kc"), 1)

            def constant(i):
                dve.wait_ge(tensor_gate.sem, tensor_gate.at(i, "const"))
                dve.tensor_tensor(SM[:, 19:20], bank[7][:, 66:67], wts0[:, :], op=ALU.add).then_inc(vector_gate.done("kcon"), 1)

            def nyquist(i):
                dve.wait_ge(scalar_spectrum.sem, scalar_spectrum.at(i, "nyqsq"))
                dve.tensor_tensor(SQN[:, 1:32], SQN[:, 1:32], SQN[:, 33:64], op=ALU.add).then_inc(vector_spectrum.done("nyq"), 1)

            def squares(i, k):
                sign, half_, octet = k // 4, (k // 2) % 2, k % 2
                dve.wait_ge(scalar_spectrum.sem, scalar_spectrum.at(i, f"w{k}"))
                if k == 0 and begun(i - 1):
                    dve.wait_ge(tensor_spectrum.sem, tensor_spectrum.at(i - 1, "chan"))
                c = sign * 1024 + octet * 512
                dve.tensor_tensor(MAG[64 * half_:64 * half_ + 64, c:c + 512], SQ[k % 2][0:64, :], SQ[k % 2][64:128, :],
                                  op=ALU.add).then_inc(vector_spectrum.done(f"w{k}"), 1)
                dve.wait_ge(vector_spectrum.sem, vector_spectrum.at(i, f"w{k}"))

            def frequency_map(i):
                dve.wait_ge(tensor_back.sem, tensor_back.at(i, "fmap"))
                src = bank[6][:, 0:128]
                dve.tensor_copy(MAP[:, 1, 0, :], src).then_inc(vector_back.done("fhi"), 1)
                dve.wait_ge(vector_back.sem, vector_back.at(i, "fhi"))
                dve.tensor_tensor(REST[1], src, MAP[:, 1, 0, :], op=ALU.subtract).then_inc(vector_back.done("frest"), 1)
                dve.wait_ge(vector_back.sem, vector_back.at(i, "frest"))
                dve.tensor_copy(MAP[:, 1, 1, :], REST[1]).then_inc(vector_back.done("fmid"), 1)
                dve.wait_ge(vector_back.sem, vector_back.at(i, "fmid"))
                dve.tensor_tensor(MAP[:, 1, 2, :], REST[1], MAP[:, 1, 1, :], op=ALU.subtract).then_inc(vector_back.done("fmap"), 1)

            def group_sum(i):
                dve.wait_ge(tensor_back.sem, tensor_back.at(i, "gsum1"))
                if begun(i - 1):
                    dve.wait_ge(tensor_back.sem, tensor_back.at(i - 1, "wmap"))
                dve.tensor_copy(TG, bank[4][:, 0:128]).then_inc(vector_back.done("gsum"), 1)

            def weight_map(i):
                dve.wait_ge(tensor_back.sem, tensor_back.at(i, "wmap"))
                dve.wait_ge(vector_gate.sem, vector_gate.at(i, "kcon"))
                if begun(i - 1):
                    dve.wait_ge(map_stored, 16 * (2 * i))
                src, k = bank[5][:, 0:128], SM[:, 19:20]
                dve.tensor_scalar(MAP[:, 0, 0, :], src, k, None, ALU.add).then_inc(vector_back.done("whi"), 1)
                dve.wait_ge(vector_back.sem, vector_back.at(i, "whi"))
                dve.scalar_tensor_tensor(REST[0], src, k, MAP[:, 0, 0, :], op0=ALU.add,
                                         op1=ALU.subtract).then_inc(vector_back.done("wrest"), 1)
                dve.wait_ge(vector_back.sem, vector_back.at(i, "wrest"))
                dve.tensor_copy(MAP[:, 0, 1, :], REST[0]).then_inc(vector_back.done("wmid"), 1)
                dve.wait_ge(vector_back.sem, vector_back.at(i, "wmid"))
                dve.tensor_tensor(MAP[:, 0, 2, :], REST[0], MAP[:, 0, 1, :], op=ALU.subtract).then_inc(vector_back.done("wmap"), 1)

            def multiply(i, u):
                for q in range(4):
                    dve.wait_ge(scalar_back.sem, scalar_back.at(i, f"sig{2 * q + 1}"))
                    dve.scalar_tensor_tensor(SIG[q], SIG[q], PAR[u][:, 9:10], X[u][:, q * 1024:(q + 1) * 1024],
                                             op0=ALU.add, op1=ALU.mult).then_inc(vector_back.done(f"mul{q}"), 1)

            def period(i, u, new=True):
                constant(i)
                if new:
                    add_low(i + 1, 1 - u)
                    sums(i + 1, 1 - u)
                nyquist(i)
                squares(i, 0)
                squares(i, 1)
                if new:
                    variance(i + 1, 1 - u)
                    normalise(i + 1, 1 - u)
                group_sum(i)
                squares(i, 2)
                if new:
                    gate_input(i + 1, 1 - u)
                    filter_mean(i + 1, 1 - u)
                squares(i, 3)
                if new:
                    gate_columns(i + 1, 1 - u)
                for k in range(4, 8):
                    squares(i, k)
                if new:
                    logits(i + 1)
                    gate_rows(i + 1, 1 - u)
                weight_map(i)
                frequency_map(i)
                if new:
                    gate_small(i + 1)
                    weights(i + 1)
                multiply(i, u)

            add_low(0, 0)
            sums(0, 0)
            variance(0, 0)
            normalise(0, 0)
            gate_input(0, 0)
            filter_mean(0, 0)
            gate_columns(0, 0)
            logits(0)
            gate_rows(0, 0)
            gate_small(0)
            weights(0)
            period(0, 0)
            period(1, 1)
            with dve.Fori(1, NT // 2 - 1) as pr:
                period(2 * pr, 0)
                period(2 * pr + 1, 1)
            period(NT - 2, 0)
            period(NT - 1, 1, new=False)

        @block.tensor
        def _(pe):
            mm = pe.matmul
            pe.wait_ge(cst, 16 * N_CONST)
            pe.wait_ge(upl, 16 * 1)
            pe.wait_ge(blocks, 16 * (3 * NG))
            pe.wait_ge(vector_setup.sem, vector_setup.at(0, "selw2"))
            mm(bank[0][0:ARG_ROWS, 128:256], argw_t[:, :], ident[:, :], start=True, stop=True).then_inc(tensor_setup.done("argw"), 1)
            pe.wait_ge(vector_setup.sem, vector_setup.at(0, "s1"))
            mm(bank[0][:, 0:1], wpbd[:, :], cw[:, 35:36], start=True, stop=True).then_inc(tensor_setup.done("p"), 1)
            pe.wait_ge(vector_setup.sem, vector_setup.at(0, "c1"))
            mm(bank[0][:, 1:2], gones[:, :], cw[:, 43:44], start=True, stop=True).then_inc(tensor_setup.done("const"), 1)
            pe.wait_ge(vector_setup.sem, vector_setup.at(0, "argw"))

            def image1(b):
                pe.wait_ge(vector_pool.sem, vector_pool.at(b * TPB + TPB - 1, "sum"))
                pe.wait_ge(scalar_squares.sem, scalar_squares.at(b * TPB + TPB - 1, "sq"))
                if begun(b - 1):
                    pe.wait_ge(vector_imagestats.sem, vector_imagestats.at(b - 1, "var0"))
                mm(bank[0][:, 0:16], gones[:, :], st, start=True, stop=True).then_inc(tensor_imagestats.done("stats"), 1)
                pe.wait_ge(vector_imagestats.sem, vector_imagestats.at(b, "xn7"))
                if begun(b - 1):
                    pe.wait_ge(vector_image_end.sem, vector_image_end.at(b - 1, "oT"))
                for o in range(4):
                    for t in range(TPB):
                        ins = mm(bank[1 + o // 2][:, (o % 2) * LOW:(o % 2 + 1) * LOW], wq[:, t, o * P:(o + 1) * P],
                                 xn[:, t, :], start=(t == 0), stop=(t == TPB - 1))
                ins.then_inc(tensor_qkv.done("qk"), 1)
                for m in range(2):
                    for t in range(TPB):
                        ins = mm(bank[3][:, m * TD:(m + 1) * TD], xn[:, t, m * P:(m + 1) * P],
                                 wq[:, t, 2 * TD:3 * TD], start=(t == 0), stop=(t == TPB - 1))
                ins.then_inc(tensor_qkv.done("v"), 1)
                pe.wait_ge(scalar_qkv.sem, scalar_qkv.at(b, "sq"))
                if begun(b - 1):
                    pe.wait_ge(vector_image_end.sem, vector_image_end.at(b - 1, "cov"))
                mm(bank[4][:, :], gones[:, :], qk2[:, 0:2, :], start=True, stop=True)
                mm(bank[5][:, :], gones[:, :], qk2[:, 2:4, :], start=True, stop=True).then_inc(tensor_qkv.done("norms"), 1)

            def head_scores(b, h):
                n = b * TPB + h
                lo, o = 32 * (h % 4), h // 4
                pe.wait_ge(vector_qkv.sem, vector_qkv.at(b, "kn"))
                if begun(n - 2):
                    pe.wait_ge(scalar_head.sem, scalar_head.at(n - 2, "exp1"))
                for l in range(2):
                    ins = mm(bank[SCORE_BANKS[h % 2]][:, l * LOW:(l + 1) * LOW], qk[lo:lo + 32, o, l * P:(l + 1) * P],
                             qk[lo:lo + 32, 2 + o, :], start=True, stop=True)
                ins.then_inc(tensor_scores.done("scores"), 1)

            def head_transpose(b, h):
                n = b * TPB + h
                pe.wait_ge(vector_head.sem, vector_head.at(n, "scale1"))
                if begun(n - 1):
                    pe.wait_ge(vector_head.sem, vector_head.at(n - 1, "probT"))
                for m in range(2):
                    for l in range(2):
                        ins = pe.transpose(bank[7][:, m * LOW + l * P:m * LOW + (l + 1) * P],
                                           prob[:, l, m * P:(m + 1) * P], ident[:, :])
                ins.then_inc(tensor_head.done("transpose"), 1)

            def head_out(b, h):
                n = b * TPB + h
                lo, o = 32 * (h % 4), h // 4
                pe.wait_ge(vector_head.sem, vector_head.at(n, "probT"))
                d = slice(DPH * h, DPH * h + DPH)
                for m in range(2):
                    mm(bank[1][lo:lo + 32, o * LOW:(o + 1) * LOW], vt[:, m, d], probT[:, m, :],
                       start=(m == 0), stop=(m == 1))
                for l in range(2):
                    for m in range(2):
                        ins = mm(bank[2][:, l * TD + DPH * h:l * TD + DPH * h + DPH], probT[:, m, l * P:(l + 1) * P],
                                 vt[:, m, d], start=(m == 0), stop=(m == 1))
                ins.then_inc(tensor_head.done("out"), 1)

            def finish1(b):
                pe.wait_ge(vector_image_end.sem, vector_image_end.at(b, "oT"))
                for l in range(2):
                    for k in range(2):
                        ins = mm(bank[4][:, l * TD:(l + 1) * TD], gram[:, k, l * P:(l + 1) * P], oT[:, k, :],
                                 start=(k == 0), stop=(k == 1))
                ins.then_inc(tensor_image_end.done("ko"), 1)
                pe.wait_ge(vector_image_end.sem, vector_image_end.at(b, "ko"))
                for o in range(2):
                    for k in range(2):
                        ins = mm(bank[5][:, o * TD:(o + 1) * TD], oT[:, k, o * P:(o + 1) * P], ko[:, k, :],
                                 start=(k == 0), stop=(k == 1))
                ins.then_inc(tensor_image_end.done("cov"), 1)

            def heads(b):
                head_scores(b, 0)
                for h in range(HEADS):
                    if h + 1 < HEADS:
                        head_scores(b, h + 1)
                    head_transpose(b, h)
                    head_out(b, h)

            image1(0)

            def image_step(b):
                heads(b - 1)
                finish1(b - 1)
                image1(b)

            image_step(1)
            with pe.Fori(2, B) as b:
                image_step(b)
            heads(B - 1)
            finish1(B - 1)

            pe.wait_ge(vector_image_end.sem, vector_image_end.at(B - 1, "cov"))
            for o in range(2):
                for c in range(2):
                    for k in range(2):
                        ins = mm(bank[2 * o + c][:, :], cov[:, k, o * P:(o + 1) * P], wp[:, k, c * 512:(c + 1) * 512],
                                 start=(k == 0), stop=(k == 1))
            ins.then_inc(tensor_bn.done("z"), 1)
            pe.wait_ge(vector_bn.sem, vector_bn.at(0, "wm1"))
            for c in range(2):
                for o in range(2):
                    ins = mm(bank[4 + c][:, :], ones, wm[:, o, c * 512:(c + 1) * 512], start=(o == 0), stop=(o == 1))
            ins.then_inc(tensor_bn.done("mean"), 1)
            for c in range(2):
                for o in range(2):
                    ins = mm(bank[6 + c][:, :], ones, zw[:, o, c * 512:(c + 1) * 512], start=(o == 0), stop=(o == 1))
            ins.then_inc(tensor_bn.done("sq"), 1)

            def low(b):
                pe.wait_ge(vector_ob.sem, vector_ob.at(b, "ob"))
                for k in range(2):
                    if begun(b - 1):
                        pe.wait_ge(vector_low.sem, vector_low.at(b - 1, f"add1{k}"))
                    for c in range(2):
                        for o in range(2):
                            ins = mm(bank[2 * k + c][:, :], ob[:, o, k * P:(k + 1) * P], wp[:, o, c * 512:(c + 1) * 512],
                                     start=(o == 0), stop=(o == 1))
                    ins.then_inc(tensor_low.done(f"y{k}"), 1)

            low(0)
            with pe.Fori(1, B) as b:
                low(b)
            pe.wait_ge(vector_low.sem, vector_low.at(B - 1, "add11"))

            def up(i, u, q):
                if q < 2:
                    if begun(i - 2):
                        pe.wait_ge(scalar_back.sem, scalar_back.at(i - 2, f"sig{6 + q}"))
                    if begun(i - 1):
                        pe.wait_ge(vector_front.sem, vector_front.at(i - 1, f"add{6 + q}"))
                else:
                    pe.wait_ge(vector_front.sem, vector_front.at(i, f"add{q - 2}"))
                mm(bank[q % 2][:, 0:128], YS[u][:, 2 * q, :], upmat[:, 128:256], start=True, stop=True)
                mm(bank[q % 2][:, 128:384], YS[u][:, 2 * q + 1, :], upmat[:, :], start=True, stop=True)
                mm(bank[q % 2][:, 384:512], YS[u][:, 2 * q + 2, :], upmat[:, 0:128], start=True,
                   stop=True).then_inc(tensor_front.done(f"up{q}"), 1)

            def stats(i, u):
                pe.wait_ge(vector_front.sem, vector_front.at(i, "total"))
                pe.wait_ge(scalar_front.sem, scalar_front.at(i, "sq"))
                if begun(i - 1):
                    pe.wait_ge(vector_gate.sem, vector_gate.at(i - 1, "kcon"))
                mm(bank[7][:, 0:2], gones[:, :], PAR[u][:, 0:2], start=True, stop=True).then_inc(tensor_front.done("stats"), 1)

            def gate(i, u):
                pe.wait_ge(vector_front.sem, vector_front.at(i, "cat"))
                mm(bank[7][:, 128:256], w1bd[:, :], CATS[u], start=True, stop=True).then_inc(tensor_gate.done("w1"), 1)

            def taps2(i, u):
                pe.wait_ge(vector_front.sem, vector_front.at(i, "gx"))
                for k, (c0, n) in enumerate(TAP_FILLS):
                    if k == 2:
                        pe.wait_ge(scalar_taps.sem, scalar_taps.at(i, "t0"))
                    else:
                        if begun(i - 1):
                            pe.wait_ge(vector_back.sem, vector_back.at(i - 1, ("gsum", "wmap")[k]))
                    for c in range(n):
                        ins = mm(bank[4 + k % 2][:, 36 * c:36 * c + P], X[u][:, (c0 + c) * P:(c0 + c + 1) * P],
                                 taps[:, :], start=True, stop=True)
                    ins.then_inc(tensor_taps.done(f"t{k}"), 1)

            def pointwise(i):
                pe.wait_ge(vector_gate.sem, vector_gate.at(i, "dwb"))
                pe.wait_ge(scalar_gate.sem, scalar_gate.at(i, "sig"))
                mm(bank[7][:, 64:65], wptbd[:, :], SM[:, 8:9], start=True, stop=True).then_inc(tensor_gate.done("pw"), 1)

            def logits(i):
                pe.wait_ge(vector_gate.sem, vector_gate.at(i, "lsel"))
                mm(bank[7][:, 320:352], gones[:, :], FRL, start=True, stop=True).then_inc(tensor_gate.done("lrow"), 1)

            def constant(i):
                pe.wait_ge(vector_gate.sem, vector_gate.at(i, "kc"))
                mm(bank[7][:, 66:67], gcols[:, :], SM[:, 18:19], start=True, stop=True).then_inc(tensor_gate.done("const"), 1)

            def row_transform(i, k):
                if k == 0:
                    pe.wait_ge(g2l, 16 * (2 * (i + 1)))
                if k >= 2:
                    pe.wait_ge(scalar_spectrum.sem, scalar_spectrum.at(i, f"h{k - 2}"))
                elif begun(i - 1):
                    pe.wait_ge(scalar_back.sem, scalar_back.at(i - 1, f"sig{2 + k}"))
                for c in range(4):
                    ins = mm(bank[2 + k % 2][:, c * P:(c + 1) * P], G2[:, (4 * k + c) * P:(4 * k + c + 1) * P],
                             dft_h[:, :], start=True, stop=True)
                ins.then_inc(tensor_spectrum.done(f"h{k}"), 1)

            def nyquist_turn(i, u):
                pe.wait_ge(vector_front.sem, vector_front.at(i, "altn"))
                if begun(i - 1):
                    pe.wait_ge(vector_back.sem, vector_back.at(i - 1, "fmap"))
                mm(bank[6][0:64, 384:512], ALT[u], ident[:, :], start=True, stop=True).then_inc(tensor_spectrum.done("nyqt"), 1)

            def nyquist(i):
                pe.wait_ge(scalar_spectrum.sem, scalar_spectrum.at(i, "nyqt"))
                mm(bank[6][:, 384:448], ALTT, dft_h[0:64, 0:64], start=True, stop=True).then_inc(tensor_spectrum.done("nyq"), 1)

            def column_transform(i, k):
                ah = AH.rearrange("p (c k) -> p c k", k=64)
                sign, half_, octet = k // 4, (k // 2) % 2, k % 2
                if k < 2:
                    pe.wait_ge(scalar_spectrum.sem, scalar_spectrum.at(i, f"h{6 + k}"))
                else:
                    pe.wait_ge(scalar_spectrum.sem, scalar_spectrum.at(i, f"w{k - 2}"))
                c0 = 2 * (half_ * 16 + octet * 8)
                dst = bank[2 + k % 2][:, :].rearrange("p (c k) -> p c k", k=32)
                mm(dst, dft_w[:, 0:P], ah[:, c0:c0 + 16, sign:sign + 32], start=True, stop=False)
                mm(dst[:, :, 1 - sign:32 - sign], dft_w[:, (1 + sign) * P:(2 + sign) * P], ah[:, c0:c0 + 16, 33:64],
                   start=False, stop=True).then_inc(tensor_spectrum.done(f"w{k}"), 1)

            def channel_sum(i):
                pe.wait_ge(scalar_spectrum.sem, scalar_spectrum.at(i, "root1"))
                pe.wait_ge(scalar_spectrum.sem, scalar_spectrum.at(i, "nyqsq"))
                mag = MAG.rearrange("p (s c k) -> p s c k", s=2, k=64)
                dst = bank[6][0:64, 128:256].rearrange("p (s k) -> p s k", s=2)
                for c in range(16):
                    ins = mm(dst, spread[:, 64 - 2 * c:P - 2 * c], mag[:, :, c, :], start=(c == 0), stop=(c == 15))
                ins.then_inc(tensor_spectrum.done("chan"), 1)

            def group_sum(i, part):
                pe.wait_ge(vector_gate.sem, vector_gate.at(i, "alg"))
                if begun(i - 1):
                    pe.wait_ge(scalar_back.sem, scalar_back.at(i - 1, "sig5"))
                else:
                    pe.wait_ge(scalar_taps.sem, scalar_taps.at(i, "t2"))
                for c in range(16 * part, 16 * part + 16):
                    ins = mm(bank[4][:, NG * c:NG * c + P], GT[:, c * P:(c + 1) * P], ALG, start=True, stop=True)
                ins.then_inc(tensor_back.done(f"gsum{part}"), 1)

            def weight_map(i):
                pe.wait_ge(vector_back.sem, vector_back.at(i, "gsum"))
                for n, (tap, d) in enumerate(SHIFT_PLAN):
                    mm(bank[5][:, 0:128], TP[:, tap, 1 + d:33 + d, :], shifts[:, n * P:(n + 1) * P],
                       start=(n == 0), stop=False)
                mm(bank[5][:, 0:128], TG, ident[:, :], start=False, stop=True).then_inc(tensor_back.done("wmap"), 1)

            def frequency_map(i):
                pe.wait_ge(scalar_spectrum.sem, scalar_spectrum.at(i, "fm1"))
                for k in range(2):
                    dst = bank[6][:, 64 * k:64 + 64 * k]
                    mm(dst, resize[:, k * P:(k + 1) * P], NYM, start=True, stop=False)
                    for j in range(2):
                        ins = mm(dst, resize_half[:, (2 * j + k) * P:(2 * j + k + 1) * P], FM[:, 64 * j:64 * j + 64],
                                 start=False, stop=(j == 1))
                ins.then_inc(tensor_back.done("fmap"), 1)

            def arguments(i, new):
                pe.wait_ge(mapl, 16 * ((1 + PARTS) * (i + 1)))
                for q in range(8):
                    if q < 2:
                        pe.wait_ge(vector_front.sem, vector_front.at(i + 1 if new else i, f"add{6 + q}"))
                    elif q < 4:
                        pe.wait_ge(scalar_spectrum.sem, scalar_spectrum.at(i, f"w{4 + q}"))
                    elif q < 6:
                        if new:
                            pe.wait_ge(scalar_taps.sem, scalar_taps.at(i + 1, f"t{q - 3}"))
                        else:
                            pe.wait_ge(vector_back.sem, vector_back.at(i, ("wmap", "gsum")[q - 4]))
                    else:
                        pe.wait_ge(scalar_back.sem, scalar_back.at(i, f"sig{q - 6}"))
                    mm(bank[ARG_BANKS[q]][:, :], argw[:, :], ROWS[:, q * 512:(q + 1) * 512], start=True,
                       stop=True).then_inc(tensor_back.done(f"arg{q}"), 1)

            def period(i, u, n, new=True):
                constant(i)
                if new:
                    pe.wait_ge(YL[1 - u], 16 * (6 * (n + 1)))
                nyquist_turn(i, u)
                for k in range(8):
                    row_transform(i, k)
                    if new and k >= 1:
                        up(i + 1, 1 - u, k - 1)
                if new:
                    up(i + 1, 1 - u, 7)
                nyquist(i)
                column_transform(i, 0)
                column_transform(i, 1)
                group_sum(i, 0)
                if new:
                    stats(i + 1, 1 - u)
                group_sum(i, 1)
                for k in range(2, 8):
                    column_transform(i, k)
                    if new and k == 3:
                        gate(i + 1, 1 - u)
                    elif new and k == 5:
                        pointwise(i + 1)
                weight_map(i)
                if new:
                    logits(i + 1)
                channel_sum(i)
                frequency_map(i)
                if new:
                    taps2(i + 1, 1 - u)
                arguments(i, new)

            pe.wait_ge(YL[0], 16 * 6)
            for k in range(8):
                up(0, 0, k)
            stats(0, 0)
            gate(0, 0)
            pointwise(0)
            logits(0)
            taps2(0, 0)
            period(0, 0, 0)
            period(1, 1, 1)
            with pe.Fori(1, NT // 2 - 1) as pr:
                period(2 * pr, 0, pr)
                period(2 * pr + 1, 1, pr + 1)
            period(NT - 2, 0, NT // 2 - 1)
            period(NT - 1, 1, 0, new=False)


def laid_out(inputs):
    g = {k: np.ascontiguousarray(v) for k, v in inputs.items()}

    def col(v):
        return np.tile(v.reshape(GC, -1), (NG, 1))

    return {
        "x": g["x"],
        "w_qkv_t": g["L0_conv_w_qkv"].T,
        "w_proj_t": g["L0_conv_w_proj"].T,
        "temperature": np.repeat(g["L0_conv_temperature"].reshape(2, 4), DPH, axis=1).T,
        "bn_gamma": g["L0_conv_bn_gamma"], "bn_beta": g["L0_conv_bn_beta"],
        "w1_t": g["L1_conv_w1"].T, "w_pw": g["L1_conv_w_pw"], "w_pw_t": g["L1_conv_w_pw"].T,
        "b1": col(g["L1_conv_b1"]), "gn_gamma": col(g["L1_conv_gn_gamma"]), "gn_beta": col(g["L1_conv_gn_beta"]),
        "w_dw": col(g["L1_conv_w_dw"]), "b_dw": col(g["L1_conv_b_dw"]), "b_pw": col(g["L1_conv_b_pw"]),
        "w_fp": col(g["L1_conv_w_fp"]), "b_fp": col(g["L1_conv_b_fp"]),
        "beta_row": np.tile(g["L1_conv_gn_beta"].reshape(1, GC), (P, 1)),
    }


def kernel(**inputs):
    import concourse.bacc as bacc
    from concourse.bass_utils import run_bass_kernel_spmd

    nc = bacc.Bacc("TRN2", target_bir_lowering=False, num_devices=1)
    arrays, args = {}, {}
    for name, v in {**laid_out(inputs), **constants()}.items():
        v = np.ascontiguousarray(v)
        arrays[f"in_{name}"] = v
        args[name] = nc.dram_tensor(f"in_{name}", v.shape, mybir.dt.from_np(v.dtype), kind="ExternalInput").ap()
    out = nc.dram_tensor("out", (B, CH, H, W), F32, kind="ExternalOutput").ap()
    build(nc, args, out)
    r = run_bass_kernel_spmd(nc, [arrays], core_ids=[0])
    return r.results[0]["out"]
```
